# Optimizing a Trainium2 kernel written in Bass

```python
import numpy as np
import jax
import jax.numpy as jnp

def _softmax(x, axis=-1):
    return jax.nn.softmax(x, axis=axis)

def _gelu(x):
    return jax.nn.gelu(x, approximate=True)

def _silu(x):
    return jax.nn.silu(x)

def _sigmoid(x):
    return jax.nn.sigmoid(x)

def _layernorm(x, axis=-1, eps=1e-05):
    m = jnp.mean(x, axis=axis, keepdims=True)
    v = jnp.var(x, axis=axis, keepdims=True)
    return (x - m) / jnp.sqrt(v + eps)

def _scatter_add(tgt, idx, src, axis=0):
    return tgt.at[idx].add(src)

def _segment_sum(src, seg, n):
    return jax.ops.segment_sum(src, seg, n)
kernel_name = 'mk_xattn_seq_d4_seqx_r4_111c97'

def setup_inputs(seed: int=0):
    np.random.seed(seed)
    _w = jnp.asarray

    def _rec_inputs():
        import jax
        import jax.numpy as jnp
        _rk = jax.random.key(seed)
        x = -1.394e-06 + 0.9999 * jax.random.normal(jax.random.fold_in(_rk, 1), (16, 256, 256), jnp.float32)
        _lenS = 256 - jax.random.randint(jax.random.fold_in(_rk, 7), (16,), 0, max(1, 256 // 4) + 1, jnp.int32)
        _lenS2 = 77 - jax.random.randint(jax.random.fold_in(_rk, 8), (16,), 0, max(1, 77 // 4) + 1, jnp.int32)
        _ctx_1024P = jax.random.normal(jax.random.fold_in(_rk, 11), (16, 16, 256), jnp.float32)
        _ctx_1024c = jax.random.dirichlet(jax.random.fold_in(_rk, 511), 0.3 * jnp.ones((16,), jnp.float32), (16, 77))
        _ctx_1024t = jnp.einsum('bsk,bkd->bsd', _ctx_1024c, _ctx_1024P)
        _ctx_1024t = _ctx_1024t * jax.lax.rsqrt(jnp.mean(jnp.square(_ctx_1024t)) + 1e-12) * 0.953939
        ctx_1024 = -0.000292821 + 1.00034 * (_ctx_1024t + 0.3 * jax.random.normal(jax.random.fold_in(_rk, 611), (16, 77, 256), jnp.float32))
        _validS = jnp.arange(256)[None, :] < _lenS[:, None]
        _validS2 = jnp.arange(77)[None, :] < _lenS2[:, None]
        _causal = jnp.tril(jnp.ones((256, 256), dtype=bool))
        mask_1x1xSxS_ik0 = jnp.where(jnp.broadcast_to(_validS[0:1, None, None, :], (1, 1, 256, 256)), 0, 1).astype(jnp.int32)
        return (x, ctx_1024, mask_1x1xSxS_ik0)
    x, ctx_1024, mask_1x1xSxS_ik0 = _rec_inputs()

    def _L0_xattn_setup():
        import jax, jax.numpy as jnp
        import numpy as np
        B, T, SE, C, H = (2, 512, 512, 256, 16)
        HS = C // H
        EPS = 1e-05

        def _ln(x, g, b):
            mu = jnp.mean(x, axis=-1, keepdims=True)
            var = jnp.mean(jnp.square(x - mu), axis=-1, keepdims=True)
            return (x - mu) * jax.lax.rsqrt(var + EPS) * g + b

        def _mha(q_in, kv_in, wq, bq, wk, bk, wv, bv, causal):
            q = jnp.einsum('btc,hcd->bhtd', q_in, wq) + bq[None, :, None, :]
            k = jnp.einsum('bsc,hcd->bhsd', kv_in, wk) + bk[None, :, None, :]
            v = jnp.einsum('bsc,hcd->bhsd', kv_in, wv) + bv[None, :, None, :]
            scores = jnp.einsum('bhtd,bhsd->bhts', q, k) * q.shape[-1] ** (-0.5)
            if causal:
                t, s = (scores.shape[-2], scores.shape[-1])
                mask = jnp.tril(jnp.ones((t, s), bool))
                scores = jnp.where(mask, scores, -jnp.inf)
            p = jax.nn.softmax(scores, axis=-1)
            o = jnp.einsum('bhts,bhsd->bhtd', p, v)
            b_, h_, t_, d_ = o.shape
            return o.transpose(0, 2, 1, 3).reshape(b_, t_, h_ * d_)
        key = jax.random.key(seed)
        ks = iter(jax.random.split(key, 40))
        nrm = lambda shape, s=0.02: jax.random.normal(next(ks), shape, jnp.float32) * s
        inp = {'x_e': jax.random.normal(next(ks), (B, SE, C), jnp.float32), 'x': jax.random.normal(next(ks), (B, T, C), jnp.float32), 'mq_w': nrm((H, C, HS)), 'mq_b': nrm((H, HS)), 'mk_w': nrm((H, C, HS)), 'mk_b': nrm((H, HS)), 'mv_w': nrm((H, C, HS)), 'mv_b': nrm((H, HS)), 'm_proj_w': nrm((C, C)), 'm_proj_b': nrm((C,)), 'cq_w': nrm((H, C, HS)), 'cq_b': nrm((H, HS)), 'ck_w': nrm((H, C, HS)), 'ck_b': nrm((H, HS)), 'cv_w': nrm((H, C, HS)), 'cv_b': nrm((H, HS)), 'c_proj_w': nrm((C, C)), 'c_proj_b': nrm((C,)), 'f_w1': nrm((C, 4 * C)), 'f_b1': nrm((4 * C,)), 'f_w2': nrm((4 * C, C)), 'f_b2': nrm((C,)), 'ln1_g': jnp.ones((C,), jnp.float32), 'ln1_b': jnp.zeros((C,), jnp.float32), 'ln2_g': jnp.ones((C,), jnp.float32), 'ln2_b': jnp.zeros((C,), jnp.float32), 'ln3_g': jnp.ones((C,), jnp.float32), 'ln3_b': jnp.zeros((C,), jnp.float32)}
        return inp
    _L0_xattn_all = _L0_xattn_setup()
    _L0_xattn_in = {k: v for k, v in _L0_xattn_all.items() if k in ('mq_w', 'mq_b', 'mk_w', 'mk_b', 'mv_w', 'mv_b', 'm_proj_w', 'm_proj_b', 'cq_w', 'cq_b', 'ck_w', 'ck_b', 'cv_w', 'cv_b', 'c_proj_w', 'c_proj_b', 'f_w1', 'f_b1', 'f_w2', 'f_b2', 'ln1_g', 'ln1_b', 'ln2_g', 'ln2_b', 'ln3_g', 'ln3_b')}
    del _L0_xattn_all

    def _L1_xattn_setup():
        import jax, jax.numpy as jnp
        import numpy as np
        B, S, SE, D, H, FF, E, K = (2, 512, 512, 256, 16, 1024, 8, 2)
        HD = D // H

        def _layernorm(x, g, b):
            m = x.mean(-1, keepdims=True)
            v = ((x - m) ** 2).mean(-1, keepdims=True)
            return (x - m) / jnp.sqrt(v + 1e-05) * g + b

        def _attn(q_in, k_in, v_in, wq, bq, wk, bk, wv, bv, wo, bo, causal):
            Bq, Sq, Dm = q_in.shape
            Sk = k_in.shape[1]
            Q = (q_in @ wq + bq).reshape(Bq, Sq, H, HD)
            Kp = (k_in @ wk + bk).reshape(Bq, Sk, H, HD)
            V = (v_in @ wv + bv).reshape(Bq, Sk, H, HD)
            scores = jnp.einsum('bqhd,bkhd->bhqk', Q, Kp) / jnp.sqrt(jnp.float32(HD))
            if causal:
                mask = jnp.tril(jnp.ones((Sq, Sk), bool))
                scores = jnp.where(mask, scores, -jnp.inf)
            a = jax.nn.softmax(scores, axis=-1)
            o = jnp.einsum('bhqk,bkhd->bqhd', a, V).reshape(Bq, Sq, Dm)
            return o @ wo + bo

        def _moe(x, rw, rb, w1, b1, w2, b2):
            T = x.shape[0] * x.shape[1]
            xf = x.reshape(T, D)
            router_weights = jax.nn.softmax(xf @ rw + rb, axis=-1)
            topw, topi = jax.lax.top_k(router_weights, K)
            topw = jax.nn.softmax(topw, axis=-1)
            combine = jnp.zeros((T, E), xf.dtype).at[jnp.arange(T)[:, None], topi].add(topw)
            h = jax.nn.gelu(jnp.einsum('td,edf->etf', xf, w1) + b1[:, None, :], approximate=False)
            eo = jnp.einsum('etf,efd->etd', h, w2) + b2[:, None, :]
            out = jnp.einsum('etd,te->td', eo, combine)
            return out.reshape(x.shape)
        key = jax.random.key(seed)
        ks = jax.random.split(key, 32)
        w = lambda k, shape: jax.random.normal(k, shape, jnp.float32) * 0.02
        inp = {'x': jax.random.normal(ks[0], (B, S, D), jnp.float32), 'encoder_output': jax.random.normal(ks[1], (B, SE, D), jnp.float32), 'sa_wq': w(ks[2], (D, D)), 'sa_bq': jnp.zeros((D,), jnp.float32), 'sa_wk': w(ks[3], (D, D)), 'sa_bk': jnp.zeros((D,), jnp.float32), 'sa_wv': w(ks[4], (D, D)), 'sa_bv': jnp.zeros((D,), jnp.float32), 'sa_wo': w(ks[5], (D, D)), 'sa_bo': jnp.zeros((D,), jnp.float32), 'ca_wq': w(ks[6], (D, D)), 'ca_bq': jnp.zeros((D,), jnp.float32), 'ca_wk': w(ks[7], (D, D)), 'ca_bk': jnp.zeros((D,), jnp.float32), 'ca_wv': w(ks[8], (D, D)), 'ca_bv': jnp.zeros((D,), jnp.float32), 'ca_wo': w(ks[9], (D, D)), 'ca_bo': jnp.zeros((D,), jnp.float32), 'ln1_g': jnp.ones((D,), jnp.float32), 'ln1_b': jnp.zeros((D,), jnp.float32), 'ln2_g': jnp.ones((D,), jnp.float32), 'ln2_b': jnp.zeros((D,), jnp.float32), 'ln3_g': jnp.ones((D,), jnp.float32), 'ln3_b': jnp.zeros((D,), jnp.float32), 'router_w': w(ks[10], (D, E)), 'router_b': jnp.zeros((E,), jnp.float32), 'e_w1': w(ks[11], (E, D, FF)), 'e_b1': jnp.zeros((E, FF), jnp.float32), 'e_w2': w(ks[12], (E, FF, D)), 'e_b2': jnp.zeros((E, D), jnp.float32)}
        return inp
    _L1_xattn_all = _L1_xattn_setup()
    _L1_xattn_in = {k: v for k, v in _L1_xattn_all.items() if k in ('sa_wq', 'sa_bq', 'sa_wk', 'sa_bk', 'sa_wv', 'sa_bv', 'sa_wo', 'sa_bo', 'ca_wq', 'ca_bq', 'ca_wk', 'ca_bk', 'ca_wv', 'ca_bv', 'ca_wo', 'ca_bo', 'ln1_g', 'ln1_b', 'ln2_g', 'ln2_b', 'ln3_g', 'ln3_b', 'router_w', 'router_b', 'e_w1', 'e_b1', 'e_w2', 'e_b2')}
    del _L1_xattn_all

    def _L2_xattn_setup():
        import jax, jax.numpy as jnp
        import numpy as np
        DIM = 256
        HEADS = 16
        HEAD_DIM = DIM // HEADS
        NEG = -1e+30
        EPS = 1e-05

        def _linear(x, w, b):
            return jnp.einsum('bnd,od->bno', x, w) + b

        def _mha(x, ctx, wq, bq, wk, bk, wv, bv, wo, bo, mask):
            B, N, D = x.shape
            M = ctx.shape[1]
            q = _linear(x, wq, bq).reshape(B, N, HEADS, HEAD_DIM).transpose(0, 2, 1, 3)
            k = _linear(ctx, wk, bk).reshape(B, M, HEADS, HEAD_DIM).transpose(0, 2, 1, 3)
            v = _linear(ctx, wv, bv).reshape(B, M, HEADS, HEAD_DIM).transpose(0, 2, 1, 3)
            scores = jnp.einsum('bhqd,bhkd->bhqk', q, k) / np.sqrt(HEAD_DIM).astype(np.float32)
            if mask is not None:
                scores = jnp.where(mask == 0, NEG, scores)
            attn = jax.nn.softmax(scores, axis=-1)
            out = jnp.einsum('bhqk,bhkd->bhqd', attn, v)
            out = out.transpose(0, 2, 1, 3).reshape(B, N, D)
            return _linear(out, wo, bo)

        def _ln(x, g, b):
            mu = jnp.mean(x, axis=-1, keepdims=True)
            var = jnp.mean(jnp.square(x - mu), axis=-1, keepdims=True)
            return (x - mu) * jax.lax.rsqrt(var + EPS) * g + b
        key = jax.random.key(seed)
        ks = jax.random.split(key, 24)
        B, N, M = (2, 512, 256)
        s = 0.02
        d = {'x': jax.random.normal(ks[0], (B, N, DIM), jnp.float32), 'memory': jax.random.normal(ks[1], (B, M, DIM), jnp.float32), 'mask': jnp.tril(jnp.ones((N, N), jnp.int32))[None, None]}
        i = 2
        for p in ['sa', 'ca']:
            for nm in ['q', 'k', 'v', 'o']:
                d[f'{p}_w{nm}'] = jax.random.normal(ks[i], (DIM, DIM), jnp.float32) * s
                i += 1
                d[f'{p}_b{nm}'] = jnp.zeros((DIM,), jnp.float32)
        d['ff_w1'] = jax.random.normal(ks[i], (4 * DIM, DIM), jnp.float32) * s
        i += 1
        d['ff_b1'] = jnp.zeros((4 * DIM,), jnp.float32)
        d['ff_w2'] = jax.random.normal(ks[i], (DIM, 4 * DIM), jnp.float32) * s
        i += 1
        d['ff_b2'] = jnp.zeros((DIM,), jnp.float32)
        for j in (1, 2, 3):
            d[f'ln{j}_g'] = jnp.ones((DIM,), jnp.float32)
            d[f'ln{j}_b'] = jnp.zeros((DIM,), jnp.float32)
        return d
    _L2_xattn_all = _L2_xattn_setup()
    _L2_xattn_in = {k: v for k, v in _L2_xattn_all.items() if k in ('sa_wq', 'sa_bq', 'sa_wk', 'sa_bk', 'sa_wv', 'sa_bv', 'sa_wo', 'sa_bo', 'ca_wq', 'ca_bq', 'ca_wk', 'ca_bk', 'ca_wv', 'ca_bv', 'ca_wo', 'ca_bo', 'ff_w1', 'ff_b1', 'ff_w2', 'ff_b2', 'ln1_g', 'ln1_b', 'ln2_g', 'ln2_b', 'ln3_g', 'ln3_b')}
    del _L2_xattn_all

    def _L3_xattn_setup():
        import jax, jax.numpy as jnp
        import numpy as np
        HEAD_NUM = 16
        DIM = 256
        key = jax.random.key(seed)
        ks = jax.random.split(key, 12)
        B, SQ, SKV, D = (4, 512, 1024, DIM)
        s = 1.0 / np.sqrt(D)
        inp = {'query_seq': jax.random.normal(ks[0], (B, SQ, D), jnp.float32), 'key_value_seq': jax.random.normal(ks[1], (B, SKV, D), jnp.float32), 'Wq': jax.random.normal(ks[2], (D, D), jnp.float32) * s, 'bq': jax.random.normal(ks[3], (D,), jnp.float32) * 0.01, 'Wk': jax.random.normal(ks[4], (D, D), jnp.float32) * s, 'bk': jax.random.normal(ks[5], (D,), jnp.float32) * 0.01, 'Wv': jax.random.normal(ks[6], (D, D), jnp.float32) * s, 'bv': jax.random.normal(ks[7], (D,), jnp.float32) * 0.01, 'Wo': jax.random.normal(ks[8], (D, D), jnp.float32) * s, 'ln_gamma': jnp.ones((D,), jnp.float32), 'ln_beta': jnp.zeros((D,), jnp.float32)}
        return inp
    _L3_xattn_all = _L3_xattn_setup()
    _L3_xattn_in = {k: v for k, v in _L3_xattn_all.items() if k in ('Wq', 'bq', 'Wk', 'bk', 'Wv', 'bv', 'Wo', 'ln_gamma', 'ln_beta')}
    del _L3_xattn_all
    return {'x': x, 'ctx_1024': ctx_1024, 'mask_1x1xSxS_ik0': mask_1x1xSxS_ik0, 'L0_xattn_mq_w': _L0_xattn_in['mq_w'], 'L0_xattn_mq_b': _L0_xattn_in['mq_b'], 'L0_xattn_mk_w': _L0_xattn_in['mk_w'], 'L0_xattn_mk_b': _L0_xattn_in['mk_b'], 'L0_xattn_mv_w': _L0_xattn_in['mv_w'], 'L0_xattn_mv_b': _L0_xattn_in['mv_b'], 'L0_xattn_m_proj_w': _L0_xattn_in['m_proj_w'], 'L0_xattn_m_proj_b': _L0_xattn_in['m_proj_b'], 'L0_xattn_cq_w': _L0_xattn_in['cq_w'], 'L0_xattn_cq_b': _L0_xattn_in['cq_b'], 'L0_xattn_ck_w': _L0_xattn_in['ck_w'], 'L0_xattn_ck_b': _L0_xattn_in['ck_b'], 'L0_xattn_cv_w': _L0_xattn_in['cv_w'], 'L0_xattn_cv_b': _L0_xattn_in['cv_b'], 'L0_xattn_c_proj_w': _L0_xattn_in['c_proj_w'], 'L0_xattn_c_proj_b': _L0_xattn_in['c_proj_b'], 'L0_xattn_f_w1': _L0_xattn_in['f_w1'], 'L0_xattn_f_b1': _L0_xattn_in['f_b1'], 'L0_xattn_f_w2': _L0_xattn_in['f_w2'], 'L0_xattn_f_b2': _L0_xattn_in['f_b2'], 'L0_xattn_ln1_g': _L0_xattn_in['ln1_g'], 'L0_xattn_ln1_b': _L0_xattn_in['ln1_b'], 'L0_xattn_ln2_g': _L0_xattn_in['ln2_g'], 'L0_xattn_ln2_b': _L0_xattn_in['ln2_b'], 'L0_xattn_ln3_g': _L0_xattn_in['ln3_g'], 'L0_xattn_ln3_b': _L0_xattn_in['ln3_b'], 'L1_xattn_sa_wq': _L1_xattn_in['sa_wq'], 'L1_xattn_sa_bq': _L1_xattn_in['sa_bq'], 'L1_xattn_sa_wk': _L1_xattn_in['sa_wk'], 'L1_xattn_sa_bk': _L1_xattn_in['sa_bk'], 'L1_xattn_sa_wv': _L1_xattn_in['sa_wv'], 'L1_xattn_sa_bv': _L1_xattn_in['sa_bv'], 'L1_xattn_sa_wo': _L1_xattn_in['sa_wo'], 'L1_xattn_sa_bo': _L1_xattn_in['sa_bo'], 'L1_xattn_ca_wq': _L1_xattn_in['ca_wq'], 'L1_xattn_ca_bq': _L1_xattn_in['ca_bq'], 'L1_xattn_ca_wk': _L1_xattn_in['ca_wk'], 'L1_xattn_ca_bk': _L1_xattn_in['ca_bk'], 'L1_xattn_ca_wv': _L1_xattn_in['ca_wv'], 'L1_xattn_ca_bv': _L1_xattn_in['ca_bv'], 'L1_xattn_ca_wo': _L1_xattn_in['ca_wo'], 'L1_xattn_ca_bo': _L1_xattn_in['ca_bo'], 'L1_xattn_ln1_g': _L1_xattn_in['ln1_g'], 'L1_xattn_ln1_b': _L1_xattn_in['ln1_b'], 'L1_xattn_ln2_g': _L1_xattn_in['ln2_g'], 'L1_xattn_ln2_b': _L1_xattn_in['ln2_b'], 'L1_xattn_ln3_g': _L1_xattn_in['ln3_g'], 'L1_xattn_ln3_b': _L1_xattn_in['ln3_b'], 'L1_xattn_router_w': _L1_xattn_in['router_w'], 'L1_xattn_router_b': _L1_xattn_in['router_b'], 'L1_xattn_e_w1': _L1_xattn_in['e_w1'], 'L1_xattn_e_b1': _L1_xattn_in['e_b1'], 'L1_xattn_e_w2': _L1_xattn_in['e_w2'], 'L1_xattn_e_b2': _L1_xattn_in['e_b2'], 'L2_xattn_sa_wq': _L2_xattn_in['sa_wq'], 'L2_xattn_sa_bq': _L2_xattn_in['sa_bq'], 'L2_xattn_sa_wk': _L2_xattn_in['sa_wk'], 'L2_xattn_sa_bk': _L2_xattn_in['sa_bk'], 'L2_xattn_sa_wv': _L2_xattn_in['sa_wv'], 'L2_xattn_sa_bv': _L2_xattn_in['sa_bv'], 'L2_xattn_sa_wo': _L2_xattn_in['sa_wo'], 'L2_xattn_sa_bo': _L2_xattn_in['sa_bo'], 'L2_xattn_ca_wq': _L2_xattn_in['ca_wq'], 'L2_xattn_ca_bq': _L2_xattn_in['ca_bq'], 'L2_xattn_ca_wk': _L2_xattn_in['ca_wk'], 'L2_xattn_ca_bk': _L2_xattn_in['ca_bk'], 'L2_xattn_ca_wv': _L2_xattn_in['ca_wv'], 'L2_xattn_ca_bv': _L2_xattn_in['ca_bv'], 'L2_xattn_ca_wo': _L2_xattn_in['ca_wo'], 'L2_xattn_ca_bo': _L2_xattn_in['ca_bo'], 'L2_xattn_ff_w1': _L2_xattn_in['ff_w1'], 'L2_xattn_ff_b1': _L2_xattn_in['ff_b1'], 'L2_xattn_ff_w2': _L2_xattn_in['ff_w2'], 'L2_xattn_ff_b2': _L2_xattn_in['ff_b2'], 'L2_xattn_ln1_g': _L2_xattn_in['ln1_g'], 'L2_xattn_ln1_b': _L2_xattn_in['ln1_b'], 'L2_xattn_ln2_g': _L2_xattn_in['ln2_g'], 'L2_xattn_ln2_b': _L2_xattn_in['ln2_b'], 'L2_xattn_ln3_g': _L2_xattn_in['ln3_g'], 'L2_xattn_ln3_b': _L2_xattn_in['ln3_b'], 'L3_xattn_Wq': _L3_xattn_in['Wq'], 'L3_xattn_bq': _L3_xattn_in['bq'], 'L3_xattn_Wk': _L3_xattn_in['Wk'], 'L3_xattn_bk': _L3_xattn_in['bk'], 'L3_xattn_Wv': _L3_xattn_in['Wv'], 'L3_xattn_bv': _L3_xattn_in['bv'], 'L3_xattn_Wo': _L3_xattn_in['Wo'], 'L3_xattn_ln_gamma': _L3_xattn_in['ln_gamma'], 'L3_xattn_ln_beta': _L3_xattn_in['ln_beta']}

def reference(x, ctx_1024, mask_1x1xSxS_ik0, L0_xattn_mq_w, L0_xattn_mq_b, L0_xattn_mk_w, L0_xattn_mk_b, L0_xattn_mv_w, L0_xattn_mv_b, L0_xattn_m_proj_w, L0_xattn_m_proj_b, L0_xattn_cq_w, L0_xattn_cq_b, L0_xattn_ck_w, L0_xattn_ck_b, L0_xattn_cv_w, L0_xattn_cv_b, L0_xattn_c_proj_w, L0_xattn_c_proj_b, L0_xattn_f_w1, L0_xattn_f_b1, L0_xattn_f_w2, L0_xattn_f_b2, L0_xattn_ln1_g, L0_xattn_ln1_b, L0_xattn_ln2_g, L0_xattn_ln2_b, L0_xattn_ln3_g, L0_xattn_ln3_b, L1_xattn_sa_wq, L1_xattn_sa_bq, L1_xattn_sa_wk, L1_xattn_sa_bk, L1_xattn_sa_wv, L1_xattn_sa_bv, L1_xattn_sa_wo, L1_xattn_sa_bo, L1_xattn_ca_wq, L1_xattn_ca_bq, L1_xattn_ca_wk, L1_xattn_ca_bk, L1_xattn_ca_wv, L1_xattn_ca_bv, L1_xattn_ca_wo, L1_xattn_ca_bo, L1_xattn_ln1_g, L1_xattn_ln1_b, L1_xattn_ln2_g, L1_xattn_ln2_b, L1_xattn_ln3_g, L1_xattn_ln3_b, L1_xattn_router_w, L1_xattn_router_b, L1_xattn_e_w1, L1_xattn_e_b1, L1_xattn_e_w2, L1_xattn_e_b2, L2_xattn_sa_wq, L2_xattn_sa_bq, L2_xattn_sa_wk, L2_xattn_sa_bk, L2_xattn_sa_wv, L2_xattn_sa_bv, L2_xattn_sa_wo, L2_xattn_sa_bo, L2_xattn_ca_wq, L2_xattn_ca_bq, L2_xattn_ca_wk, L2_xattn_ca_bk, L2_xattn_ca_wv, L2_xattn_ca_bv, L2_xattn_ca_wo, L2_xattn_ca_bo, L2_xattn_ff_w1, L2_xattn_ff_b1, L2_xattn_ff_w2, L2_xattn_ff_b2, L2_xattn_ln1_g, L2_xattn_ln1_b, L2_xattn_ln2_g, L2_xattn_ln2_b, L2_xattn_ln3_g, L2_xattn_ln3_b, L3_xattn_Wq, L3_xattn_bq, L3_xattn_Wk, L3_xattn_bk, L3_xattn_Wv, L3_xattn_bv, L3_xattn_Wo, L3_xattn_ln_gamma, L3_xattn_ln_beta):
    import jax
    import jax.numpy as jnp

    def _L0_xattn_ref(x_e, x, mq_w, mq_b, mk_w, mk_b, mv_w, mv_b, m_proj_w, m_proj_b, cq_w, cq_b, ck_w, ck_b, cv_w, cv_b, c_proj_w, c_proj_b, f_w1, f_b1, f_w2, f_b2, ln1_g, ln1_b, ln2_g, ln2_b, ln3_g, ln3_b):
        import jax, jax.numpy as jnp
        import numpy as np
        B, T, SE, C, H = (2, 512, 512, 256, 16)
        HS = C // H
        EPS = 1e-05

        def _ln(x, g, b):
            mu = jnp.mean(x, axis=-1, keepdims=True)
            var = jnp.mean(jnp.square(x - mu), axis=-1, keepdims=True)
            return (x - mu) * jax.lax.rsqrt(var + EPS) * g + b

        def _mha(q_in, kv_in, wq, bq, wk, bk, wv, bv, causal):
            q = jnp.einsum('btc,hcd->bhtd', q_in, wq) + bq[None, :, None, :]
            k = jnp.einsum('bsc,hcd->bhsd', kv_in, wk) + bk[None, :, None, :]
            v = jnp.einsum('bsc,hcd->bhsd', kv_in, wv) + bv[None, :, None, :]
            scores = jnp.einsum('bhtd,bhsd->bhts', q, k) * q.shape[-1] ** (-0.5)
            if causal:
                t, s = (scores.shape[-2], scores.shape[-1])
                mask = jnp.tril(jnp.ones((t, s), bool))
                scores = jnp.where(mask, scores, -jnp.inf)
            p = jax.nn.softmax(scores, axis=-1)
            o = jnp.einsum('bhts,bhsd->bhtd', p, v)
            b_, h_, t_, d_ = o.shape
            return o.transpose(0, 2, 1, 3).reshape(b_, t_, h_ * d_)
        h = _mha(_ln(x, ln1_g, ln1_b), _ln(x, ln1_g, ln1_b), mq_w, mq_b, mk_w, mk_b, mv_w, mv_b, causal=True)
        x = x + h @ m_proj_w + m_proj_b
        h = _mha(_ln(x, ln2_g, ln2_b), x_e, cq_w, cq_b, ck_w, ck_b, cv_w, cv_b, causal=False)
        x = x + h @ c_proj_w + c_proj_b
        h = jax.nn.relu(_ln(x, ln3_g, ln3_b) @ f_w1 + f_b1) @ f_w2 + f_b2
        return x + h

    def _L1_xattn_ref(x, encoder_output, sa_wq, sa_bq, sa_wk, sa_bk, sa_wv, sa_bv, sa_wo, sa_bo, ca_wq, ca_bq, ca_wk, ca_bk, ca_wv, ca_bv, ca_wo, ca_bo, ln1_g, ln1_b, ln2_g, ln2_b, ln3_g, ln3_b, router_w, router_b, e_w1, e_b1, e_w2, e_b2):
        import jax, jax.numpy as jnp
        import numpy as np
        B, S, SE, D, H, FF, E, K = (2, 512, 512, 256, 16, 1024, 8, 2)
        HD = D // H

        def _layernorm(x, g, b):
            m = x.mean(-1, keepdims=True)
            v = ((x - m) ** 2).mean(-1, keepdims=True)
            return (x - m) / jnp.sqrt(v + 1e-05) * g + b

        def _attn(q_in, k_in, v_in, wq, bq, wk, bk, wv, bv, wo, bo, causal):
            Bq, Sq, Dm = q_in.shape
            Sk = k_in.shape[1]
            Q = (q_in @ wq + bq).reshape(Bq, Sq, H, HD)
            Kp = (k_in @ wk + bk).reshape(Bq, Sk, H, HD)
            V = (v_in @ wv + bv).reshape(Bq, Sk, H, HD)
            scores = jnp.einsum('bqhd,bkhd->bhqk', Q, Kp) / jnp.sqrt(jnp.float32(HD))
            if causal:
                mask = jnp.tril(jnp.ones((Sq, Sk), bool))
                scores = jnp.where(mask, scores, -jnp.inf)
            a = jax.nn.softmax(scores, axis=-1)
            o = jnp.einsum('bhqk,bkhd->bqhd', a, V).reshape(Bq, Sq, Dm)
            return o @ wo + bo

        def _moe(x, rw, rb, w1, b1, w2, b2):
            T = x.shape[0] * x.shape[1]
            xf = x.reshape(T, D)
            router_weights = jax.nn.softmax(xf @ rw + rb, axis=-1)
            topw, topi = jax.lax.top_k(router_weights, K)
            topw = jax.nn.softmax(topw, axis=-1)
            combine = jnp.zeros((T, E), xf.dtype).at[jnp.arange(T)[:, None], topi].add(topw)
            h = jax.nn.gelu(jnp.einsum('td,edf->etf', xf, w1) + b1[:, None, :], approximate=False)
            eo = jnp.einsum('etf,efd->etd', h, w2) + b2[:, None, :]
            out = jnp.einsum('etd,te->td', eo, combine)
            return out.reshape(x.shape)
        x = _layernorm(x + _attn(x, x, x, sa_wq, sa_bq, sa_wk, sa_bk, sa_wv, sa_bv, sa_wo, sa_bo, True), ln1_g, ln1_b)
        x = _layernorm(x + _attn(x, encoder_output, encoder_output, ca_wq, ca_bq, ca_wk, ca_bk, ca_wv, ca_bv, ca_wo, ca_bo, False), ln2_g, ln2_b)
        x = _layernorm(x + _moe(x, router_w, router_b, e_w1, e_b1, e_w2, e_b2), ln3_g, ln3_b)
        return x

    def _L2_xattn_ref(x, memory, mask, sa_wq, sa_bq, sa_wk, sa_bk, sa_wv, sa_bv, sa_wo, sa_bo, ca_wq, ca_bq, ca_wk, ca_bk, ca_wv, ca_bv, ca_wo, ca_bo, ff_w1, ff_b1, ff_w2, ff_b2, ln1_g, ln1_b, ln2_g, ln2_b, ln3_g, ln3_b):
        import jax, jax.numpy as jnp
        import numpy as np
        DIM = 256
        HEADS = 16
        HEAD_DIM = DIM // HEADS
        NEG = -1e+30
        EPS = 1e-05

        def _linear(x, w, b):
            return jnp.einsum('bnd,od->bno', x, w) + b

        def _mha(x, ctx, wq, bq, wk, bk, wv, bv, wo, bo, mask):
            B, N, D = x.shape
            M = ctx.shape[1]
            q = _linear(x, wq, bq).reshape(B, N, HEADS, HEAD_DIM).transpose(0, 2, 1, 3)
            k = _linear(ctx, wk, bk).reshape(B, M, HEADS, HEAD_DIM).transpose(0, 2, 1, 3)
            v = _linear(ctx, wv, bv).reshape(B, M, HEADS, HEAD_DIM).transpose(0, 2, 1, 3)
            scores = jnp.einsum('bhqd,bhkd->bhqk', q, k) / np.sqrt(HEAD_DIM).astype(np.float32)
            if mask is not None:
                scores = jnp.where(mask == 0, NEG, scores)
            attn = jax.nn.softmax(scores, axis=-1)
            out = jnp.einsum('bhqk,bhkd->bhqd', attn, v)
            out = out.transpose(0, 2, 1, 3).reshape(B, N, D)
            return _linear(out, wo, bo)

        def _ln(x, g, b):
            mu = jnp.mean(x, axis=-1, keepdims=True)
            var = jnp.mean(jnp.square(x - mu), axis=-1, keepdims=True)
            return (x - mu) * jax.lax.rsqrt(var + EPS) * g + b
        x = _ln(x + _mha(x, x, sa_wq, sa_bq, sa_wk, sa_bk, sa_wv, sa_bv, sa_wo, sa_bo, mask), ln1_g, ln1_b)
        x = _ln(x + _mha(x, memory, ca_wq, ca_bq, ca_wk, ca_bk, ca_wv, ca_bv, ca_wo, ca_bo, None), ln2_g, ln2_b)
        h = jax.nn.relu(_linear(x, ff_w1, ff_b1))
        x = _ln(x + _linear(h, ff_w2, ff_b2), ln3_g, ln3_b)
        return x

    def _L3_xattn_ref(query_seq, key_value_seq, Wq, bq, Wk, bk, Wv, bv, Wo, ln_gamma, ln_beta):
        import jax, jax.numpy as jnp
        import numpy as np
        HEAD_NUM = 16
        DIM = 256
        B, SQ, D = query_seq.shape
        H = HEAD_NUM
        hd = D // H
        Q = query_seq @ Wq + bq
        K = key_value_seq @ Wk + bk
        V = key_value_seq @ Wv + bv
        Q = Q.reshape(B, SQ, H, hd).transpose(0, 2, 1, 3)
        K = K.reshape(B, -1, H, hd).transpose(0, 2, 1, 3)
        V = V.reshape(B, -1, H, hd).transpose(0, 2, 1, 3)
        scores = jnp.einsum('bhqd,bhkd->bhqk', Q, K) / jnp.sqrt(jnp.float32(hd))
        attn = jax.nn.softmax(scores, axis=-1)
        ctx = jnp.einsum('bhqk,bhkd->bhqd', attn, V)
        ctx = ctx.transpose(0, 2, 1, 3).reshape(B, SQ, D)
        attended = ctx @ Wo
        x = query_seq + attended
        mu = jnp.mean(x, axis=-1, keepdims=True)
        var = jnp.var(x, axis=-1, keepdims=True)
        y = (x - mu) * jax.lax.rsqrt(var + 1e-05) * ln_gamma + ln_beta
        return y
    x = _L0_xattn_ref(ctx_1024, x, L0_xattn_mq_w, L0_xattn_mq_b, L0_xattn_mk_w, L0_xattn_mk_b, L0_xattn_mv_w, L0_xattn_mv_b, L0_xattn_m_proj_w, L0_xattn_m_proj_b, L0_xattn_cq_w, L0_xattn_cq_b, L0_xattn_ck_w, L0_xattn_ck_b, L0_xattn_cv_w, L0_xattn_cv_b, L0_xattn_c_proj_w, L0_xattn_c_proj_b, L0_xattn_f_w1, L0_xattn_f_b1, L0_xattn_f_w2, L0_xattn_f_b2, L0_xattn_ln1_g, L0_xattn_ln1_b, L0_xattn_ln2_g, L0_xattn_ln2_b, L0_xattn_ln3_g, L0_xattn_ln3_b)
    x = _L1_xattn_ref(x, ctx_1024, L1_xattn_sa_wq, L1_xattn_sa_bq, L1_xattn_sa_wk, L1_xattn_sa_bk, L1_xattn_sa_wv, L1_xattn_sa_bv, L1_xattn_sa_wo, L1_xattn_sa_bo, L1_xattn_ca_wq, L1_xattn_ca_bq, L1_xattn_ca_wk, L1_xattn_ca_bk, L1_xattn_ca_wv, L1_xattn_ca_bv, L1_xattn_ca_wo, L1_xattn_ca_bo, L1_xattn_ln1_g, L1_xattn_ln1_b, L1_xattn_ln2_g, L1_xattn_ln2_b, L1_xattn_ln3_g, L1_xattn_ln3_b, L1_xattn_router_w, L1_xattn_router_b, L1_xattn_e_w1, L1_xattn_e_b1, L1_xattn_e_w2, L1_xattn_e_b2)
    x = _L2_xattn_ref(x, ctx_1024, mask_1x1xSxS_ik0, L2_xattn_sa_wq, L2_xattn_sa_bq, L2_xattn_sa_wk, L2_xattn_sa_bk, L2_xattn_sa_wv, L2_xattn_sa_bv, L2_xattn_sa_wo, L2_xattn_sa_bo, L2_xattn_ca_wq, L2_xattn_ca_bq, L2_xattn_ca_wk, L2_xattn_ca_bk, L2_xattn_ca_wv, L2_xattn_ca_bv, L2_xattn_ca_wo, L2_xattn_ca_bo, L2_xattn_ff_w1, L2_xattn_ff_b1, L2_xattn_ff_w2, L2_xattn_ff_b2, L2_xattn_ln1_g, L2_xattn_ln1_b, L2_xattn_ln2_g, L2_xattn_ln2_b, L2_xattn_ln3_g, L2_xattn_ln3_b)
    x = _L3_xattn_ref(x, ctx_1024, L3_xattn_Wq, L3_xattn_bq, L3_xattn_Wk, L3_xattn_bk, L3_xattn_Wv, L3_xattn_bv, L3_xattn_Wo, L3_xattn_ln_gamma, L3_xattn_ln_beta)
    return x

_drawn_inputs = setup_inputs


def setup_inputs(seed=0):
    import zlib

    import numpy as np

    out = dict(_drawn_inputs(seed))
    spreads = {'L0_xattn_ln1_g': (1.0, 0.6),
     'L0_xattn_ln1_b': (0.0, 0.556),
     'L0_xattn_ln2_g': (1.0, 0.6),
     'L0_xattn_ln2_b': (0.0, 0.8),
     'L0_xattn_ln3_g': (1.0, 0.2),
     'L0_xattn_ln3_b': (0.0, 0.46),
     'L1_xattn_sa_bq': (0.0, 0.8),
     'L1_xattn_sa_bk': (0.0, 2.0),
     'L1_xattn_sa_bv': (0.0, 0.1),
     'L1_xattn_sa_bo': (0.0, 0.1),
     'L1_xattn_ca_bq': (0.0, 0.8),
     'L1_xattn_ca_bk': (0.0, 2.0),
     'L1_xattn_ca_bv': (0.0, 0.1),
     'L1_xattn_ca_bo': (0.0, 0.1),
     'L1_xattn_ln1_g': (1.0, 0.2),
     'L1_xattn_ln1_b': (0.0, 0.1),
     'L1_xattn_ln2_g': (1.0, 0.2),
     'L1_xattn_ln2_b': (0.0, 0.1),
     'L1_xattn_ln3_g': (1.0, 0.2),
     'L1_xattn_ln3_b': (0.0, 0.1),
     'L1_xattn_router_b': (0.0, 0.1),
     'L1_xattn_e_b1': (0.0, 0.404),
     'L1_xattn_e_b2': (0.0, 0.1),
     'L2_xattn_sa_bq': (0.0, 0.8),
     'L2_xattn_sa_bk': (0.0, 2.0),
     'L2_xattn_sa_bv': (0.0, 0.277),
     'L2_xattn_sa_bo': (0.0, 0.1),
     'L2_xattn_ca_bq': (0.0, 0.8),
     'L2_xattn_ca_bk': (0.0, 2.0),
     'L2_xattn_ca_bv': (0.0, 0.272),
     'L2_xattn_ca_bo': (0.0, 0.1),
     'L2_xattn_ff_b1': (0.0, 0.1),
     'L2_xattn_ff_b2': (0.0, 0.1),
     'L2_xattn_ln1_g': (1.0, 0.2),
     'L2_xattn_ln1_b': (0.0, 0.1),
     'L2_xattn_ln2_g': (1.0, 0.2),
     'L2_xattn_ln2_b': (0.0, 0.1),
     'L2_xattn_ln3_g': (1.0, 0.2),
     'L2_xattn_ln3_b': (0.0, 0.1),
     'L3_xattn_ln_gamma': (1.0, 0.2),
     'L3_xattn_ln_beta': (0.0, 0.1)}
    factors = {'L0_xattn_mq_w': 8.0,
     'L0_xattn_mq_b': 8.0,
     'L0_xattn_mk_w': 8.0,
     'L0_xattn_mk_b': 64.0,
     'L0_xattn_mv_w': 2.8,
     'L0_xattn_mv_b': 7.609,
     'L0_xattn_cq_w': 8.0,
     'L0_xattn_cq_b': 30.975,
     'L0_xattn_ck_w': 8.0,
     'L0_xattn_ck_b': 64.0,
     'L0_xattn_cv_b': 6.202,
     'L0_xattn_c_proj_b': 2.823,
     'L0_xattn_f_b1': 4.832,
     'L0_xattn_f_b2': 2.726,
     'L1_xattn_sa_wq': 8.0,
     'L1_xattn_sa_wk': 8.0,
     'L1_xattn_sa_wv': 2.763,
     'L1_xattn_ca_wq': 8.0,
     'L1_xattn_ca_wk': 8.0,
     'L2_xattn_sa_wq': 8.0,
     'L2_xattn_sa_wk': 8.0,
     'L2_xattn_ca_wq': 8.0,
     'L2_xattn_ca_wk': 8.0,
     'L3_xattn_bq': 31.79,
     'L3_xattn_bk': 64.0,
     'L3_xattn_bv': 6.945}
    for name, (base, spread) in spreads.items():
        noise = np.random.default_rng([zlib.crc32(name.encode()), seed]).standard_normal(out[name].shape)
        drawn = base * np.exp(spread * noise) if base else spread * noise
        out[name] = jnp.asarray(drawn.astype(out[name].dtype))
    for name, factor in factors.items():
        out[name] = (out[name] * factor).astype(out[name].dtype)
    return out
```

```python
from contextlib import ExitStack

import numpy as np
import concourse.bass as bass
import concourse.mybir as mybir

F32, BF16 = mybir.dt.float32, mybir.dt.bfloat16
I32, U32 = mybir.dt.int32, mybir.dt.uint32
ALU = mybir.AluOpType
ACT = mybir.ActivationFunctionType
AX = mybir.AxisListType

P = 128
B, S, D = 16, 256, 256
H, HD = 16, 16
C = 77
FF, E = 1024, 8
NB = 2
T = NB * S
NT = T // P
TRIPS = B // NB
KT = D // P
FT = FF // P
QT = S // P
NPART = 3
STACK = 6 * HD
EPS = 1e-5
NEG = -float(2 ** 100)
SCALE = HD ** -0.5


class Token:

    def __init__(self, line, k, back=0):
        self.line, self.k, self.back = line, k, back

    @property
    def prev(self):
        return Token(self.line, self.k, 1)


class Late:

    def __init__(self):
        self.tokens = ()


class Line:

    def __init__(self, sem, step, ahead):
        self.sem, self.step, self.ahead, self.n = sem, step, ahead, 0

    def count(self):
        self.n += 1
        return Token(self, self.n)


class Loop:

    ENGINES = ("sync", "tensor", "scalar", "vector", "gpsimd")

    def __init__(self, nc, ctx, name, trips):
        self.nc, self.ctx, self.name, self.trips = nc, ctx, name, trips
        self.queue = {e: [] for e in self.ENGINES}
        self.before = {e: [] for e in self.ENGINES}
        self.lines = {}
        self.owner = {}
        self.carrier = {e: ctx.enter_context(nc.semaphore(f"{name}_{e}_waits")) for e in self.ENGINES}

    def line(self, name, owner, step):
        if name not in self.lines:
            sem = self.ctx.enter_context(self.nc.semaphore(f"{self.name}_{name}"))
            self.lines[name] = Line(sem, step, not (owner == "gpsimd" and step == 16))
            self.owner[name] = owner
        return self.lines[name]

    def do(self, engine, emit):
        line = self.line(f"{engine}_done", engine, 1)
        self.queue[engine].append(("do", emit, line))
        return line.count()

    def quiet(self, engine, emit):
        self.queue[engine].append(("do", emit, None))

    def dma(self, engine, stream, emit):
        line = self.line(f"dma_{stream}", engine, 16)
        self.queue[engine].append(("do", emit, line))
        return line.count()

    def wait(self, engine, *tokens, alone=None):
        self.queue[engine].append(("wait", tokens, engine in ("sync", "gpsimd") if alone is None else alone))

    def emit(self, block):
        for engine in self.ENGINES:
            getter = {"sync": block.sync, "tensor": block.tensor, "scalar": block.scalar,
                      "vector": block.vector, "gpsimd": block.gpsimd}[engine]
            getter(lambda eng, engine=engine: self.run(engine, eng))

    def run(self, engine, eng):
        for name, line in self.lines.items():
            if self.owner[name] == engine and line.ahead:
                eng.sem_inc(line.sem, line.n * line.step)
        with eng.Fori(0, self.trips) as i:
            seen = {}
            for kind, what, line in self.queue[engine]:
                if kind == "do":
                    ins = what(i)
                    if line is not None:
                        ins.then_inc(line.sem, line.step)
                    continue
                for t in flat(what):
                    assert t.line.ahead or not t.back
                    level = t.k + (t.line.n if t.line.ahead and not t.back else 0)
                    if seen.get(id(t.line), -1) >= level:
                        continue
                    seen[id(t.line)] = level
                    eng.wait_ge(t.line.sem, i * (t.line.n * t.line.step) + level * t.line.step)
                    if line:
                        eng.sem_inc(self.carrier[engine], 1)
        for name, line in self.lines.items():
            if self.owner[name] == engine and name.startswith("dma_"):
                eng.wait_ge(line.sem, (self.trips + line.ahead) * line.n * line.step)


def flat(tokens):
    for t in tokens:
        if isinstance(t, Token):
            yield t
        elif isinstance(t, Late):
            yield from (x.prev for x in flat(t.tokens))
        else:
            yield from flat(t)


class Buffer:

    def __init__(self, ap):
        self.ap, self.ready, self.carried = ap, (), Late()
        self.free = (self.carried,)

    def written(self, *tokens):
        self.ready, self.free = tokens, ()

    def read(self, *tokens):
        self.free += tokens

    def close(self):
        self.carried.tokens = () if self.free == (self.carried,) else self.free


class Ring:

    def __init__(self, aps):
        self.buffers, self.at = [Buffer(ap) for ap in aps], 0

    def next(self):
        self.at += 1
        return self.buffers[(self.at - 1) % len(self.buffers)]


def whole(handle):
    return handle[tuple(slice(None) for _ in handle.shape)]


class Work:

    def __init__(self, nc, ctx, name, loop):
        self.nc, self.ctx, self.name, self.loop = nc, ctx, name, loop
        self.all = []

    def sb(self, name, shape, dt=F32):
        return whole(self.ctx.enter_context(self.nc.sbuf_tensor(f"{self.name}_{name}", shape, dt)))

    def buffer(self, name, shape, dt=F32):
        b = Buffer(self.sb(name, shape, dt))
        self.all.append(b)
        return b

    def ring(self, name, n, shape, dt=F32):
        r = Ring([self.sb(f"{name}{k}", shape, dt) for k in range(n)])
        self.all += r.buffers
        return r

    def psum(self, name, banks, width=512):
        r = Ring([whole(self.ctx.enter_context(self.nc.psum_tensor(f"{self.name}_{name}{k}", [P, b, width], F32)))
                  for k, b in enumerate(banks)])
        self.all += r.buffers
        return r

    def close(self):
        for b in self.all:
            b.close()


def transpose_tokens(w, src, dst, b, scale=None, bias=None, ident=None):
    nc, loop = w.nc, w.loop
    bank = w.pj.next()
    loop.wait("tensor", bank.free, src.ready)
    for k in range(KT):
        for q in range(QT):
            t = QT * b + q
            emit = lambda i, k=k, q=q, t=t: nc.tensor.transpose(
                bank.ap[:, 0, k * S + q * P:k * S + (q + 1) * P], src.ap[:, t, k * P:(k + 1) * P], w.identf)
            turned = loop.do("tensor", emit)
    bank.written(turned)
    src.read(turned)
    loop.wait("scalar", turned, dst.free)
    if scale is None:
        put = loop.do("scalar", lambda i: nc.scalar.activation(
            dst.ap[:, :, b * S:(b + 1) * S], bank.ap[:, 0, :].rearrange("p (k t) -> p k t", k=KT), ACT.Copy))
    else:
        for k in range(KT):
            put = loop.do("scalar", lambda i, k=k: nc.scalar.activation(
                dst.ap[:, k, b * S:(b + 1) * S], bank.ap[:, 0, k * S:(k + 1) * S], ACT.Identity,
                bias=bias[:, k:k + 1], scale=scale[:, k:k + 1]))
    bank.free = (put,)
    return put


def normalise(w, x, out):
    nc, loop = w.nc, w.loop
    st, mv, rs = w.ln_stats, w.ln_moments, w.ln_rstd
    loop.wait("vector", x.ready, st.free)
    for t in range(NT):
        got = loop.do("vector", lambda i, t=t: nc.vector.bn_stats(st.ap[:, t, :], x.ap[:, t, :]))
    st.written(got)
    loop.wait("vector", got, mv.free, alone=True)
    for t in range(NT):
        got = loop.do("vector", lambda i, t=t: nc.vector.bn_aggr(mv.ap[:, t, :], st.ap[:, t, :]))
    mv.written(got)
    st.read(got)
    loop.wait("gpsimd", got, rs.free)
    e = loop.do("gpsimd", lambda i: nc.gpsimd.tensor_scalar(rs.ap[:, 0, :], mv.ap[:, :, 1], EPS, None, ALU.add))
    loop.wait("gpsimd", e)
    r = loop.do("gpsimd", lambda i: nc.gpsimd.tensor_tensor(rs.ap[:, 1, :], rs.ap[:, 0, :], w.minus_half, ALU.pow))
    rs.written(r)
    loop.wait("vector", r, out.free)
    for t in range(NT):
        put = loop.do("vector", lambda i, t=t: nc.vector.tensor_scalar(
            out.ap[:, t, :], x.ap[:, t, :], mv.ap[:, t, 0:1], rs.ap[:, 1, t:t + 1], ALU.subtract, ALU.mult))
    x.read(put)
    mv.read(put)
    rs.read(put)
    out.written(put)


def gain_and_shift(w, x, g, b):
    nc, loop = w.nc, w.loop
    loop.wait("gpsimd", x.ready, x.free)
    m = loop.do("gpsimd", lambda i: nc.gpsimd.tensor_tensor(x.ap[:, :, :], x.ap[:, :, :], g, ALU.mult))
    loop.wait("gpsimd", m)
    a = loop.do("gpsimd", lambda i: nc.gpsimd.tensor_tensor(x.ap[:, :, :], x.ap[:, :, :], b, ALU.add))
    x.written(a)


def project_parts(w, weight, bias, x, n, parts):
    nc, loop = w.nc, w.loop
    rest = w.rest.next()
    loop.wait("scalar", parts.free)
    loop.wait("vector", rest.free)
    loop.wait("gpsimd", parts.free)
    done, rests = [], []
    for m in range(KT):
        bank = w.pj.next()
        loop.wait("tensor", bank.free, x.ready)
        for k in range(KT):
            mm = loop.do("tensor", lambda i, k=k, m=m, bank=bank: nc.tensor.matmul(
                bank.ap[:, 0, 0:n], weight[:, k, m * P:(m + 1) * P], x.ap[:, k, 0:n],
                start=(k == 0), stop=(k == KT - 1)))
        loop.wait("scalar", mm)
        p1 = loop.do("scalar", lambda i, m=m, bank=bank: nc.scalar.activation(
            parts.ap[:, 0, m, 0:n], bank.ap[:, 0, 0:n], ACT.Identity, bias=bias[:, m:m + 1]))
        loop.wait("vector", p1)
        r1 = loop.do("vector", lambda i, m=m, bank=bank: nc.vector.scalar_tensor_tensor(
            rest.ap[:, m, 0:n], bank.ap[:, 0, 0:n], bias[:, m:m + 1], parts.ap[:, 0, m, 0:n],
            ALU.add, ALU.subtract))
        bank.free = (r1,)
        loop.wait("gpsimd", r1)
        p2 = loop.do("gpsimd", lambda i, m=m: nc.gpsimd.tensor_copy(parts.ap[:, 1, m, 0:n], rest.ap[:, m, 0:n]))
        loop.wait("gpsimd", p2)
        p3 = loop.do("gpsimd", lambda i, m=m: nc.gpsimd.tensor_tensor(
            parts.ap[:, 2, m, 0:n], rest.ap[:, m, 0:n], parts.ap[:, 1, m, 0:n], ALU.subtract))
        done.append(p3)
        rests.append(p3)
    rest.free = (rests[-1],)
    x.read(mm)
    parts.written(*done)


def stack_parts(w, parts, scratch, stacked, n, order, name):
    nc, loop = w.nc, w.loop
    loop.wait("sync", scratch.free)
    for m in range(KT):
        loop.wait("sync", parts.ready[m])
        out = loop.dma("sync", f"{name}_out", lambda i, m=m: nc.sync.dma_start(
            scratch.ap[:, m * P:(m + 1) * P, 0:n].rearrange("s p t -> p s t"), parts.ap[:, :, m, 0:n]))
    parts.read(out)
    loop.wait("sync", out, stacked.free)
    for first, sources in order:
        k = len(sources)
        for j, s in enumerate(sources):
            back = loop.dma("sync", f"{name}_in", lambda i, j=j, s=s: nc.sync.dma_start(
                stacked.ap[(first + j) * HD:(first + j + 1) * HD, :, 0:n],
                scratch.ap[s, :, 0:n].rearrange("(h d) t -> d h t", d=HD)))
    scratch.free = (back,)
    stacked.written(back)


Q_ORDER = [(0, (0, 0, 1, 1, 0, 2))]
K_ORDER = [(0, (0, 1, 0, 1, 2, 0))]


def project_values(w, weight, x, tiles, values):
    nc, loop = w.nc, w.loop
    loop.wait("vector", values.free)
    for a in range(0, len(tiles), 2):
        bank = w.pj.next()
        loop.wait("tensor", bank.free, x.ready)
        pair = tiles[a:a + 2]
        for j, (at, keys) in enumerate(pair):
            for k in range(KT):
                mm = loop.do("tensor", lambda i, j=j, at=at, keys=keys, k=k, bank=bank: nc.tensor.matmul(
                    bank.ap[0:keys, 0, j * D:(j + 1) * D], x.ap[:, k, at:at + keys], weight[:, k, :],
                    start=(k == 0), stop=(k == KT - 1)))
        loop.wait("vector", mm)
        keys = pair[0][1]
        for j in range(len(pair)):
            put = loop.do("vector", lambda i, a=a, j=j, keys=keys, bank=bank: nc.vector.tensor_copy(
                values.ap[0:keys, a + j, :, 0:HD],
                bank.ap[0:keys, 0, j * D:(j + 1) * D].rearrange("p (h d) -> p h d", d=HD)))
        bank.free = (put,)
    x.read(mm)
    values.written(put)


def attend(w, qs, ks, values, keys_of, n_key_tiles, causal, mask, heads_t, bv):
    nc, loop = w.nc, w.loop
    G = 2
    maxima = w.maxima
    loop.wait("vector", maxima.free)

    def score_mask(ap, m, last):
        return loop.do("tensor", lambda i: nc.tensor.matmul(ap, w.identb, m, start=False, stop=True))

    got_max = [[], []]

    def query_major(b, hp):
        bank = w.sc.next()
        at, n = keys_of(b)
        loop.wait("tensor", bank.free, qs.ready, ks.ready)
        for j in range(G):
            h = G * hp + j
            off = 0
            for q in range(QT):
                m = P * (q + 1) if causal else n
                mm = loop.do("tensor", lambda i, j=j, h=h, q=q, m=m, off=off: nc.tensor.matmul(
                    bank.ap[:, j, off:off + m], qs.ap[0:STACK, h, b * S + q * P:b * S + (q + 1) * P],
                    ks.ap[0:STACK, h, at:at + m], start=True, stop=(mask is None)))
                if mask is not None:
                    mo, mw = (off + q * P, P) if causal else (off, n)
                    mm = score_mask(bank.ap[:, j, mo:mo + mw], mask[0][:, q, q * P:(q + 1) * P] if causal
                                    else mask[0][:, q, :], True)
                off += m
        loop.wait("vector", mm)
        heads = slice(G * hp, G * (hp + 1))
        if causal:
            off = 0
            for q in range(QT):
                m = P * (q + 1)
                r = loop.do("vector", lambda i, q=q, m=m, off=off: nc.vector.tensor_reduce(
                    maxima.ap[:, QT * b + q, heads], bank.ap[:, :, off:off + m], AX.X, ALU.max))
                off += m
        else:
            r = loop.do("vector", lambda i: nc.vector.tensor_reduce(
                maxima.ap[:, QT * b:QT * (b + 1), heads].rearrange("p q h -> p h q"),
                bank.ap[:, :, 0:QT * n].rearrange("p j (q n) -> p j q n", q=QT), AX.X, ALU.max))
        bank.free = (r,)
        got_max[b] = (r,)

    def shift_rows(b):
        bank = w.pj.next()
        loop.wait("tensor", bank.free, got_max[b])
        for q in range(QT):
            tr = loop.do("tensor", lambda i, q=q: nc.tensor.transpose(
                bank.ap[0:H, 0, q * P:(q + 1) * P], maxima.ap[:, QT * b + q, :], w.identf))
        nm, rest = w.shift.next(), w.shift_rest.next()
        src = bank.ap[0:H, 0, 0:S]
        loop.wait("scalar", tr, nm.free)
        p1 = loop.do("scalar", lambda i: nc.scalar.mul(nm.ap[:, 0, :], src, -1.0))
        loop.wait("vector", p1, rest.free)
        r1 = loop.do("vector", lambda i: nc.vector.scalar_tensor_tensor(
            rest.ap[:, :], src, -1.0, nm.ap[:, 0, :], ALU.mult, ALU.subtract))
        bank.free = (r1,)
        loop.wait("vector", r1)
        p2 = loop.do("vector", lambda i: nc.vector.tensor_copy(nm.ap[:, 1, :], rest.ap[:, :]))
        loop.wait("vector", p2)
        p3 = loop.do("vector", lambda i: nc.vector.tensor_tensor(nm.ap[:, 2, :], rest.ap[:, :], nm.ap[:, 1, :],
                                                                  ALU.subtract))
        rest.free = (p3,)
        loop.wait("sync", p3, w.shift_dram.free)
        out = loop.dma("sync", "shift_out", lambda i: nc.sync.dma_start(
            w.shift_dram.ap[b].rearrange("s h t -> h s t"), nm.ap[:, :, :]))
        nm.free = (out,)
        loop.wait("sync", out)
        back = loop.dma("sync", "shift_in", lambda i: nc.sync.dma_start(
            qs.ap[STACK:STACK + NPART, :, b * S:(b + 1) * S], w.shift_dram.ap[b]))
        w.shift_dram.free = (back,)
        return tr, back

    turned = [None, None]
    shifted = [None, None]
    for b in range(NB):
        for hp in range(H // G):
            query_major(b, hp)
            if b == 1 and hp == 2:
                turned[0], shifted[0] = shift_rows(0)
    turned[1], shifted[1] = shift_rows(1)
    maxima.free = (turned[1],)

    kmajor_last = None
    loop.wait("scalar", heads_t.free)
    for b in range(NB):
        at, n = keys_of(b)
        outs = []
        o_bank = None
        for g in range(H // 4):
            pr = w.prob.next()
            for hp in range(2):
                bank = w.sc.next()
                loop.wait("tensor", bank.free, shifted[b])
                width = 0
                for j in range(G):
                    h = 4 * g + G * hp + j
                    width = 0
                    for kt in range(n_key_tiles):
                        kn = min(P, n - kt * P)
                        q0 = kt * P if causal else 0
                        qn = S - q0
                        mm = loop.do("tensor", lambda i, b=b, at=at, j=j, h=h, kt=kt, kn=kn, q0=q0, qn=qn, width=width, bank=bank:
                                     nc.tensor.matmul(
                                         bank.ap[0:kn, j, width:width + qn],
                                         ks.ap[0:STACK + NPART, h, at + kt * P:at + kt * P + kn],
                                         qs.ap[0:STACK + NPART, h, b * S + q0:b * S + q0 + qn],
                                         start=True, stop=(mask is None)))
                        if mask is not None:
                            mn = P if causal else qn
                            mm = score_mask(bank.ap[:, j, width:width + mn],
                                            mask[1][:, kt, q0:q0 + mn], True)
                        width += qn
                loop.wait("scalar", mm, pr.free)
                rows = min(P, n)
                ex = loop.do("scalar", lambda i, hp=hp, bank=bank, pr=pr, width=width, rows=rows: nc.scalar.activation(
                    pr.ap[0:rows, G * hp:G * (hp + 1), 0:width], bank.ap[0:rows, :, 0:width], ACT.Exp, scale=SCALE))
                bank.free = (ex,)
            kmajor_last = mm
            if g % 2 == 0:
                o_bank = w.pv.next()
                loop.wait("tensor", o_bank.free)
            loop.wait("tensor", ex, values.ready)
            base = (g % 2) * S
            at_p = 0
            for kt in range(n_key_tiles):
                kn = min(P, n - kt * P)
                q0 = kt * P if causal else 0
                qn = S - q0
                for j in range(4):
                    mm = loop.do("tensor", lambda i, b=b, j=j, kt=kt, kn=kn, q0=q0, qn=qn, at_p=at_p, base=base, g=g,
                                 pr=pr, o_bank=o_bank: nc.tensor.matmul(
                                     o_bank.ap[32 * j:32 * j + 32, 0, base + q0:base + S],
                                     values.ap[0:kn, n_key_tiles * b + kt, 4 * g + j, :],
                                     pr.ap[0:kn, j, at_p:at_p + qn],
                                     start=(kt == 0), stop=(kt == n_key_tiles - 1), tile_position=(0, 32 * j)))
                at_p += qn
            pr.free = (mm,)
            if g % 2 == 1:
                raw = w.raw.next()
                loop.wait("vector", mm, raw.free)
                ev = loop.do("vector", lambda i, raw=raw, o_bank=o_bank: nc.vector.tensor_copy(
                    raw.ap[:, :], o_bank.ap[:, 0, :]))
                raw.written(ev)
                o_bank.free = (ev,)
                outs.append(raw)
        heads_bank = None
        normed = w.normed.next()
        loop.wait("vector", normed.free)
        for q in range(QT):
            bank = w.pv.next()
            loop.wait("tensor", bank.free)
            for g in range(H // 4):
                loop.wait("tensor", outs[g // 2].ready)
                tr = loop.do("tensor", lambda i, g=g, q=q, bank=bank, raw=outs[g // 2]: nc.tensor.transpose(
                    bank.ap[:, 0, g * P:(g + 1) * P],
                    raw.ap[:, (g % 2) * S + q * P:(g % 2) * S + (q + 1) * P], w.identf))
            loop.wait("vector", tr, w.recip.free)
            per_head = bank.ap[:, 0, :].rearrange("p (h c) -> p h c", c=32)
            rc = loop.do("vector", lambda i, per_head=per_head: nc.vector.reciprocal(
                w.recip.ap[:, :], per_head[:, :, HD]))
            loop.wait("vector", rc)
            mu = loop.do("vector", lambda i, per_head=per_head, q=q, normed=normed: nc.vector.tensor_tensor(
                normed.ap[:, q, :].rearrange("p (h c) -> p h c", c=HD), per_head[:, :, 0:HD],
                w.recip.ap[:, :].rearrange("p (h o) -> p h o", o=1).broadcast_to([P, H, HD]), ALU.mult))
            w.recip.free = (mu,)
            bank.free = (mu,)
        for raw in outs:
            raw.free = (tr,)
        bank = w.pj.next()
        loop.wait("tensor", bank.free, mu)
        for q in range(QT):
            for k in range(KT):
                tr = loop.do("tensor", lambda i, q=q, k=k, bank=bank, normed=normed: nc.tensor.transpose(
                    bank.ap[:, 0, k * S + q * P:k * S + (q + 1) * P], normed.ap[:, q, k * P:(k + 1) * P], w.identf))
        normed.free = (tr,)
        loop.wait("scalar", tr)
        for k in range(KT):
            put = loop.do("scalar", lambda i, k=k, b=b, bank=bank: nc.scalar.activation(
                heads_t.ap[:, k, b * S:(b + 1) * S], bank.ap[:, 0, k * S:(k + 1) * S], ACT.Identity,
                bias=bv[:, k:k + 1]))
        bank.free = (put,)
    heads_t.written(put)
    qs.free = (kmajor_last,)
    ks.free = (kmajor_last,)
    values.free = pr.free


def project_out(w, weight, heads_t, residual, x):
    nc, loop = w.nc, w.loop
    kt = heads_t.ap.shape[1]
    put = None
    loop.wait("vector", residual.ready, x.free)
    for a in range(0, NT, 2):
        bank = w.pj.next()
        loop.wait("tensor", bank.free, heads_t.ready)
        for j in range(2):
            for k in range(kt):
                mm = loop.do("tensor", lambda i, a=a, j=j, k=k, bank=bank: nc.tensor.matmul(
                    bank.ap[:, 0, j * D:(j + 1) * D], heads_t.ap[:, k, (a + j) * P:(a + j + 1) * P],
                    weight[:, k, :], start=(k == 0), stop=(k == kt - 1)))
        loop.wait("vector", mm)
        put = loop.do("vector", lambda i, a=a, bank=bank: nc.vector.tensor_tensor(
            x.ap[:, a:a + 2, :], bank.ap[:, 0, :].rearrange("p (t n) -> p t n", t=2),
            residual.ap[:, a:a + 2, :], ALU.add))
        bank.free = (put,)
    heads_t.read(mm)
    residual.read(put)
    x.written(put)


def add_bias(w, x, row, out):
    nc, loop = w.nc, w.loop
    loop.wait("gpsimd", x.ready, out.free)
    put = loop.do("gpsimd", lambda i: nc.gpsimd.tensor_tensor(out.ap[:, :, :], x.ap[:, :, :], row, ALU.add))
    x.read(put)
    out.written(put)


def feed_forward(w, w1, b1, w2, xt, residual, x):
    nc, loop = w.nc, w.loop
    hid = w.hidden
    loop.wait("scalar", hid.free)
    for f in range(FT):
        bank = w.pj.next()
        loop.wait("tensor", bank.free, xt.ready)
        for k in range(KT):
            mm = loop.do("tensor", lambda i, f=f, k=k, bank=bank: nc.tensor.matmul(
                bank.ap[:, 0, :], w1[:, k, f * P:(f + 1) * P], xt.ap[:, k, :], start=(k == 0), stop=(k == KT - 1)))
        loop.wait("scalar", mm)
        put = loop.do("scalar", lambda i, f=f, bank=bank: nc.scalar.activation(
            hid.ap[:, f, :], bank.ap[:, 0, :], ACT.Relu, bias=b1[:, f:f + 1]))
        bank.free = (put,)
    xt.read(mm)
    hid.written(put)
    project_out(w, w2, hid, residual, x)


def route(w, rw, rb, iota, xt, combine):
    nc, loop = w.nc, w.loop
    r = w.route
    bank = w.pj.next()
    loop.wait("tensor", bank.free, xt.ready)
    for t in range(NT):
        for k in range(KT):
            mm = loop.do("tensor", lambda i, t=t, k=k: nc.tensor.matmul(
                bank.ap[:, 0, t * E:(t + 1) * E], xt.ap[:, k, t * P:(t + 1) * P], rw[:, k, :],
                start=(k == 0), stop=(k == KT - 1)))
    xt.read(mm)
    logit, prob = r["logit"], r["prob"]
    per_tile = lambda a: a.unsqueeze(2).broadcast_to([P, NT, E])

    def v(emit, *waits):
        loop.wait("vector", *waits)
        return loop.do("vector", emit)
    a = v(lambda i: nc.vector.tensor_tensor(
        logit, bank.ap[:, 0, 0:NT * E].rearrange("p (t e) -> p t e", e=E),
        rb.unsqueeze(1).broadcast_to([P, NT, E]), ALU.add), mm, combine.free)
    bank.free = (a,)
    a = v(lambda i: nc.vector.tensor_reduce(r["max"], logit, AX.X, ALU.max), a)
    a = v(lambda i: nc.vector.tensor_tensor(logit, logit, per_tile(r["max"]), ALU.subtract), a)
    loop.wait("scalar", a)
    e = loop.do("scalar", lambda i: nc.scalar.activation(prob, logit, ACT.Exp))
    a = v(lambda i: nc.vector.tensor_reduce(r["sum"], prob, AX.X, ALU.add), e)
    a = v(lambda i: nc.vector.reciprocal(r["rsum"], r["sum"]), a)
    a = v(lambda i: nc.vector.tensor_tensor(prob, prob, per_tile(r["rsum"]), ALU.mult), a)
    loop.wait("vector", a, alone=True)
    for t in range(NT):
        top = loop.do("vector", lambda i, t=t: nc.vector.max(r["top"][:, t, :], prob[:, t, :]))
    loop.wait("vector", top, alone=True)
    for t in range(NT):
        at = loop.do("vector", lambda i, t=t: nc.vector.max_index(r["at"][:, t, :], r["top"][:, t, :], prob[:, t, :]))
    d = v(lambda i: nc.vector.tensor_tensor(r["gap"], r["top"][:, :, 1], r["top"][:, :, 0], ALU.subtract))
    f = v(lambda i: nc.vector.tensor_copy(r["at_f"], r["at"]), at)
    loop.wait("scalar", d)
    e = loop.do("scalar", lambda i: nc.scalar.activation(r["e2"], r["gap"], ACT.Exp))
    a = v(lambda i: nc.vector.tensor_scalar(r["one_e2"], r["e2"], 1.0, None, ALU.add), e)
    a = v(lambda i: nc.vector.reciprocal(r["w"][:, 0, :], r["one_e2"]), a)
    a = v(lambda i: nc.vector.tensor_tensor(r["w"][:, 1, :], r["e2"], r["w"][:, 0, :], ALU.mult), a)
    loop.wait("vector", a, f)
    for t in range(NT):
        loop.do("vector", lambda i, t=t: nc.vector.tensor_scalar(
            r["second"][:, t, :], iota, r["at_f"][:, t, 1:2], r["w"][:, 1, t:t + 1], ALU.is_equal, ALU.mult))
        a = loop.do("vector", lambda i, t=t: nc.vector.tensor_scalar(
            combine.ap[:, t, :], iota, r["at_f"][:, t, 0:1], r["w"][:, 0, t:t + 1], ALU.is_equal, ALU.mult))
    a = v(lambda i: nc.vector.tensor_tensor(combine.ap[:, :, :], combine.ap[:, :, :], r["second"], ALU.add), a)
    combine.written(a)


class Constants:

    def __init__(self, nc, ctx, name):
        self.nc, self.ctx, self.name, self.loads, self.fills = nc, ctx, name, [], []

    def sb(self, name, shape, dt=F32):
        return whole(self.ctx.enter_context(self.nc.sbuf_tensor(f"{self.name}_{name}", shape, dt)))

    def weight(self, name, src):
        rows, cols = src.shape
        t = self.sb(name, [P, rows // P, cols])
        self.loads.append((t[:, :, :], src.rearrange("(k p) n -> p k n", p=P)))
        return t

    def load(self, name, shape, src, dt=F32):
        t = self.sb(name, shape, dt)
        self.loads.append((t[tuple(slice(None) for _ in shape)], src))
        return t

    def fill(self, ap, value):
        self.fills.append((ap, value))

    def emit(self):
        nc = self.nc
        with nc.semaphore(f"{self.name}_loaded") as loaded, nc.semaphore(f"{self.name}_filled") as filled, \
                nc.Block() as block:
            @block.sync
            def _(eng):
                for dst, src in self.loads:
                    eng.dma_start(dst, src).then_inc(loaded, 16)
                eng.wait_ge(loaded, 16 * len(self.loads))

            @block.gpsimd
            def _(eng):
                for k, (ap, value) in enumerate(self.fills):
                    eng.memset(ap, value).then_inc(filled, 1)
                    eng.wait_ge(filled, k + 1)
                eng.wait_ge(filled, len(self.fills))


def attention_buffers(w, dram, q_order_name="q"):
    w.tok = w.ring("tok", 5, [P, NT, D])
    w.xt = w.ring("xt", 2, [P, KT, T])
    w.parts_q = w.buffer("parts_q", [P, NPART, KT, T], BF16)
    w.parts_k = w.buffer("parts_k", [P, NPART, KT, T], BF16)
    w.rest = w.ring("rest", 1, [P, KT, T])
    w.qs = w.buffer("qs", [STACK + NPART, H, T], BF16)
    w.ks = w.buffer("ks", [STACK + NPART, H, T], BF16)
    w.values = w.buffer("values", [P, NT, H, 32])
    w.maxima = w.buffer("maxima", [P, NB * QT, H])
    w.shift = w.ring("shift", 1, [H, NPART, S], BF16)
    w.shift_rest = w.ring("shift_rest", 1, [H, S])
    w.prob = w.ring("prob", 2, [P, 4, 2 * S])
    w.raw = w.ring("raw", 2, [P, 2 * S])
    w.normed = w.ring("normed", 2, [P, QT, D])
    w.recip = w.buffer("recip", [P, H])
    w.heads_t = w.buffer("heads_t", [P, KT, T])
    w.ctx_t = w.buffer("ctx_t", [P, KT, NB * C])
    w.ln_stats = w.buffer("ln_stats", [P, NT, 6])
    w.ln_moments = w.buffer("ln_moments", [P, NT, 2])
    w.ln_rstd = w.buffer("ln_rstd", [P, 2, NT])
    w.q_dram, w.k_dram, w.shift_dram = Buffer(dram["q"]), Buffer(dram["k"]), Buffer(dram["shift"])
    w.all += [w.q_dram, w.k_dram, w.shift_dram]
    w.sc = w.psum("scores", [2, 2])
    w.pj = w.psum("project", [1, 1])
    w.pv = w.psum("pv", [1, 1])


def self_attention(w, wt, xt, mask, causal, heads_t):
    q_bias, k_bias, v_bias = wt["biases"]
    project_parts(w, wt["q"], q_bias, xt, T, w.parts_q)
    stack_parts(w, w.parts_q, w.q_dram, w.qs, T, Q_ORDER, "q")
    project_parts(w, wt["k"], k_bias, xt, T, w.parts_k)
    stack_parts(w, w.parts_k, w.k_dram, w.ks, T, K_ORDER, "k")
    project_values(w, wt["v"], xt, [(t * P, P) for t in range(NT)], w.values)
    attend(w, w.qs, w.ks, w.values, lambda b: (b * S, S), QT, causal, mask, heads_t, v_bias)


def cross_attention(w, wt, xt, heads_t):
    q_bias, k_bias, v_bias = wt["biases"]
    project_parts(w, wt["k"], k_bias, w.ctx_t, NB * C, w.parts_k)
    stack_parts(w, w.parts_k, w.k_dram, w.ks, NB * C, K_ORDER, "k")
    project_parts(w, wt["q"], q_bias, xt, T, w.parts_q)
    stack_parts(w, w.parts_q, w.q_dram, w.qs, T, Q_ORDER, "q")
    project_values(w, wt["v"], w.ctx_t, [(b * C, C) for b in range(NB)], w.values)
    attend(w, w.qs, w.ks, w.values, lambda b: (b * C, C), 1, False, None, heads_t, v_bias)


def to_features(w, x, scale=None, bias=None):
    xt = w.xt.next()
    xt.written(*[transpose_tokens(w, x, xt, b, scale, bias) for b in range(NB)])
    return xt


def attention_layer(w, wt, kind, x_for_qkv_t, x, mask=None, causal=False):
    residual = w.tok.next()
    if wt["out_bias"] is not None:
        add_bias(w, x, wt["out_bias"], residual)
    else:
        residual = x
    if kind == "self":
        self_attention(w, wt, x_for_qkv_t, mask, causal, w.heads_t)
    else:
        cross_attention(w, wt, x_for_qkv_t, w.heads_t)
    out = w.tok.next()
    project_out(w, wt["o"], w.heads_t, residual, out)
    return out


def post_norm(w, x, gain, shift):
    out = w.tok.next()
    normalise(w, x, out)
    gain_and_shift(w, out, gain, shift)
    return out


def load_tokens(w, src, name):
    nc, loop = w.nc, w.loop
    buf = w.loaded
    loop.wait("gpsimd", buf.free)
    buf.written(loop.dma("gpsimd", name, lambda i: nc.gpsimd.dma_start(buf.ap[:, :, :], src(i))))
    return buf


def load_context(w, ctx_t):
    nc, loop = w.nc, w.loop
    loop.wait("gpsimd", w.ctx_t.free)
    w.ctx_t.written(loop.dma("gpsimd", "ctx", lambda i: nc.gpsimd.dma_start(w.ctx_t.ap[:, :, :], ctx_t(i))))


def store(w, x, dst, name):
    nc, loop = w.nc, w.loop
    loop.wait("sync", x.ready)
    x.read(loop.dma("sync", name, lambda i: nc.sync.dma_start(dst(i), x.ap)))


def pairs(ap):
    v = ap.rearrange("(i b) (q p) d -> i p (b q) d", b=NB, p=P)
    return lambda i: v[i]


def by_feature(c, name, packed, at, n):
    return packed[:, at:at + n]


def build(nc, a, out):
    def scratch(name, shape, dt=F32):
        return nc.dram_tensor(name, shape, dt, kind="Internal").ap()

    x1, x2 = scratch("x_moe_in", [B, S, D]), scratch("x_moe_out", [B, S, D])
    combine_dram = scratch("combine", [TRIPS, P, NT, E])
    dram = {"q": scratch("q_parts", [NPART, D, T], BF16), "k": scratch("k_parts", [NPART, D, T], BF16),
            "shift": scratch("shift_parts", [NB, NPART, H, S], BF16)}
    ctx_v = a["ctx_t"].rearrange("(k p) (i t) -> i p k t", p=P, t=NB * C)
    ctx_t = lambda i: ctx_v[i]
    cols, rows = a["columns"], a["rows"]

    def common(c):
        packed = c.load("columns", [P, len(COLUMNS)], cols)
        column = lambda name: packed[:, COLUMNS.index((name, 0)):COLUMNS.index((name, 0)) + sum(n == name for n, _ in COLUMNS)]
        identf = c.load("identity", [P, P], a["identity"])
        return column, identf

    def row(c, name):
        r = c.load("row_" + name, [P, D], rows[ROWS.index(name)].partition_broadcast(P))
        return r[:, :].unsqueeze(1).broadcast_to([P, NT, D])

    def attention_weights(c, column, layer, at, names, bias_names, out_bias):
        wt = {k: c.weight(f"{layer}_{at}_{k}", a[n]) for k, n in zip("qkvo", names)}
        wt["biases"] = [column(n) for n in bias_names]
        wt["out_bias"] = row(c, out_bias) if out_bias else None
        return wt

    def attention_constants(w, c):
        w.minus_half = c.sb("minus_half", [P, NT])[:, :]
        c.fill(w.minus_half, -0.5)
        attention_buffers(w, dram)
        c.fill(w.values.ap[:, :, :, HD:HD + 1], 1.0)
        c.fill(w.values.ap[:, :, :, HD + 1:32], 0.0)
        c.fill(w.ks.ap[STACK:STACK + NPART, :, :], 1.0)
        w.identb = c.sb("identb", [P, P], BF16)[:, :]

    with ExitStack() as ctx:
        c = Constants(nc, ctx, "a_const")
        column, identf = common(c)
        loop = Loop(nc, ctx, "a", TRIPS)
        w = Work(nc, ctx, "a", loop)
        w.identf = identf[:, :]
        attention_constants(w, c)
        L0s = attention_weights(c, column, "l0", "self", ["L0_xattn_mq_w", "L0_xattn_mk_w", "L0_xattn_mv_w", "L0_xattn_m_proj_w"],
                                ["L0_xattn_mq_b", "L0_xattn_mk_b", "L0_xattn_mv_b"], "L0_xattn_m_proj_b")
        L0c = attention_weights(c, column, "l0", "cross", ["L0_xattn_cq_w", "L0_xattn_ck_w", "L0_xattn_cv_w", "L0_xattn_c_proj_w"],
                                ["L0_xattn_cq_b", "L0_xattn_ck_b", "L0_xattn_cv_b"], "L0_xattn_c_proj_b")
        f1, f2 = c.weight("f1", a["L0_xattn_f_w1"]), c.weight("f2", a["L0_xattn_f_w2"])
        f_b2 = row(c, "L0_xattn_f_b2")
        n1 = lambda q: f"L1_xattn_{q}"
        L1 = {at: attention_weights(c, column, "l1", at, [n1(f"{at}_w{k}") for k in "qkvo"],
                                    [n1(f"{at}_b{k}") for k in "qkv"], n1(f"{at}_bo")) for at in ("sa", "ca")}
        ln = {k: row(c, n1(k)) for k in ("ln1_g", "ln1_b", "ln2_g", "ln2_b")}
        rw = c.weight("router", a["L1_xattn_router_w"])
        rb = c.load("router_b", [P, E], a["L1_xattn_router_b"].partition_broadcast(P))
        iota = c.load("iota", [P, E], a["iota"].partition_broadcast(P))
        causal_f = c.load("causal", [P, 2, P], a["causal"])
        mask_b = c.sb("mask_b", [P, 2, P], BF16)
        w.hidden = w.buffer("hidden", [P, FT, T])
        w.loaded = w.buffer("loaded", [P, NT, D])
        w.combine = w.buffer("combine", [P, NT, E])
        w.route = {n: w.sb("route_" + n, s, d)[tuple(slice(None) for _ in s)] for n, s, d in [
            ("logit", [P, NT, E], F32), ("prob", [P, NT, E], F32), ("max", [P, NT], F32), ("sum", [P, NT], F32),
            ("rsum", [P, NT], F32), ("top", [P, NT, E], F32), ("at", [P, NT, E], U32), ("at_f", [P, NT, E], F32),
            ("gap", [P, NT], F32), ("e2", [P, NT], F32), ("one_e2", [P, NT], F32), ("w", [P, 2, NT], F32),
            ("second", [P, NT, E], F32)]}
        c.emit()
        with nc.Block() as block:
            @block.vector
            def _(eng):
                eng.tensor_copy(w.identb, w.identf)
                eng.tensor_copy(mask_b[:, :, :], causal_f[:, :, :])
        mask_q = [mask_b[:, 0:1, :]]
        mask = (Diagonal(mask_b[:, 0, :]), Diagonal(mask_b[:, 1, :]))

        x = load_tokens(w, pairs(a["x"]), "x")
        load_context(w, ctx_t)
        xn = w.tok.next()
        normalise(w, x, xn)
        xt = to_features(w, xn, column("L0_xattn_ln1_g"), column("L0_xattn_ln1_b"))
        x = attention_layer(w, L0s, "self", xt, x, mask, True)
        xn = w.tok.next()
        normalise(w, x, xn)
        xt = to_features(w, xn, column("L0_xattn_ln2_g"), column("L0_xattn_ln2_b"))
        x = attention_layer(w, L0c, "cross", xt, x)
        xn = w.tok.next()
        normalise(w, x, xn)
        xt = to_features(w, xn, column("L0_xattn_ln3_g"), column("L0_xattn_ln3_b"))
        residual = w.tok.next()
        add_bias(w, x, f_b2, residual)
        x = w.tok.next()
        feed_forward(w, f1, column("L0_xattn_f_b1"), f2, xt, residual, x)

        xt = to_features(w, x)
        x = attention_layer(w, L1["sa"], "self", xt, x, mask, True)
        x = post_norm(w, x, ln["ln1_g"], ln["ln1_b"])
        xt = to_features(w, x)
        x = attention_layer(w, L1["ca"], "cross", xt, x)
        x = post_norm(w, x, ln["ln2_g"], ln["ln2_b"])
        store(w, x, pairs(x1), "x1")
        xt = to_features(w, x)
        route(w, rw, rb[:, :], iota[:, :], xt, w.combine)
        store(w, w.combine, lambda i: combine_dram[i], "combine")
        w.close()
        with nc.Block() as block:
            loop.emit(block)

    with ExitStack() as ctx:
        c = Constants(nc, ctx, "b_const")
        column, identf = common(c)
        loop = Loop(nc, ctx, "b", TRIPS)
        w = Work(nc, ctx, "b", loop)
        w.identf = identf[:, :]
        w.minus_half = c.sb("minus_half", [P, NT])[:, :]
        c.fill(w.minus_half, -0.5)
        w1 = [c.weight(f"w1_{e}", a["L1_xattn_e_w1"][e]) for e in range(E)]
        w2 = [c.weight(f"w2_{e}", a["L1_xattn_e_w2"][e]) for e in range(E)]
        b2 = c.load("b2", [E, D], a["L1_xattn_e_b2"])
        b1 = column("L1_xattn_e_b1")
        g3, s3 = row(c, n1("ln3_g")), row(c, n1("ln3_b"))
        w.tok = w.ring("tok", 2, [P, NT, D])
        w.loaded = w.buffer("loaded", [P, NT, D])
        w.combine = w.buffer("combine", [P, NT, E])
        combine_t = w.buffer("combine_t", [E, T])
        w.xt = w.ring("xt", 1, [P, KT, T])
        hidden = w.ring("hidden", 1, [P, FT, T])
        w.ln_stats = w.buffer("ln_stats", [P, NT, 6])
        w.ln_moments = w.buffer("ln_moments", [P, NT, 2])
        w.ln_rstd = w.buffer("ln_rstd", [P, 2, NT])
        w.pj = w.psum("project", [1] * 8)
        c.emit()

        x = load_tokens(w, pairs(x1), "x")
        loop.wait("gpsimd", w.combine.free)
        w.combine.written(loop.dma("gpsimd", "combine", lambda i: nc.gpsimd.dma_start(
            w.combine.ap[:, :, :], combine_dram[i])))
        xt = to_features(w, x)
        bank = w.pj.next()
        loop.wait("tensor", bank.free, w.combine.ready)
        for t in range(NT):
            tr = loop.do("tensor", lambda i, t=t, bank=bank: nc.tensor.transpose(
                bank.ap[0:E, 0, t * P:(t + 1) * P], w.combine.ap[:, t, :], w.identf))
        loop.wait("vector", tr, combine_t.free)
        put = loop.do("vector", lambda i, bank=bank: nc.vector.tensor_copy(combine_t.ap[:, :], bank.ap[0:E, 0, :]))
        bank.free = (put,)
        combine_t.written(put)
        acc = w.tok.next()
        loop.wait("vector", x.ready, acc.free)
        for t0 in range(0, NT, 2):
            bank = w.pj.next()
            loop.wait("tensor", bank.free, combine_t.ready)
            for j in range(2):
                mm = loop.do("tensor", lambda i, t0=t0, j=j, bank=bank: nc.tensor.matmul(
                    bank.ap[:, 0, j * D:(j + 1) * D], combine_t.ap[:, (t0 + j) * P:(t0 + j + 1) * P], b2[:, :],
                    start=True, stop=True))
            loop.wait("vector", mm)
            put = loop.do("vector", lambda i, t0=t0, bank=bank, x=x: nc.vector.tensor_tensor(
                acc.ap[:, t0:t0 + 2, :], bank.ap[:, 0, :].rearrange("p (t n) -> p t n", t=2),
                x.ap[:, t0:t0 + 2, :], ALU.add))
            bank.free = (put,)
        combine_t.read(mm)
        x.read(put)
        acc_ready = [put] * NT
        for e in range(E):
            hid = hidden.next()
            loop.wait("scalar", hid.free)
            for f in range(FT):
                bank = w.pj.next()
                loop.wait("tensor", bank.free, xt.ready)
                for k in range(KT):
                    mm = loop.do("tensor", lambda i, e=e, f=f, k=k, bank=bank: nc.tensor.matmul(
                        bank.ap[:, 0, :], w1[e][:, k, f * P:(f + 1) * P], xt.ap[:, k, :],
                        start=(k == 0), stop=(k == KT - 1)))
                loop.wait("scalar", mm)
                put = loop.do("scalar", lambda i, e=e, f=f, bank=bank, hid=hid: nc.scalar.activation(
                    hid.ap[:, f, :], bank.ap[:, 0, :], ACT.Gelu, bias=b1[:, e * FT + f:e * FT + f + 1]))
                bank.free = (put,)
            xt.read(mm)
            hid.written(put)
            for t0 in range(0, NT, 2):
                bank = w.pj.next()
                loop.wait("tensor", bank.free, hid.ready)
                for j in range(2):
                    for f in range(FT):
                        mm = loop.do("tensor", lambda i, e=e, t0=t0, j=j, f=f, bank=bank, hid=hid: nc.tensor.matmul(
                            bank.ap[:, 0, j * D:(j + 1) * D], hid.ap[:, f, (t0 + j) * P:(t0 + j + 1) * P],
                            w2[e][:, f, :], start=(f == 0), stop=(f == FT - 1)))
                loop.wait("vector", mm, w.combine.ready)
                for j in range(2):
                    t = t0 + j
                    loop.wait("vector", acc_ready[t])
                    acc_ready[t] = loop.do("vector", lambda i, e=e, j=j, t=t, bank=bank: nc.vector.scalar_tensor_tensor(
                        acc.ap[:, t, :], bank.ap[:, 0, j * D:(j + 1) * D], w.combine.ap[:, t, e:e + 1],
                        acc.ap[:, t, :], ALU.mult, ALU.add))
                bank.free = (acc_ready[t],)
            hid.read(mm)
        acc.written(*acc_ready)
        w.combine.read(tr, acc_ready[NT - 1])
        x = post_norm(w, acc, g3, s3)
        store(w, x, pairs(x2), "x2")
        w.close()
        with nc.Block() as block:
            loop.emit(block)

    with ExitStack() as ctx:
        c = Constants(nc, ctx, "c_const")
        column, identf = common(c)
        loop = Loop(nc, ctx, "c", TRIPS)
        w = Work(nc, ctx, "c", loop)
        w.identf = identf[:, :]
        attention_constants(w, c)
        n2 = lambda q: f"L2_xattn_{q}"
        L2 = {at: attention_weights(c, column, "l2", at, [n2(f"{at}_w{k}") for k in "qkvo"],
                                    [n2(f"{at}_b{k}") for k in "qkv"], n2(f"{at}_bo")) for at in ("sa", "ca")}
        f1, f2 = c.weight("f1", a[n2("ff_w1")]), c.weight("f2", a[n2("ff_w2")])
        f_b2 = row(c, n2("ff_b2"))
        ln = {k: row(c, n2(k)) for k in ("ln1_g", "ln1_b", "ln2_g", "ln2_b", "ln3_g", "ln3_b")}
        L3 = attention_weights(c, column, "l3", "cross", [f"L3_xattn_W{k}" for k in "qkvo"],
                               [f"L3_xattn_b{k}" for k in "qkv"], None)
        g, s = row(c, "L3_xattn_ln_gamma"), row(c, "L3_xattn_ln_beta")
        mask_i = c.load("mask_i", [P, QT, S], a["mask"].rearrange("(q p) k -> p q k", p=P), I32)
        mask_f = c.sb("mask_f", [P, QT, S])
        mask_q = c.sb("mask_q", [P, QT, S], BF16)
        mask_k = c.sb("mask_k", [P, QT, S], BF16)
        w.hidden = w.buffer("hidden", [P, FT, T])
        w.loaded = w.buffer("loaded", [P, NT, D])
        c.emit()
        with nc.semaphore("mask_f_done") as mask_f_done, nc.semaphore("mask_turned") as mask_turned, nc.Block() as block:
            mask_bank = w.pj.buffers[0].ap

            @block.vector
            def _(eng):
                eng.tensor_copy(w.identb, w.identf)
                eng.tensor_scalar(mask_f[:, :, :], mask_i[:, :, :], 0.0, NEG, ALU.is_equal, ALU.mult).then_inc(mask_f_done, 1)
                eng.wait_ge(mask_f_done, 1)
                eng.tensor_copy(mask_q[:, :, :], mask_f[:, :, :])
                eng.wait_ge(mask_turned, 1)
                eng.tensor_copy(mask_k[:, :, :], mask_bank[:, 0, :].rearrange("p (k q) -> p k q", k=QT))

            @block.tensor
            def _(eng):
                eng.wait_ge(mask_f_done, 1)
                for k in range(QT):
                    for q in range(QT):
                        ins = eng.transpose(mask_bank[:, 0, k * S + q * P:k * S + (q + 1) * P],
                                            mask_f[:, q, k * P:(k + 1) * P], w.identf)
                ins.then_inc(mask_turned, 1)

        x = load_tokens(w, pairs(x2), "x")
        load_context(w, ctx_t)
        xt = to_features(w, x)
        x = attention_layer(w, L2["sa"], "self", xt, x, (mask_q, mask_k), False)
        x = post_norm(w, x, ln["ln1_g"], ln["ln1_b"])
        xt = to_features(w, x)
        x = attention_layer(w, L2["ca"], "cross", xt, x)
        x = post_norm(w, x, ln["ln2_g"], ln["ln2_b"])
        xt = to_features(w, x)
        residual = w.tok.next()
        add_bias(w, x, f_b2, residual)
        x = w.tok.next()
        feed_forward(w, f1, column(n2("ff_b1")), f2, xt, residual, x)
        x = post_norm(w, x, ln["ln3_g"], ln["ln3_b"])
        xt = to_features(w, x)
        x = attention_layer(w, L3, "cross", xt, x)
        x = post_norm(w, x, g, s)
        store(w, x, pairs(out), "out")
        w.close()
        with nc.Block() as block:
            loop.emit(block)


class Diagonal:

    def __init__(self, tile):
        self.tile = tile

    def __getitem__(self, _):
        return self.tile


_VECTORS = (["L0_xattn_ln1_g", "L0_xattn_ln1_b", "L0_xattn_ln2_g", "L0_xattn_ln2_b", "L0_xattn_ln3_g",
             "L0_xattn_ln3_b", "L0_xattn_mq_b", "L0_xattn_mk_b", "L0_xattn_mv_b", "L0_xattn_cq_b",
             "L0_xattn_ck_b", "L0_xattn_cv_b", "L0_xattn_f_b1", "L1_xattn_e_b1", "L2_xattn_ff_b1"]
            + [f"{l}_xattn_{at}_b{k}" for l in ("L1", "L2") for at in ("sa", "ca") for k in "qkv"]
            + [f"L3_xattn_b{k}" for k in "qkv"])
_SIZES = {"L0_xattn_f_b1": FF, "L1_xattn_e_b1": E * FF, "L2_xattn_ff_b1": FF}
COLUMNS = [(n, k) for n in _VECTORS for k in range(_SIZES.get(n, D) // P)]
ROWS = (["L0_xattn_m_proj_b", "L0_xattn_c_proj_b", "L0_xattn_f_b2", "L2_xattn_ff_b2",
         "L3_xattn_ln_gamma", "L3_xattn_ln_beta"]
        + [f"{l}_xattn_{at}_bo" for l in ("L1", "L2") for at in ("sa", "ca")]
        + [f"{l}_xattn_ln{k}_{j}" for l in ("L1", "L2") for k in (1, 2, 3) for j in "gb"])


def kernel(**inputs):
    import concourse.bacc as bacc
    from concourse.bass_utils import run_bass_kernel_spmd

    v = {k: np.asarray(x) for k, x in inputs.items()}
    arrays = {"x": v["x"], "mask": v["mask_1x1xSxS_ik0"].reshape(S, S),
              "ctx_t": v["ctx_1024"].reshape(B * C, D).T,
              "columns": np.concatenate([v[n].reshape(-1, P) for n in _VECTORS]).T,
              "rows": np.stack([v[n] for n in ROWS]),
              "identity": np.eye(P, dtype=np.float32),
              "iota": np.arange(E, dtype=np.float32)}
    k, q = np.meshgrid(np.arange(P), np.arange(P))
    future = np.where(k > q, np.float32(NEG), np.float32(0))
    arrays["causal"] = np.stack([future, future.T], axis=1)
    for n in ("mq", "mk", "mv", "cq", "ck", "cv"):
        arrays[f"L0_xattn_{n}_w"] = v[f"L0_xattn_{n}_w"].transpose(1, 0, 2).reshape(D, D)
    for n in ("L0_xattn_m_proj_w", "L0_xattn_c_proj_w", "L0_xattn_f_w1", "L0_xattn_f_w2", "L1_xattn_router_w",
              "L1_xattn_router_b", "L1_xattn_e_w1", "L1_xattn_e_w2", "L1_xattn_e_b2"):
        arrays[n] = v[n]
    for at in ("sa", "ca"):
        for m in "qkvo":
            arrays[f"L1_xattn_{at}_w{m}"] = v[f"L1_xattn_{at}_w{m}"]
            arrays[f"L2_xattn_{at}_w{m}"] = v[f"L2_xattn_{at}_w{m}"].T
    for m in (1, 2):
        arrays[f"L2_xattn_ff_w{m}"] = v[f"L2_xattn_ff_w{m}"].T
    for m in "qkvo":
        arrays[f"L3_xattn_W{m}"] = v[f"L3_xattn_W{m}"]
    arrays = {n: np.ascontiguousarray(x) for n, x in arrays.items()}

    nc = bacc.Bacc("TRN2", target_bir_lowering=False, num_devices=1)
    ins = {n: nc.dram_tensor(f"in_{n}", x.shape, mybir.dt.from_np(x.dtype), kind="ExternalInput").ap()
           for n, x in arrays.items()}
    out = nc.dram_tensor("out", (B, S, D), F32, kind="ExternalOutput").ap()
    build(nc, ins, out)
    r = run_bass_kernel_spmd(nc, [{f"in_{n}": x for n, x in arrays.items()}], core_ids=[0])
    return r.results[0]["out"]
```

```python
from contextlib import ExitStack

import numpy as np
import concourse.bass as bass
import concourse.mybir as mybir

F32, BF16 = mybir.dt.float32, mybir.dt.bfloat16
I32, U32 = mybir.dt.int32, mybir.dt.uint32
ALU = mybir.AluOpType
ACT = mybir.ActivationFunctionType
AX = mybir.AxisListType

P = 128
B, S, D = 16, 256, 256
H, HD = 16, 16
C = 77
FF, E = 1024, 8
LANES = 2
NB = 2 * LANES
TRIPS = B // NB
KT = D // P
FT = FF // P
QT = S // P
NPART = 3
STACK = 6 * HD
EPS = 1e-5
GROUP = S
UNROLL = 2
GROUPS = -(-(2 * B * S // GROUP + E) // UNROLL) * UNROLL
Y = [1.8, 2.0, 10, 14, 1.3, .8, 7, 1.3, 1.2, .8, 5, 2]
LEAD = 12.0
NEG = -float(2 ** 100)
SCALE = HD ** -0.5


class Token:

    def __init__(self, line, k, back=0):
        self.line, self.k, self.back = line, k, back

    @property
    def prev(self):
        return Token(self.line, self.k, 1)


class Late:

    def __init__(self):
        self.tokens = ()


class Line:

    def __init__(self, sem, step, ahead):
        self.sem, self.step, self.ahead, self.n = sem, step, ahead, 0

    def count(self):
        self.n += 1
        return Token(self, self.n)


class Loop:

    ENGINES = ("sync", "tensor", "scalar", "vector", "gpsimd")

    def __init__(self, nc, ctx, name, trips):
        self.nc, self.ctx, self.name, self.trips = nc, ctx, name, trips
        self.queue = {e: [] for e in self.ENGINES}
        self.before = []
        self.lines = {}
        self.owner = {}
        self.carrier = {e: ctx.enter_context(nc.semaphore(f"{name}_{e}_waits")) for e in self.ENGINES}

    def line(self, name, owner, step):
        if name not in self.lines:
            sem = self.ctx.enter_context(self.nc.semaphore(f"{self.name}_{name}"))
            self.lines[name] = Line(sem, step, not (owner == "gpsimd" and step == 16))
            self.owner[name] = owner
        return self.lines[name]

    def do(self, engine, emit):
        line = self.line(f"{engine}_done", engine, 1)
        self.queue[engine].append(("do", emit, line))
        return line.count()

    def quiet(self, engine, emit):
        self.queue[engine].append(("do", emit, None))

    def dma(self, engine, stream, emit):
        line = self.line(f"dma_{stream}", engine, 16)
        self.queue[engine].append(("do", emit, line))
        return line.count()

    def dma_ahead(self, stream, emit):
        name = f"dma_{stream}"
        if name not in self.lines:
            self.line(name, "gpsimd", 16).ahead = True
        line = self.lines[name]
        self.queue["gpsimd"].append(("next", emit, line))
        self.before.append(("next", emit, line))
        return line.count()

    def wait_ahead(self, token):
        self.queue["gpsimd"].append(("wait", (token,), True))
        self.before.append(("wait", token, None))

    def wait(self, engine, *tokens, alone=None):
        self.queue[engine].append(("wait", tokens, engine in ("sync", "gpsimd") if alone is None else alone))

    def emit(self, block):
        for engine in self.ENGINES:
            getter = {"sync": block.sync, "tensor": block.tensor, "scalar": block.scalar,
                      "vector": block.vector, "gpsimd": block.gpsimd}[engine]
            getter(lambda eng, engine=engine: self.run(engine, eng))

    def run(self, engine, eng):
        for name, line in self.lines.items():
            if self.owner[name] == engine and line.ahead and (engine != "gpsimd" or line.step == 1):
                eng.sem_inc(line.sem, line.n * line.step)
        if engine == "gpsimd":
            for kind, what, line in self.before:
                if kind == "next":
                    what(0).then_inc(line.sem, line.step)
                else:
                    eng.wait_ge(what.line.sem, what.k * what.line.step)
                    eng.sem_inc(self.carrier[engine], 1)
        with eng.Fori(0, self.trips) as i:
            seen = {}
            if engine == "gpsimd" and self.before:
                following = eng.value_load(self.next_trip[0:1, bass.ds(i, 1)], min_val=0, max_val=self.trips - 1)
            for kind, what, line in self.queue[engine]:
                if kind != "wait":
                    ins = what(following if kind == "next" else i)
                    if line is not None:
                        ins.then_inc(line.sem, line.step)
                    continue
                for t in flat(what):
                    assert t.line.ahead or not t.back
                    level = t.k + (t.line.n if t.line.ahead and not t.back else 0)
                    if seen.get(id(t.line), -1) >= level:
                        continue
                    seen[id(t.line)] = level
                    eng.wait_ge(t.line.sem, i * (t.line.n * t.line.step) + level * t.line.step)
                    if line:
                        eng.sem_inc(self.carrier[engine], 1)
        for name, line in self.lines.items():
            if self.owner[name] == engine and name.startswith("dma_"):
                eng.wait_ge(line.sem, (self.trips + line.ahead) * line.n * line.step)


def flat(tokens):
    for t in tokens:
        if isinstance(t, Token):
            yield t
        elif isinstance(t, Late):
            yield from (x.prev for x in flat(t.tokens))
        else:
            yield from flat(t)


class Buffer:

    def __init__(self, ap):
        self.ap, self.ready, self.carried = ap, (), Late()
        self.free = (self.carried,)

    def written(self, *tokens):
        self.ready, self.free = tokens, ()

    def read(self, *tokens):
        self.free += tokens

    def close(self):
        self.carried.tokens = () if self.free == (self.carried,) else self.free


class View:

    def __init__(self, base, ap):
        self.base, self.ap = base, ap

    @property
    def free(self):
        return self.base.free

    @property
    def ready(self):
        return self.base.ready

    def written(self, *tokens):
        self.base.written(*tokens)

    def read(self, *tokens):
        self.base.read(*tokens)


class Ring:

    def __init__(self, aps):
        self.buffers, self.at = [Buffer(ap) for ap in aps], 0

    def next(self):
        self.at += 1
        return self.buffers[(self.at - 1) % len(self.buffers)]


def whole(handle):
    return handle[tuple(slice(None) for _ in handle.shape)]


class Work:

    def __init__(self, nc, ctx, name, loop, tiles, psum_of=None):
        self.nc, self.ctx, self.name, self.loop = nc, ctx, name, loop
        self.nt, self.t = tiles, tiles * P
        self.all = []
        if psum_of is not None:
            self.sc, self.pj = psum_of.sc, psum_of.pj
            self.pv = self.psum("pv", [1])

    def sb(self, name, shape, dt=F32):
        return whole(self.ctx.enter_context(self.nc.sbuf_tensor(f"{self.name}_{name}", shape, dt)))

    def buffer(self, name, shape, dt=F32):
        b = Buffer(self.sb(name, shape, dt))
        self.all.append(b)
        return b

    def ring(self, name, n, shape, dt=F32):
        r = Ring([self.sb(f"{name}{k}", shape, dt) for k in range(n)])
        self.all += r.buffers
        return r

    def psum(self, name, banks, width=512):
        r = Ring([whole(self.ctx.enter_context(self.nc.psum_tensor(f"{self.name}_{name}{k}", [P, b, width], F32)))
                  for k, b in enumerate(banks)])
        self.all += r.buffers
        return r

    def close(self):
        for b in self.all:
            b.close()


def take_turns(first, second, lead):
    clocks = [[0.0, 0, first], [lead, 1, second]]
    while clocks:
        clocks.sort(key=lambda c: c[:2])
        try:
            clocks[0][0] += next(clocks[0][2])
        except StopIteration:
            clocks.pop(0)


def lane(steps, w, first):
    for b in range(first, NB, LANES):
        yield from steps(w, b)


def to_features(w, x, scale=None, bias=None):
    nc, loop = w.nc, w.loop
    dst = w.xt.next()
    loop.wait("scalar", dst.free)
    puts = []
    for b in range(w.nt // QT):
        bank = w.pj.next()
        loop.wait("tensor", bank.free, x.ready)
        for k in range(KT):
            for q in range(QT):
                turned = loop.do("tensor", lambda i, b=b, k=k, q=q, bank=bank: nc.tensor.transpose(
                    bank.ap[:, 0, k * S + q * P:k * S + (q + 1) * P], x.ap[:, QT * b + q, k * P:(k + 1) * P], w.identf))
        x.read(turned)
        loop.wait("scalar", turned)
        if scale is None:
            put = loop.do("scalar", lambda i, b=b, bank=bank: nc.scalar.activation(
                dst.ap[:, :, b * S:(b + 1) * S], bank.ap[:, 0, :].rearrange("p (k t) -> p k t", k=KT), ACT.Copy))
        else:
            for k in range(KT):
                put = loop.do("scalar", lambda i, b=b, k=k, bank=bank: nc.scalar.activation(
                    dst.ap[:, k, b * S:(b + 1) * S], bank.ap[:, 0, k * S:(k + 1) * S], ACT.Identity,
                    bias=bias[:, k:k + 1], scale=scale[:, k:k + 1]))
        bank.free = (put,)
        puts.append(put)
    dst.written(*puts)
    return dst


def normalise(w, x, out):
    nc, loop = w.nc, w.loop
    st, mv, rs = w.ln_stats, w.ln_moments, w.ln_rstd
    loop.wait("vector", x.ready, st.free)
    for t in range(w.nt):
        got = loop.do("vector", lambda i, t=t: nc.vector.bn_stats(st.ap[:, t, :], x.ap[:, t, :]))
    loop.wait("vector", got, mv.free, alone=True)
    for t in range(w.nt):
        got = loop.do("vector", lambda i, t=t: nc.vector.bn_aggr(mv.ap[:, t, :], st.ap[:, t, :]))
    st.free = (got,)
    loop.wait("gpsimd", got, rs.free)
    e = loop.do("gpsimd", lambda i: nc.gpsimd.tensor_scalar(rs.ap[:, 0, :], mv.ap[:, :, 1], EPS, None, ALU.add))
    loop.wait("gpsimd", e)
    r = loop.do("gpsimd", lambda i: nc.gpsimd.tensor_tensor(rs.ap[:, 1, :], rs.ap[:, 0, :], w.minus_half, ALU.pow))
    yield Y[10]
    loop.wait("vector", r, out.free)
    for t in range(w.nt):
        put = loop.do("vector", lambda i, t=t: nc.vector.tensor_scalar(
            out.ap[:, t, :], x.ap[:, t, :], mv.ap[:, t, 0:1], rs.ap[:, 1, t:t + 1], ALU.subtract, ALU.mult))
    x.read(put)
    mv.free = rs.free = (put,)
    out.written(put)
    yield Y[11]


def gain_and_shift(w, x, g, b):
    nc, loop = w.nc, w.loop
    over = lambda row: row.unsqueeze(1).broadcast_to([P, w.nt, D])
    loop.wait("gpsimd", x.ready, x.free)
    m = loop.do("gpsimd", lambda i: nc.gpsimd.tensor_tensor(x.ap, x.ap, over(g), ALU.mult))
    loop.wait("gpsimd", m)
    a = loop.do("gpsimd", lambda i: nc.gpsimd.tensor_tensor(x.ap, x.ap, over(b), ALU.add))
    x.written(a)


def project_parts(w, weight, bias, x, n, parts):
    nc, loop = w.nc, w.loop
    rest = w.rest
    loop.wait("scalar", parts.free)
    loop.wait("vector", rest.free)
    bank = w.pj.next()
    loop.wait("tensor", bank.free, x.ready)
    for m in range(KT):
        for k in range(KT):
            mm = loop.do("tensor", lambda i, k=k, m=m: nc.tensor.matmul(
                bank.ap[:, 0, m * n:(m + 1) * n], weight[:, k, m * P:(m + 1) * P], x.ap[:, k, 0:n],
                start=(k == 0), stop=(k == KT - 1)))
    x.read(mm)
    loop.wait("scalar", mm)
    for m in range(KT):
        p1 = loop.do("scalar", lambda i, m=m: nc.scalar.activation(
            parts.ap[:, 0, m, 0:n], bank.ap[:, 0, m * n:(m + 1) * n], ACT.Identity, bias=bias[:, m:m + 1]))
    loop.wait("vector", p1)
    for m in range(KT):
        r1 = loop.do("vector", lambda i, m=m: nc.vector.scalar_tensor_tensor(
            rest.ap[:, m, 0:n], bank.ap[:, 0, m * n:(m + 1) * n], bias[:, m:m + 1], parts.ap[:, 0, m, 0:n],
            ALU.add, ALU.subtract))
    bank.free = (r1,)
    loop.wait("scalar", r1)
    p2 = loop.do("scalar", lambda i: nc.scalar.activation(parts.ap[:, 1, :, 0:n], rest.ap[:, :, 0:n], ACT.Copy))
    loop.wait("vector", p2)
    p3 = loop.do("vector", lambda i: nc.vector.tensor_tensor(
        parts.ap[:, 2, :, 0:n], rest.ap[:, :, 0:n], parts.ap[:, 1, :, 0:n], ALU.subtract))
    rest.free = (p3,)
    parts.written(p3)


def send_parts(w, parts, scratch, n, name):
    nc, loop = w.nc, w.loop
    put_v = scratch.ap[:, 0:D * n].rearrange("s (m p t) -> m p s t", m=KT, p=P)
    loop.wait("sync", parts.ready, scratch.free)
    for m in range(KT):
        out = loop.dma("sync", f"{w.name}_{name}_out", lambda i, m=m: nc.sync.dma_start(
            put_v[m], parts.ap[:, :, m, 0:n]))
    parts.read(out)
    scratch.written(out)


def stack_parts(w, scratch, stacked, n, runs, name):
    nc, loop = w.nc, w.loop
    get_v = scratch.ap[:, 0:D * n].rearrange("s (d x) -> s d x", d=HD)
    loop.wait("sync", scratch.ready, stacked.free)
    for first, count, same in runs:
        rows = slice(first * HD, (first + count) * HD)
        if same is None:
            src = get_v[0:count]
        else:
            src = get_v[same:same + 1].broadcast_to([count, HD, H * n])
        back = loop.dma("sync", f"{w.name}_{name}_in", lambda i, rows=rows, src=src: nc.sync.dma_start(
            stacked.ap[rows].rearrange("r h t -> r (h t)"), src))
    scratch.free = (back,)
    stacked.written(back)


Q_RUNS = [(0, 3, 0), (3, 2, 1), (5, 1, 2)]
K_RUNS = [(0, 3, None), (3, 2, None), (5, 1, None)]


def project_values(w, weight, x, tiles, values):
    nc, loop = w.nc, w.loop
    bank = w.pj.next()
    loop.wait("tensor", bank.free, x.ready)
    for j, (at, keys) in enumerate(tiles):
        for k in range(KT):
            mm = loop.do("tensor", lambda i, j=j, at=at, keys=keys, k=k: nc.tensor.matmul(
                bank.ap[0:keys, 0, j * D:(j + 1) * D], x.ap[:, k, at:at + keys], weight[:, k, :],
                start=(k == 0), stop=(k == KT - 1)))
    x.read(mm)
    loop.wait("vector", values.free, mm)
    n, keys = len(tiles), tiles[0][1]
    put = loop.do("vector", lambda i: nc.vector.tensor_copy(
        values.ap[0:keys, 0:n, :, 0:HD],
        bank.ap[0:keys, 0, 0:n * D].rearrange("p (t h d) -> p t h d", h=H, d=HD)))
    bank.free = (put,)
    values.written(put)


def attend(w, qs, ks, values, n, causal, mask, heads_t, bv):
    nc, loop = w.nc, w.loop
    G = 2
    key_tiles = -(-n // P)
    maxima = w.maxima
    loop.wait("vector", maxima.free)

    def add_mask(ap, m):
        return loop.do("tensor", lambda i: nc.tensor.matmul(ap, w.identb, m, start=False, stop=True))

    def query_major(hp):
        bank = w.sc.next()
        loop.wait("tensor", bank.free, qs.ready, ks.ready)
        for j in range(G):
            h = G * hp + j
            off = 0
            for q in range(QT):
                m = P * (q + 1) if causal else n
                mm = loop.do("tensor", lambda i, j=j, h=h, q=q, m=m, off=off: nc.tensor.matmul(
                    bank.ap[:, j, off:off + m], qs.ap[0:STACK, h, q * P:(q + 1) * P],
                    ks.ap[0:STACK, h, 0:m], start=True, stop=(mask is None)))
                if mask is not None:
                    mo, mw = (off + q * P, P) if causal else (off, n)
                    mm = add_mask(bank.ap[:, j, mo:mo + mw], mask[0][:, q, :])
                off += m
        loop.wait("vector", mm)
        heads = slice(G * hp, G * (hp + 1))
        if causal:
            off = 0
            for q in range(QT):
                m = P * (q + 1)
                r = loop.do("vector", lambda i, q=q, m=m, off=off: nc.vector.tensor_reduce(
                    maxima.ap[:, q, heads], bank.ap[:, :, off:off + m], AX.X, ALU.max))
                off += m
        else:
            r = loop.do("vector", lambda i: nc.vector.tensor_reduce(
                maxima.ap[:, :, heads].rearrange("p q h -> p h q"),
                bank.ap[:, :, 0:QT * n].rearrange("p j (q n) -> p j q n", q=QT), AX.X, ALU.max))
        bank.free = (r,)
        return r

    def shift_rows(got_max):
        bank = w.pj.next()
        loop.wait("tensor", bank.free, got_max)
        for q in range(QT):
            tr = loop.do("tensor", lambda i, q=q: nc.tensor.transpose(
                bank.ap[0:H, 0, q * P:(q + 1) * P], maxima.ap[:, q, :], w.identf))
        maxima.free = (tr,)
        nm, rest = w.shift, w.rest.ap[0:H, 0, :]
        src = bank.ap[0:H, 0, 0:S]
        loop.wait("scalar", tr, nm.free)
        p1 = loop.do("scalar", lambda i: nc.scalar.mul(nm.ap[:, 0, :], src, -1.0))
        loop.wait("vector", p1, w.rest.free)
        r1 = loop.do("vector", lambda i: nc.vector.scalar_tensor_tensor(
            rest, src, -1.0, nm.ap[:, 0, :], ALU.mult, ALU.subtract))
        bank.free = (r1,)
        loop.wait("vector", r1)
        p2 = loop.do("vector", lambda i: nc.vector.tensor_copy(nm.ap[:, 1, :], rest))
        loop.wait("vector", p2)
        p3 = loop.do("vector", lambda i: nc.vector.tensor_tensor(nm.ap[:, 2, :], rest, nm.ap[:, 1, :], ALU.subtract))
        w.rest.free = (p3,)
        loop.wait("sync", p3, w.shift_dram.free)
        out = loop.dma("sync", f"{w.name}_shift_out", lambda i: nc.sync.dma_start(
            w.shift_dram.ap.rearrange("s h t -> h s t"), nm.ap))
        nm.free = (out,)
        loop.wait("sync", out)
        back = loop.dma("sync", f"{w.name}_shift_in", lambda i: nc.sync.dma_start(
            qs.ap[STACK:STACK + NPART, :, :], w.shift_dram.ap))
        w.shift_dram.free = (back,)
        return back

    spans = []
    width = 0
    for kt in range(key_tiles):
        q0 = kt * P if causal else 0
        spans.append((min(P, n - kt * P), q0, S - q0, width))
        width += S - q0
    rows = min(P, n)

    def key_major(g, shifted):
        pr = w.prob.next()
        for hp in range(2):
            bank = w.sc.next()
            loop.wait("tensor", bank.free, shifted)
            for j in range(G):
                h = 4 * g + G * hp + j
                for kt, (kn, q0, qn, at) in enumerate(spans):
                    mm = loop.do("tensor", lambda i, bank=bank, j=j, h=h, kt=kt, kn=kn, q0=q0, qn=qn, at=at: nc.tensor.matmul(
                        bank.ap[0:kn, j, at:at + qn], ks.ap[0:STACK + NPART, h, kt * P:kt * P + kn],
                        qs.ap[0:STACK + NPART, h, q0:q0 + qn], start=True, stop=(mask is None)))
                    if mask is not None:
                        mn = P if causal else qn
                        mm = add_mask(bank.ap[:, j, at:at + mn], mask[1][:, kt, :])
            loop.wait("scalar", mm, pr.free)
            ex = loop.do("scalar", lambda i, hp=hp, bank=bank: nc.scalar.activation(
                pr.ap[0:rows, G * hp:G * (hp + 1), 0:width], bank.ap[0:rows, :, 0:width], ACT.Exp, scale=SCALE))
            bank.free = (ex,)
        pr.written(ex)
        return pr, mm

    def weigh_values(g, pr, o_bank):
        loop.wait("tensor", pr.ready, values.ready, o_bank.free)
        base = (g % 2) * S
        for kt, (kn, q0, qn, at) in enumerate(spans):
            for j in range(4):
                mm = loop.do("tensor", lambda i, j=j, kt=kt, kn=kn, q0=q0, qn=qn, at=at: nc.tensor.matmul(
                    o_bank.ap[32 * j:32 * j + 32, 0, base + q0:base + S],
                    values.ap[0:kn, kt, 4 * g + j, :], pr.ap[0:kn, j, at:at + qn],
                    start=(kt == 0), stop=(kt == key_tiles - 1), tile_position=(0, 32 * j)))
        pr.free = (mm,)
        return mm

    for hp in range(H // G):
        got_max = query_major(hp)
        yield Y[4] if n > P else Y[5]
    shifted = shift_rows(got_max)
    yield Y[6]
    pending, raws = None, []
    for g in range(H // 4 + 1):
        if g < H // 4:
            pr, scored = key_major(g, shifted)
            yield Y[7] if n > P else Y[8]
        if pending is not None:
            if (g - 1) % 2 == 0:
                o_bank = w.pv.next()
            mm = weigh_values(g - 1, pending, o_bank)
            if (g - 1) % 2 == 1:
                raw = w.raw.next()
                loop.wait("vector", mm, raw.free)
                ev = loop.do("vector", lambda i, raw=raw, o_bank=o_bank: nc.vector.tensor_copy(
                    raw.ap, o_bank.ap[:, 0, :]))
                raw.written(ev)
                o_bank.free = (ev,)
                raws.append(raw)
            yield Y[9]
        pending = pr
    qs.free = ks.free = (scored,)
    values.free = (mm,)
    yield 1
    normed = w.normed
    loop.wait("vector", normed.free)
    for q in range(QT):
        bank = w.pv.next()
        loop.wait("tensor", bank.free)
        for g in range(H // 4):
            loop.wait("tensor", raws[g // 2].ready)
            tr = loop.do("tensor", lambda i, g=g, q=q, bank=bank, raw=raws[g // 2]: nc.tensor.transpose(
                bank.ap[:, 0, g * P:(g + 1) * P],
                raw.ap[:, (g % 2) * S + q * P:(g % 2) * S + (q + 1) * P], w.identf))
        loop.wait("vector", tr)
        per_head = bank.ap[:, 0, :].rearrange("p (h c) -> p h c", c=32)
        rc = loop.do("vector", lambda i, q=q, per_head=per_head: nc.vector.reciprocal(
            w.recip[:, q, :], per_head[:, :, HD]))
        loop.wait("vector", rc)
        mu = loop.do("vector", lambda i, per_head=per_head, q=q: nc.vector.tensor_tensor(
            normed.ap[:, q, :].rearrange("p (h c) -> p h c", c=HD), per_head[:, :, 0:HD],
            w.recip[:, q, :].unsqueeze(2).broadcast_to([P, H, HD]), ALU.mult))
        bank.free = (mu,)
    for raw in raws:
        raw.free = (tr,)
    yield 3
    bank = w.pj.next()
    loop.wait("tensor", bank.free, mu)
    for q in range(QT):
        for k in range(KT):
            tr = loop.do("tensor", lambda i, q=q, k=k, bank=bank: nc.tensor.transpose(
                bank.ap[:, 0, k * S + q * P:k * S + (q + 1) * P], normed.ap[:, q, k * P:(k + 1) * P], w.identf))
    normed.free = (tr,)
    loop.wait("scalar", tr, heads_t.free)
    for k in range(KT):
        put = loop.do("scalar", lambda i, k=k, bank=bank: nc.scalar.activation(
            heads_t.ap[:, k, :], bank.ap[:, 0, k * S:(k + 1) * S], ACT.Identity, bias=bv[:, k:k + 1]))
    bank.free = (put,)
    heads_t.written(put)
    yield 2


def project_out(w, weight, heads_t, residual, x):
    nc, loop = w.nc, w.loop
    kt = heads_t.ap.shape[1]
    loop.wait("vector", residual.ready, x.free)
    for a in range(0, w.nt, 2):
        bank = w.pj.next()
        loop.wait("tensor", bank.free, heads_t.ready)
        for j in range(2):
            for k in range(kt):
                mm = loop.do("tensor", lambda i, a=a, j=j, k=k, bank=bank: nc.tensor.matmul(
                    bank.ap[:, 0, j * D:(j + 1) * D], heads_t.ap[:, k, (a + j) * P:(a + j + 1) * P],
                    weight[:, k, :], start=(k == 0), stop=(k == kt - 1)))
        loop.wait("vector", mm)
        put = loop.do("vector", lambda i, a=a, bank=bank: nc.vector.tensor_tensor(
            x.ap[:, a:a + 2, :], bank.ap[:, 0, :].rearrange("p (t n) -> p t n", t=2),
            residual.ap[:, a:a + 2, :], ALU.add))
        bank.free = (put,)
    heads_t.read(mm)
    residual.read(put)
    x.written(put)
    yield 0.9 * kt


def add_bias(w, x, row, out):
    nc, loop = w.nc, w.loop
    loop.wait("gpsimd", x.ready, out.free)
    put = loop.do("gpsimd", lambda i: nc.gpsimd.tensor_tensor(
        out.ap, x.ap, row.unsqueeze(1).broadcast_to([P, w.nt, D]), ALU.add))
    x.read(put)
    out.written(put)


def feed_forward(w, w1, b1, w2, xt, residual, x):
    nc, loop = w.nc, w.loop
    hid = w.hidden
    loop.wait("scalar", hid.free)
    for f0 in range(0, FT, 2):
        bank = w.pj.next()
        loop.wait("tensor", bank.free, xt.ready)
        for f in (f0, f0 + 1):
            for k in range(KT):
                mm = loop.do("tensor", lambda i, f=f, k=k, bank=bank: nc.tensor.matmul(
                    bank.ap[:, 0, (f % 2) * S:(f % 2 + 1) * S], w1[:, k, f * P:(f + 1) * P], xt.ap[:, k, :],
                    start=(k == 0), stop=(k == KT - 1)))
        loop.wait("scalar", mm)
        for f in (f0, f0 + 1):
            put = loop.do("scalar", lambda i, f=f, bank=bank: nc.scalar.activation(
                hid.ap[:, f, :], bank.ap[:, 0, (f % 2) * S:(f % 2 + 1) * S], ACT.Relu, bias=b1[:, f:f + 1]))
        bank.free = (put,)
        yield 1.8
    xt.read(mm)
    hid.written(put)
    yield from project_out(w, w2, hid, residual, x)


def route(w, rw, rb, xt, pick):
    nc, loop = w.nc, w.loop
    r = w.route
    bank = w.pj.next()
    loop.wait("tensor", bank.free, xt.ready)
    for t in range(w.nt):
        for k in range(KT):
            mm = loop.do("tensor", lambda i, t=t, k=k: nc.tensor.matmul(
                bank.ap[:, 0, t * E:(t + 1) * E], xt.ap[:, k, t * P:(t + 1) * P], rw[:, k, :],
                start=(k == 0), stop=(k == KT - 1)))
    xt.read(mm)
    logit, prob = r["logit"], r["prob"]
    per_tile = lambda a: a.unsqueeze(2).broadcast_to([P, w.nt, E])

    def v(emit, *waits):
        loop.wait("vector", *waits)
        return loop.do("vector", emit)
    a = v(lambda i: nc.vector.tensor_tensor(
        logit, bank.ap[:, 0, 0:w.nt * E].rearrange("p (t e) -> p t e", e=E),
        rb.unsqueeze(1).broadcast_to([P, w.nt, E]), ALU.add), mm)
    bank.free = (a,)
    a = v(lambda i: nc.vector.tensor_reduce(r["max"], logit, AX.X, ALU.max), a)
    a = v(lambda i: nc.vector.tensor_tensor(logit, logit, per_tile(r["max"]), ALU.subtract), a)
    loop.wait("scalar", a)
    e = loop.do("scalar", lambda i: nc.scalar.activation(prob, logit, ACT.Exp))
    yield 2
    a = v(lambda i: nc.vector.tensor_reduce(r["sum"], prob, AX.X, ALU.add), e)
    a = v(lambda i: nc.vector.reciprocal(r["rsum"], r["sum"]), a)
    a = v(lambda i: nc.vector.tensor_tensor(prob, prob, per_tile(r["rsum"]), ALU.mult), a)
    loop.wait("vector", a, alone=True)
    for t in range(w.nt):
        top = loop.do("vector", lambda i, t=t: nc.vector.max(r["top"][:, t, :], prob[:, t, :]))
    loop.wait("vector", top, alone=True)
    for t in range(w.nt):
        at = loop.do("vector", lambda i, t=t: nc.vector.max_index(r["at"][:, t, :], r["top"][:, t, :], prob[:, t, :]))
    d = v(lambda i: nc.vector.tensor_tensor(r["gap"], r["top"][:, :, 1], r["top"][:, :, 0], ALU.subtract))
    v(lambda i: nc.vector.tensor_copy(pick.ap[:, :, 0:2], r["at"][:, :, 0:2]), at, pick.free)
    loop.wait("scalar", d)
    e = loop.do("scalar", lambda i: nc.scalar.activation(r["e2"], r["gap"], ACT.Exp))
    yield 2
    a = v(lambda i: nc.vector.tensor_scalar(r["one_e2"], r["e2"], 1.0, None, ALU.add), e)
    a = v(lambda i: nc.vector.reciprocal(pick.ap[:, :, 2], r["one_e2"]), a)
    a = v(lambda i: nc.vector.tensor_tensor(pick.ap[:, :, 3], r["e2"], pick.ap[:, :, 2], ALU.mult), a)
    pick.written(a)


def chain(engine, sem):
    count = [0]

    def link(ins):
        count[0] += 1
        ins.then_inc(sem, 1)
        engine.wait_ge(sem, count[0])
    return link


def place_pairs(nc, ctx, a, pick_dram, rows_dram, owner_dram):
    def sb(name, shape, dt=F32):
        return whole(ctx.enter_context(nc.sbuf_tensor("place_" + name, shape, dt)))

    n_tiles = B * QT
    pick = sb("pick", [P, n_tiles, 4])
    before, ones = sb("before", [P, P]), sb("ones", [P, P])
    iota_e, steps = sb("iota_e", [P, E]), sb("steps", [P, S // 16])
    group_no = sb("group_no", [1, GROUPS])
    chosen = [sb(f"chosen{k}", [P, n_tiles, E]) for k in range(2)]
    member = sb("member", [P, n_tiles, E])
    total, row = sb("total", [P, n_tiles, E]), sb("row", [P, n_tiles, E])
    scan = [sb(f"scan{k}", [P, n_tiles, E]) for k in range(2)]
    over = sb("over", [P, E, S // 16])
    groups, base = sb("groups", [P, E]), sb("base", [P, E])
    ends = [sb(f"ends{k}", [P, E]) for k in range(2)]
    hit = sb("hit", [P, n_tiles, E])
    rows_f, rows_u = sb("rows_f", [P, n_tiles, 2]), sb("rows_u", [P, n_tiles, 2], U32)
    passed = sb("passed", [1, GROUPS, E - 1])
    owner_f, owner_i = sb("owner_f", [1, GROUPS]), sb("owner_i", [1, GROUPS], I32)
    within = whole(ctx.enter_context(nc.psum_tensor("place_within", [P, n_tiles * E], F32)))
    sums = whole(ctx.enter_context(nc.psum_tensor("place_sums", [P, n_tiles * E], F32)))
    by_tile = lambda ap: ap.rearrange("p (t e) -> p t e", e=E)
    with nc.semaphore("place_loaded") as loaded, nc.semaphore("place_member") as member_done, \
            nc.semaphore("place_summed") as summed, nc.semaphore("place_chain") as steps_done, \
            nc.semaphore("place_rows") as rows_done, nc.Block() as block:
        @block.sync
        def _(eng):
            loads = [(pick.rearrange("p (n q) c -> p n (q c)", q=QT), pick_dram.rearrange("n p q c -> p n (q c)")),
                     (before, a["before"]), (ones, a["ones"]), (iota_e, a["iota"].partition_broadcast(P)),
                     (steps, a["steps"].partition_broadcast(P)), (group_no, a["group_no"].partition_broadcast(1))]
            for dst, src in loads:
                eng.dma_start(dst, src).then_inc(loaded, 16)
            eng.wait_ge(loaded, 16 * len(loads))
            eng.wait_ge(rows_done, 1)
            eng.dma_start(rows_dram.rearrange("t p s -> p t s"), rows_u).then_inc(loaded, 16)
            eng.dma_start(owner_dram, owner_i).then_inc(loaded, 16)
            eng.wait_ge(loaded, 16 * (len(loads) + 2))

        @block.tensor
        def _(eng):
            eng.wait_ge(member_done, 1)
            eng.matmul(within, before, member.rearrange("p t e -> p (t e)"), start=True, stop=True)
            eng.matmul(sums, ones, member.rearrange("p t e -> p (t e)"), start=True, stop=True).then_inc(summed, 1)

        @block.vector
        def _(eng):
            link = chain(eng, steps_done)
            eng.wait_ge(loaded, 16 * 6)
            for k in range(2):
                link(eng.tensor_tensor(chosen[k], iota_e.unsqueeze(1).broadcast_to([P, n_tiles, E]),
                                       pick[:, :, k:k + 1].broadcast_to([P, n_tiles, E]), ALU.is_equal))
            eng.tensor_tensor(member, chosen[0], chosen[1], ALU.add).then_inc(member_done, 1)
            eng.wait_ge(summed, 1)
            link(eng.tensor_copy(total, by_tile(sums)))
            link(eng.tensor_copy(scan[0], total))
            at, stride = 0, 1
            while stride < n_tiles:
                x, y = scan[at], scan[1 - at]
                link(eng.tensor_copy(y[:, 0:stride, :], x[:, 0:stride, :]))
                link(eng.tensor_tensor(y[:, stride:n_tiles, :], x[:, stride:n_tiles, :],
                                       x[:, 0:n_tiles - stride, :], ALU.add))
                at, stride = 1 - at, 2 * stride
            upto = scan[at]
            link(eng.tensor_tensor(over, upto[:, n_tiles - 1, :].unsqueeze(2).broadcast_to([P, E, S // 16]),
                                   steps.unsqueeze(1).broadcast_to([P, E, S // 16]), ALU.is_gt))
            link(eng.tensor_reduce(groups, over, AX.X, ALU.add))
            link(eng.tensor_copy(ends[0], groups))
            last, stride = 0, 1
            while stride < E:
                x, y = ends[last], ends[1 - last]
                link(eng.tensor_copy(y[:, 0:stride], x[:, 0:stride]))
                link(eng.tensor_tensor(y[:, stride:E], x[:, stride:E], x[:, 0:E - stride], ALU.add))
                last, stride = 1 - last, 2 * stride
            end = ends[last]
            link(eng.tensor_tensor(base, end, groups, ALU.subtract))
            link(eng.tensor_scalar(base, base, float(GROUP), None, ALU.mult))
            link(eng.tensor_tensor(row, upto, total, ALU.subtract))
            link(eng.tensor_tensor(row, row, base.unsqueeze(1).broadcast_to([P, n_tiles, E]), ALU.add))
            link(eng.tensor_tensor(row, by_tile(within), row, ALU.add))
            for k in range(2):
                link(eng.tensor_tensor(hit, chosen[k], row, ALU.mult))
                link(eng.tensor_reduce(rows_f[:, :, k], hit, AX.X, ALU.add))
            link(eng.tensor_copy(rows_u, rows_f))
            link(eng.tensor_tensor(passed, end[0:1, 0:E - 1].unsqueeze(1).broadcast_to([1, GROUPS, E - 1]),
                                   group_no.unsqueeze(2).broadcast_to([1, GROUPS, E - 1]), ALU.is_le))
            link(eng.tensor_reduce(owner_f, passed, AX.X, ALU.add))
            eng.tensor_copy(owner_i, owner_f).then_inc(rows_done, 1)


def spread_pairs(nc, ctx, x_dram, rows_dram, sorted_dram):
    many = 8
    rows = [whole(ctx.enter_context(nc.sbuf_tensor(f"spread_rows{t}", [P, 2], U32))) for t in range(many)]
    x = whole(ctx.enter_context(nc.sbuf_tensor("spread_x", [P, many, D], F32)))
    x_v = x_dram.rearrange("(i m) (q p) d -> i p (m q) d", m=many // QT, p=P)
    trips = B * QT // many
    with nc.semaphore("spread_loaded") as loaded, nc.semaphore("spread_sent") as sent, \
            nc.semaphore("spread_waits") as waits, nc.Block() as block:
        @block.gpsimd
        def _(eng):
            with eng.Fori(0, trips) as i:
                eng.dma_start(x, x_v[i]).then_inc(loaded, 16)
                for t in range(many):
                    eng.dma_start(rows[t], rows_dram[i * many + t]).then_inc(loaded, 16)
                eng.wait_ge(loaded, (i + 1) * (16 * (many + 1)))
                eng.sem_inc(waits, 1)
                for t in range(many):
                    for k in range(2):
                        eng.indirect_dma_start(
                            sorted_dram, bass.IndirectOffsetOnAxis(ap=rows[t][:, k:k + 1], axis=0),
                            x[:, t, :], None).then_inc(sent, 16)
                eng.wait_ge(sent, (i + 1) * (32 * many))


class Constants:

    def __init__(self, nc, ctx, name):
        self.nc, self.ctx, self.name, self.loads, self.fills = nc, ctx, name, [], []

    def sb(self, name, shape, dt=F32):
        return whole(self.ctx.enter_context(self.nc.sbuf_tensor(f"{self.name}_{name}", shape, dt)))

    def weight(self, name, src):
        rows, cols = src.shape
        t = self.sb(name, [P, rows // P, cols])
        self.loads.append((t[:, :, :], src.rearrange("(k p) n -> p k n", p=P)))
        return t

    def load(self, name, shape, src, dt=F32):
        t = self.sb(name, shape, dt)
        self.loads.append((t[tuple(slice(None) for _ in shape)], src))
        return t

    def fill(self, ap, value):
        self.fills.append((ap, value))

    def emit(self):
        nc = self.nc
        with nc.semaphore(f"{self.name}_loaded") as loaded, nc.semaphore(f"{self.name}_filled") as filled, \
                nc.Block() as block:
            @block.sync
            def _(eng):
                for dst, src in self.loads:
                    eng.dma_start(dst, src).then_inc(loaded, 16)
                eng.wait_ge(loaded, 16 * len(self.loads))

            @block.gpsimd
            def _(eng):
                for k, (ap, value) in enumerate(self.fills):
                    eng.memset(ap, value).then_inc(filled, 1)
                    eng.wait_ge(filled, k + 1)
                eng.wait_ge(filled, len(self.fills))


def common_psum(w):
    w.sc = w.psum("scores", [2, 2])
    w.pj = w.psum("project", [1, 1])


def attention_buffers(w, c, dram, width):
    w.tok = w.ring("tok", 4, [P, QT, D])
    w.xt = w.ring("xt", 1, [P, KT, S])
    w.parts_q = w.buffer("parts_q", [P, NPART, KT, S], BF16)
    w.parts_k = w.buffer("parts_k", [P, NPART, KT, S], BF16)
    w.rest = w.buffer("rest", [P, KT, S])
    w.qs = w.buffer("qs", [P, H, S], BF16)
    w.hidden = View(w.qs, w.qs.ap.rearrange("p h t -> p (h t)").bitcast(F32).rearrange("p (f t) -> p f t", t=S))
    w.ks = w.buffer("ks", [STACK + NPART, H, S], BF16)
    w.values = w.buffer("values", [P, QT, H, 32])
    w.ctx_ks = w.buffer("ctx_ks", [STACK + NPART, H, C], BF16)
    w.ctx_values = w.buffer("ctx_values", [C, 1, H, 32])
    w.maxima = w.buffer("maxima", [P, QT, H])
    w.shift = w.buffer("shift", [H, NPART, S], BF16)
    w.prob = w.ring("prob", 2, [P, 4, width])
    w.raw = w.ring("raw", 2, [P, 2 * S])
    w.normed = w.buffer("normed", [P, QT, D])
    w.recip = w.sb("recip", [P, QT, H])
    w.heads_t = w.buffer("heads_t", [P, KT, S])
    w.ctx_t = w.buffer("ctx_t", [P, KT, C])
    w.loaded = w.buffer("loaded", [P, QT, D])
    norm_buffers(w)
    w.q_dram, w.k_dram, w.c_dram, w.shift_dram = [Buffer(dram[n]) for n in ("q", "k", "c", "shift")]
    w.all += [w.q_dram, w.k_dram, w.c_dram, w.shift_dram]
    for values, ks in ((w.values, w.ks), (w.ctx_values, w.ctx_ks)):
        c.fill(values.ap[:, :, :, HD:HD + 1], 1.0)
        c.fill(values.ap[:, :, :, HD + 1:32], 0.0)
        c.fill(ks.ap[STACK:STACK + NPART, :, :], 1.0)


def norm_buffers(w):
    w.ln_stats = w.buffer("ln_stats", [P, w.nt, 6])
    w.ln_moments = w.buffer("ln_moments", [P, w.nt, 2])
    w.ln_rstd = w.buffer("ln_rstd", [P, 2, w.nt])


def self_attention(w, wt, xt, mask, causal, heads_t, following):
    q_bias, k_bias, v_bias = wt["biases"]
    project_parts(w, wt["q"], q_bias, xt, S, w.parts_q)
    send_parts(w, w.parts_q, w.q_dram, S, "q")
    yield Y[0]
    project_parts(w, wt["k"], k_bias, xt, S, w.parts_k)
    send_parts(w, w.parts_k, w.k_dram, S, "k")
    stack_parts(w, w.q_dram, w.qs, S, Q_RUNS, "q")
    stack_parts(w, w.k_dram, w.ks, S, K_RUNS, "k")
    yield Y[0]
    project_values(w, wt["v"], xt, [(t * P, P) for t in range(QT)], w.values)
    yield Y[1]
    context_operands(w, following)
    yield Y[2]
    yield from attend(w, w.qs, w.ks, w.values, S, causal, mask, heads_t, v_bias)


def context_operands(w, wt):
    project_parts(w, wt["k"], wt["biases"][1], w.ctx_t, C, w.parts_k)
    send_parts(w, w.parts_k, w.c_dram, C, "c")
    project_values(w, wt["v"], w.ctx_t, [(0, C)], w.ctx_values)
    stack_parts(w, w.c_dram, w.ctx_ks, C, K_RUNS, "c")


def cross_attention(w, wt, xt, heads_t):
    q_bias, _, v_bias = wt["biases"]
    project_parts(w, wt["q"], q_bias, xt, S, w.parts_q)
    send_parts(w, w.parts_q, w.q_dram, S, "q")
    stack_parts(w, w.q_dram, w.qs, S, Q_RUNS, "q")
    yield Y[3]
    yield from attend(w, w.qs, w.ctx_ks, w.ctx_values, C, False, None, heads_t, v_bias)


def attention_layer(w, wt, kind, xt, x, mask=None, causal=False, following=None):
    if wt["out_bias"] is not None:
        residual = w.tok.next()
        add_bias(w, x, wt["out_bias"], residual)
    else:
        residual = x
    if kind == "self":
        yield from self_attention(w, wt, xt, mask, causal, w.heads_t, following)
    else:
        yield from cross_attention(w, wt, xt, w.heads_t)
    out = w.tok.next()
    yield from project_out(w, wt["o"], w.heads_t, residual, out)
    return out


def pre_norm(w, x, gain, shift):
    xn = w.tok.next()
    yield from normalise(w, x, xn)
    xt = to_features(w, xn, gain, shift)
    yield 2
    return xt


def post_norm_into(w, x, out, gain, shift):
    yield from normalise(w, x, out)
    gain_and_shift(w, out, gain, shift)
    yield 3


def post_norm(w, x, gain, shift):
    out = w.tok.next()
    yield from post_norm_into(w, x, out, gain, shift)
    return out


def fetch(w, buf, stream, ahead, emit):
    loop = w.loop
    loop.wait("gpsimd", buf.free)
    if ahead:
        buf.written(loop.dma_ahead(f"{w.name}_{stream}_ahead", emit))
        buf.first.tokens = buf.ready
    else:
        buf.written(loop.dma("gpsimd", f"{w.name}_{stream}", emit))


def loaded_ahead(buf):
    buf.first = Late()
    buf.ready = (buf.first,)


def next_sequence(b):
    return (b + LANES, False) if b + LANES < NB else (b % LANES, True)


def fetch_tokens(w, src, b):
    at, ahead = next_sequence(b)
    fetch(w, w.loaded, "x", ahead, lambda i: w.nc.gpsimd.dma_start(w.loaded.ap, src(at)(i)))


def fetch_context(w, ctx_t, b):
    at, ahead = next_sequence(b)
    fetch(w, w.ctx_t, "ctx", ahead, lambda i: w.nc.gpsimd.dma_start(w.ctx_t.ap, ctx_t(at)(i)))


def store(w, x, dst, name):
    nc, loop = w.nc, w.loop
    loop.wait("sync", x.ready)
    x.read(loop.dma("sync", f"{w.name}_{name}", lambda i: nc.sync.dma_start(dst(i), x.ap)))


def sequence(ap, b):
    v = ap.rearrange("(i b) (q p) d -> i b p q d", b=NB, p=P)
    return lambda i: v[i, b]


def pairs(ap):
    v = ap.rearrange("(i b) (q p) d -> i p (b q) d", b=NB, p=P)
    return lambda i: v[i]


def by_feature(c, name, packed, at, n):
    return packed[:, at:at + n]


def build(nc, a, out):
    def scratch(name, shape, dt=F32):
        return nc.dram_tensor(name, shape, dt, kind="Internal").ap()

    x1 = scratch("x_moe_in", [B, S, D])
    pick_dram = scratch("pick", [B, P, QT, 4])
    rows_dram = scratch("pair_rows", [B * QT, P, 2], U32)
    owner_dram = scratch("group_expert", [1, GROUPS], I32)
    sorted_dram = scratch("sorted_in", [GROUPS * GROUP, D])
    result_dram = scratch("sorted_out", [GROUPS * GROUP, D])
    dram = [{"q": scratch(f"q_parts{b}", [NPART, D * S], BF16), "k": scratch(f"k_parts{b}", [NPART, D * S], BF16),
             "c": scratch(f"ctx_k_parts{b}", [NPART, D * C], BF16),
             "shift": scratch(f"shift_parts{b}", [NPART, H, S], BF16)} for b in range(LANES)]
    ctx_v = a["ctx_t"].rearrange("(k p) (i b t) -> i b p k t", p=P, b=NB, t=C)
    ctx_t = lambda b: lambda i: ctx_v[i, b]
    cols, rows = a["columns"], a["rows"]

    def common(c):
        packed = c.load("columns", [P, len(COLUMNS)], cols)
        column = lambda name: packed[:, COLUMNS.index((name, 0)):COLUMNS.index((name, 0)) + sum(n == name for n, _ in COLUMNS)]
        identf = c.load("identity", [P, P], a["identity"])
        return column, identf

    def row(c, name):
        r = c.load("row_" + name, [P, D], rows[ROWS.index(name)].partition_broadcast(P))
        return r[:, :]

    def attention_weights(c, column, layer, at, names, bias_names, out_bias):
        wt = {k: c.weight(f"{layer}_{at}_{k}", a[n]) for k, n in zip("qkvo", names)}
        wt["biases"] = [column(n) for n in bias_names]
        wt["out_bias"] = row(c, out_bias) if out_bias else None
        return wt

    def attention_works(ctx, c, loop, identf, name, width):
        shared = Work(nc, ctx, name, loop, QT)
        common_psum(shared)
        loop.next_trip = c.load("next_trip", [1, TRIPS], a["next_trip"].partition_broadcast(1), I32)
        minus_half = c.sb("minus_half", [P, QT])[:, :]
        c.fill(minus_half, -0.5)
        identb = c.sb("identb", [P, P], BF16)[:, :]
        works = []
        for b in range(LANES):
            w = Work(nc, ctx, f"{name}{b}", loop, QT, psum_of=shared)
            w.identf, w.identb, w.minus_half = identf[:, :], identb, minus_half
            attention_buffers(w, c, dram[b], width)
            loaded_ahead(w.loaded)
            loaded_ahead(w.ctx_t)
            works.append(w)
        return shared, works

    with ExitStack() as ctx:
        c = Constants(nc, ctx, "a_const")
        column, identf = common(c)
        loop = Loop(nc, ctx, "a", TRIPS)
        shared, works = attention_works(ctx, c, loop, identf, "a", S + P)
        L0s = attention_weights(c, column, "l0", "self", ["L0_xattn_mq_w", "L0_xattn_mk_w", "L0_xattn_mv_w", "L0_xattn_m_proj_w"],
                                ["L0_xattn_mq_b", "L0_xattn_mk_b", "L0_xattn_mv_b"], "L0_xattn_m_proj_b")
        L0c = attention_weights(c, column, "l0", "cross", ["L0_xattn_cq_w", "L0_xattn_ck_w", "L0_xattn_cv_w", "L0_xattn_c_proj_w"],
                                ["L0_xattn_cq_b", "L0_xattn_ck_b", "L0_xattn_cv_b"], "L0_xattn_c_proj_b")
        f1, f2 = c.weight("f1", a["L0_xattn_f_w1"]), c.weight("f2", a["L0_xattn_f_w2"])
        f_b2 = row(c, "L0_xattn_f_b2")
        n1 = lambda q: f"L1_xattn_{q}"
        L1 = {at: attention_weights(c, column, "l1", at, [n1(f"{at}_w{k}") for k in "qkvo"],
                                    [n1(f"{at}_b{k}") for k in "qkv"], n1(f"{at}_bo")) for at in ("sa", "ca")}
        ln = {k: row(c, n1(k)) for k in ("ln1_g", "ln1_b", "ln2_g", "ln2_b")}
        rw = c.weight("router", a["L1_xattn_router_w"])
        rb = c.load("router_b", [P, E], a["L1_xattn_router_b"].partition_broadcast(P))
        causal_f = c.load("causal", [P, 2, P], a["causal"])
        mask_b = c.sb("mask_b", [P, 2, P], BF16)
        for w in works:
            w.pick = w.buffer("pick", [P, QT, 4])
            w.route = {n: w.sb("route_" + n, sh, d) for n, sh, d in [
                ("logit", [P, QT, E], F32), ("prob", [P, QT, E], F32), ("max", [P, QT], F32), ("sum", [P, QT], F32),
                ("rsum", [P, QT], F32), ("top", [P, QT, E], F32), ("at", [P, QT, E], U32), ("gap", [P, QT], F32),
                ("e2", [P, QT], F32), ("one_e2", [P, QT], F32)]}
        zeros = c.sb("zeros", [P, D])
        c.fill(zeros[:, :], 0.0)
        c.emit()
        with nc.semaphore("sorted_cleared") as cleared, nc.Block() as block:
            @block.vector
            def _(eng):
                eng.tensor_copy(works[0].identb, works[0].identf)
                eng.tensor_copy(mask_b[:, :, :], causal_f[:, :, :])

            @block.sync
            def _(eng):
                rows_each = GROUPS * GROUP // P
                eng.dma_start(sorted_dram.rearrange("(p r) d -> p r d", p=P),
                              zeros[:, :].unsqueeze(1).broadcast_to([P, rows_each, D])).then_inc(cleared, 16)
                eng.wait_ge(cleared, 16)
        mask = (Diagonal(mask_b[:, 0, :]), Diagonal(mask_b[:, 1, :]))

        def steps(w, b):
            xt = yield from pre_norm(w, w.loaded, column("L0_xattn_ln1_g"), column("L0_xattn_ln1_b"))
            x = yield from attention_layer(w, L0s, "self", xt, w.loaded, mask, True, L0c)
            fetch_tokens(w, lambda b: sequence(a["x"], b), b)
            xt = yield from pre_norm(w, x, column("L0_xattn_ln2_g"), column("L0_xattn_ln2_b"))
            x = yield from attention_layer(w, L0c, "cross", xt, x)
            xt = yield from pre_norm(w, x, column("L0_xattn_ln3_g"), column("L0_xattn_ln3_b"))
            residual = w.tok.next()
            add_bias(w, x, f_b2, residual)
            x = w.tok.next()
            yield from feed_forward(w, f1, column("L0_xattn_f_b1"), f2, xt, residual, x)

            xt = to_features(w, x)
            yield 2
            x = yield from attention_layer(w, L1["sa"], "self", xt, x, mask, True, L1["ca"])
            fetch_context(w, ctx_t, b)
            x = yield from post_norm(w, x, ln["ln1_g"], ln["ln1_b"])
            xt = to_features(w, x)
            yield 2
            x = yield from attention_layer(w, L1["ca"], "cross", xt, x)
            x = yield from post_norm(w, x, ln["ln2_g"], ln["ln2_b"])
            store(w, x, sequence(x1, b), "x1")
            xt = to_features(w, x)
            yield 2
            yield from route(w, rw, rb[:, :], xt, w.pick)
            store(w, w.pick, lambda i: pick_dram[i * NB + b], "pick")
            yield 3

        take_turns(lane(steps, works[0], 0), lane(steps, works[1], 1), LEAD)
        for w in [shared] + works:
            w.close()
        with nc.Block() as block:
            loop.emit(block)

    with ExitStack() as ctx:
        place_pairs(nc, ctx, a, pick_dram, rows_dram, owner_dram)
    with ExitStack() as ctx:
        spread_pairs(nc, ctx, x1, rows_dram, sorted_dram)
    with ExitStack() as ctx:
        c = Constants(nc, ctx, "b_const")
        identf = c.load("identity", [P, P], a["identity"])
        owner = c.load("owner", [1, GROUPS], owner_dram, I32)
        loop = Loop(nc, ctx, "b", GROUPS // UNROLL)
        w = Work(nc, ctx, "b", loop, QT)
        w.identf = identf[:, :]
        w.xt = w.ring("xt", 2, [P, KT, GROUP])
        xs = w.ring("x", 2, [P, QT, D])
        ys = w.ring("y", 2, [P, QT, D])
        w1s = w.ring("w1_", UNROLL, [P, KT, FF])
        w2s = w.ring("w2_", UNROLL, [P, FT, D])
        b1s = w.ring("b1_", UNROLL, [P, FT])
        b2s = w.ring("b2_", UNROLL, [P, D])
        hidden = w.ring("hidden", 2, [P, FT, GROUP])
        w.pj = w.psum("project", [1] * 8)
        c.emit()
        in_v = sorted_dram.rearrange("(i g q p) d -> i g p q d", g=UNROLL, q=QT, p=P)
        out_v = result_dram.rearrange("(i g q p) d -> i g p q d", g=UNROLL, q=QT, p=P)
        w1_v = a["L1_xattn_e_w1"].rearrange("e (k p) n -> e p k n", p=P)
        w2_v = a["L1_xattn_e_w2"].rearrange("e (k p) n -> e p k n", p=P)
        expert = {}

        def load(g):
            w1, w2, b1, b2, x = w1s.next(), w2s.next(), b1s.next(), b2s.next(), xs.next()

            def w1_load(i):
                expert[g] = nc.sync.value_load(owner[0:1, bass.ds(i * UNROLL + g, 1)], min_val=0, max_val=E - 1)
                return nc.sync.dma_start(w1.ap, w1_v[expert[g]])
            loop.wait("sync", w1.free, w2.free, b1.free, b2.free, x.free)
            w1.written(loop.dma("sync", f"w1_{g}", w1_load))
            x.written(loop.dma("sync", f"x_{g}", lambda i: nc.sync.dma_start(x.ap, in_v[i, g])))
            b1.written(loop.dma("sync", f"b1_{g}", lambda i: nc.sync.dma_start(b1.ap, a["e_b1"][expert[g]])))
            w2.written(loop.dma("sync", f"w2_{g}", lambda i: nc.sync.dma_start(w2.ap, w2_v[expert[g]])))
            b2.written(loop.dma("sync", f"b2_{g}", lambda i: nc.sync.dma_start(
                b2.ap, a["L1_xattn_e_b2"][expert[g]].partition_broadcast(P))))
            return w1, w2, b1, b2, x

        def hide(got):
            w1, w2, b1, b2, x = got
            xt, hid = to_features(w, x), hidden.next()
            loop.wait("scalar", hid.free, b1.ready)
            for f0 in range(0, FT, 2):
                bank = w.pj.next()
                loop.wait("tensor", bank.free, xt.ready, w1.ready)
                for f in (f0, f0 + 1):
                    for k in range(KT):
                        mm = loop.do("tensor", lambda i, f=f, k=k, bank=bank: nc.tensor.matmul(
                            bank.ap[:, 0, (f % 2) * GROUP:(f % 2 + 1) * GROUP], w1.ap[:, k, f * P:(f + 1) * P],
                            xt.ap[:, k, :], start=(k == 0), stop=(k == KT - 1)))
                loop.wait("scalar", mm)
                for f in (f0, f0 + 1):
                    put = loop.do("scalar", lambda i, f=f, bank=bank: nc.scalar.activation(
                        hid.ap[:, f, :], bank.ap[:, 0, (f % 2) * GROUP:(f % 2 + 1) * GROUP], ACT.Gelu,
                        bias=b1.ap[:, f:f + 1]))
                bank.free = (put,)
            xt.read(mm)
            w1.free, b1.free = (mm,), (put,)
            hid.written(put)
            return hid

        def finish(g, got, hid):
            w1, w2, b1, b2, x = got
            y = ys.next()
            bank = w.pj.next()
            loop.wait("tensor", bank.free, hid.ready, w2.ready)
            for q in range(QT):
                for f in range(FT):
                    mm = loop.do("tensor", lambda i, q=q, f=f: nc.tensor.matmul(
                        bank.ap[:, 0, q * D:(q + 1) * D], hid.ap[:, f, q * P:(q + 1) * P], w2.ap[:, f, :],
                        start=(f == 0), stop=(f == FT - 1)))
            hid.free = w2.free = (mm,)
            loop.wait("vector", mm, b2.ready, y.free)
            put = loop.do("vector", lambda i: nc.vector.tensor_tensor(
                y.ap, bank.ap[:, 0, :].rearrange("p (q n) -> p q n", q=QT),
                b2.ap.unsqueeze(1).broadcast_to([P, QT, D]), ALU.add))
            bank.free = b2.free = (put,)
            loop.wait("scalar", put)
            y.free = (loop.dma("scalar", f"y_{g}", lambda i: nc.scalar.dma_start(out_v[i, g], y.ap)),)

        got = [load(g) for g in range(UNROLL)]
        hid = hide(got[0])
        for g in range(UNROLL):
            following = hide(got[g + 1]) if g + 1 < UNROLL else None
            finish(g, got[g], hid)
            hid = following
        w.close()
        with nc.Block() as block:
            loop.emit(block)

    with ExitStack() as ctx:
        c = Constants(nc, ctx, "c_const")
        column, identf = common(c)
        loop = Loop(nc, ctx, "c", TRIPS)
        shared, works = attention_works(ctx, c, loop, identf, "c", 2 * S)
        n2 = lambda q: f"L2_xattn_{q}"
        L2 = {at: attention_weights(c, column, "l2", at, [n2(f"{at}_w{k}") for k in "qkvo"],
                                    [n2(f"{at}_b{k}") for k in "qkv"], n2(f"{at}_bo")) for at in ("sa", "ca")}
        f1, f2 = c.weight("f1", a[n2("ff_w1")]), c.weight("f2", a[n2("ff_w2")])
        f_b2 = row(c, n2("ff_b2"))
        ln = {k: row(c, n2(k)) for k in ("ln1_g", "ln1_b", "ln2_g", "ln2_b", "ln3_g", "ln3_b")}
        L3 = attention_weights(c, column, "l3", "cross", [f"L3_xattn_W{k}" for k in "qkvo"],
                               [f"L3_xattn_b{k}" for k in "qkv"], None)
        g, s = row(c, "L3_xattn_ln_gamma"), row(c, "L3_xattn_ln_beta")
        ln3 = {k: row(c, n1(f"ln3_{k}")) for k in "gb"}
        mask_i = works[0].prob.buffers[0].ap[:, 0:QT, 0:S].bitcast(I32)
        mask_f = works[0].prob.buffers[1].ap[:, 0:QT, 0:S]
        c.loads.append((mask_i, a["mask"].rearrange("(q p) k -> p q k", p=P)))
        mask_q = c.sb("mask_q", [P, QT, S], BF16)
        mask_k = c.sb("mask_k", [P, QT, S], BF16)
        c.emit()
        with nc.semaphore("mask_f_done") as mask_f_done, nc.semaphore("mask_turned") as mask_turned, nc.Block() as block:
            mask_bank = shared.pj.buffers[0].ap

            @block.vector
            def _(eng):
                eng.tensor_copy(works[0].identb, works[0].identf)
                eng.tensor_scalar(mask_f[:, :, :], mask_i[:, :, :], 0.0, NEG, ALU.is_equal, ALU.mult).then_inc(mask_f_done, 1)
                eng.wait_ge(mask_f_done, 1)
                eng.tensor_copy(mask_q[:, :, :], mask_f[:, :, :])
                eng.wait_ge(mask_turned, 1)
                eng.tensor_copy(mask_k[:, :, :], mask_bank[:, 0, :].rearrange("p (k q) -> p k q", k=QT))

            @block.tensor
            def _(eng):
                eng.wait_ge(mask_f_done, 1)
                for k in range(QT):
                    for q in range(QT):
                        ins = eng.transpose(mask_bank[:, 0, k * S + q * P:k * S + (q + 1) * P],
                                            mask_f[:, q, k * P:(k + 1) * P], works[0].identf)
                ins.then_inc(mask_turned, 1)

        for w in works:
            w.pair_rows = w.buffer("pair_rows", [P, 2 * QT], U32)
            w.pair_y = w.buffer("pair_y", [P, 2 * QT, D])
            w.pick = w.buffer("pick", [P, QT, 4])

        for w in works:
            for buf in (w.pair_rows, w.pair_y, w.pick):
                loaded_ahead(buf)

        def fetch_pairs(w, b):
            fetch_tokens(w, lambda b: sequence(x1, b), b)
            at, ahead = next_sequence(b)
            rows, y, pick = w.pair_rows, w.pair_y, w.pick
            for q in range(QT):
                if q:
                    rows.free = ()
                fetch(w, rows, "rows", ahead, lambda i, q=q: nc.gpsimd.dma_start(
                    rows.ap[:, 2 * q:2 * q + 2], rows_dram[(i * NB + at) * QT + q]))
            fetch(w, pick, "pick", ahead, lambda i: nc.gpsimd.dma_start(pick.ap, pick_dram[i * NB + at]))
            if ahead:
                loop.wait_ahead(rows.ready[0])
            else:
                loop.wait("gpsimd", rows.ready)
            loop.wait("gpsimd", y.free)
            y.free = ()
            for j in range(2 * QT):
                fetch(w, y, "y", ahead, lambda i, j=j: nc.gpsimd.indirect_dma_start(
                    y.ap[:, j, :], None, result_dram, bass.IndirectOffsetOnAxis(ap=rows.ap[:, j:j + 1], axis=0)))
            rows.free = y.ready

        def mix_experts(w):
            x, y, pick = w.loaded, w.pair_y, w.pick
            out = w.tok.next()
            loop.wait("vector", x.ready, pick.ready, y.ready, out.free)
            for q in range(QT):
                mid = loop.do("vector", lambda i, q=q: nc.vector.scalar_tensor_tensor(
                    out.ap[:, q, :], y.ap[:, 2 * q, :], pick.ap[:, q, 2:3], x.ap[:, q, :], ALU.mult, ALU.add))
            loop.wait("vector", mid)
            for q in range(QT):
                put = loop.do("vector", lambda i, q=q: nc.vector.scalar_tensor_tensor(
                    out.ap[:, q, :], y.ap[:, 2 * q + 1, :], pick.ap[:, q, 3:4], out.ap[:, q, :], ALU.mult, ALU.add))
            x.read(mid)
            y.free = pick.free = (put,)
            out.written(put)
            yield 1
            return out

        def steps(w, b):
            x = yield from mix_experts(w)
            fetch_pairs(w, b)
            x = yield from post_norm(w, x, ln3["g"], ln3["b"])
            xt = to_features(w, x)
            yield 2
            x = yield from attention_layer(w, L2["sa"], "self", xt, x, (mask_q, mask_k), False, L2["ca"])
            x = yield from post_norm(w, x, ln["ln1_g"], ln["ln1_b"])
            xt = to_features(w, x)
            yield 2
            x = yield from attention_layer(w, L2["ca"], "cross", xt, x)
            x = yield from post_norm(w, x, ln["ln2_g"], ln["ln2_b"])
            xt = to_features(w, x)
            yield 2
            residual = w.tok.next()
            add_bias(w, x, f_b2, residual)
            x = w.tok.next()
            context_operands(w, L3)
            fetch_context(w, ctx_t, b)
            yield from feed_forward(w, f1, column(n2("ff_b1")), f2, xt, residual, x)
            x = yield from post_norm(w, x, ln["ln3_g"], ln["ln3_b"])
            xt = to_features(w, x)
            yield 2
            x = yield from attention_layer(w, L3, "cross", xt, x)
            x = yield from post_norm(w, x, g, s)
            store(w, x, sequence(out, b), "out")
            yield 2

        take_turns(lane(steps, works[0], 0), lane(steps, works[1], 1), LEAD)
        for w in [shared] + works:
            w.close()
        with nc.Block() as block:
            loop.emit(block)


class Diagonal:

    def __init__(self, tile):
        self.tile = tile

    def __getitem__(self, _):
        return self.tile


_VECTORS = (["L0_xattn_ln1_g", "L0_xattn_ln1_b", "L0_xattn_ln2_g", "L0_xattn_ln2_b", "L0_xattn_ln3_g",
             "L0_xattn_ln3_b", "L0_xattn_mq_b", "L0_xattn_mk_b", "L0_xattn_mv_b", "L0_xattn_cq_b",
             "L0_xattn_ck_b", "L0_xattn_cv_b", "L0_xattn_f_b1", "L2_xattn_ff_b1"]
            + [f"{l}_xattn_{at}_b{k}" for l in ("L1", "L2") for at in ("sa", "ca") for k in "qkv"]
            + [f"L3_xattn_b{k}" for k in "qkv"])
_TURNED = [n for n in _VECTORS if n[-2:] in ("bq", "bk") or n[-3:-1] == "q_" or n[-4:] in ("mq_b", "mk_b", "cq_b", "ck_b")]
_SIZES = {"L0_xattn_f_b1": FF, "L2_xattn_ff_b1": FF}
COLUMNS = [(n, k) for n in _VECTORS for k in range(_SIZES.get(n, D) // P)]
ROWS = (["L0_xattn_m_proj_b", "L0_xattn_c_proj_b", "L0_xattn_f_b2", "L2_xattn_ff_b2",
         "L3_xattn_ln_gamma", "L3_xattn_ln_beta"]
        + [f"{l}_xattn_{at}_bo" for l in ("L1", "L2") for at in ("sa", "ca")]
        + [f"{l}_xattn_ln{k}_{j}" for l in ("L1", "L2") for k in (1, 2, 3) for j in "gb"])


def kernel(**inputs):
    import concourse.bacc as bacc
    from concourse.bass_utils import run_bass_kernel_spmd

    v = {k: np.asarray(x) for k, x in inputs.items()}
    turn = lambda x: np.moveaxis(x.reshape(x.shape[:-1] + (H, HD)), -1, -2).reshape(x.shape)
    arrays = {"x": v["x"], "mask": v["mask_1x1xSxS_ik0"].reshape(S, S),
              "ctx_t": v["ctx_1024"].reshape(B * C, D).T,
              "columns": np.concatenate([(turn(v[n].reshape(D)) if n in _TURNED else v[n]).reshape(-1, P)
                                         for n in _VECTORS]).T,
              "rows": np.stack([v[n] for n in ROWS]),
              "identity": np.eye(P, dtype=np.float32),
              "iota": np.arange(E, dtype=np.float32),
              "ones": np.ones((P, P), np.float32),
              "before": np.triu(np.ones((P, P), np.float32), 1),
              "steps": np.arange(S // 16, dtype=np.float32) * GROUP,
              "next_trip": ((np.arange(TRIPS) + 1) % TRIPS).astype(np.int32),
              "group_no": np.arange(GROUPS, dtype=np.float32),
              "e_b1": v["L1_xattn_e_b1"].reshape(E, FT, P).transpose(0, 2, 1)}
    k, q = np.meshgrid(np.arange(P), np.arange(P))
    future = np.where(k > q, np.float32(NEG), np.float32(0))
    arrays["causal"] = np.stack([future, future.T], axis=1)
    for n in ("mq", "mk", "mv", "cq", "ck", "cv"):
        arrays[f"L0_xattn_{n}_w"] = v[f"L0_xattn_{n}_w"].transpose(1, 0, 2).reshape(D, D)
    for n in ("L0_xattn_m_proj_w", "L0_xattn_c_proj_w", "L0_xattn_f_w1", "L0_xattn_f_w2", "L1_xattn_router_w",
              "L1_xattn_router_b", "L1_xattn_e_w1", "L1_xattn_e_w2", "L1_xattn_e_b2"):
        arrays[n] = v[n]
    for at in ("sa", "ca"):
        for m in "qkvo":
            arrays[f"L1_xattn_{at}_w{m}"] = v[f"L1_xattn_{at}_w{m}"]
            arrays[f"L2_xattn_{at}_w{m}"] = v[f"L2_xattn_{at}_w{m}"].T
    for m in (1, 2):
        arrays[f"L2_xattn_ff_w{m}"] = v[f"L2_xattn_ff_w{m}"].T
    for m in "qkvo":
        arrays[f"L3_xattn_W{m}"] = v[f"L3_xattn_W{m}"]
    for n in ("L0_xattn_mq_w", "L0_xattn_mk_w", "L0_xattn_cq_w", "L0_xattn_ck_w", "L3_xattn_Wq", "L3_xattn_Wk",
              *(f"{l}_xattn_{at}_w{m}" for l in ("L1", "L2") for at in ("sa", "ca") for m in "qk")):
        arrays[n] = turn(arrays[n])
    arrays = {n: np.ascontiguousarray(x) for n, x in arrays.items()}

    nc = bacc.Bacc("TRN2", target_bir_lowering=False, num_devices=1)
    ins = {n: nc.dram_tensor(f"in_{n}", x.shape, mybir.dt.from_np(x.dtype), kind="ExternalInput").ap()
           for n, x in arrays.items()}
    out = nc.dram_tensor("out", (B, S, D), F32, kind="ExternalOutput").ap()
    build(nc, ins, out)
    r = run_bass_kernel_spmd(nc, [{f"in_{n}": x for n, x in arrays.items()}], core_ids=[0])
    return r.results[0]["out"]
```

```python
from contextlib import ExitStack

import numpy as np
import concourse.bass as bass
import concourse.mybir as mybir

F32, BF16 = mybir.dt.float32, mybir.dt.bfloat16
I32, U32 = mybir.dt.int32, mybir.dt.uint32
ALU = mybir.AluOpType
ACT = mybir.ActivationFunctionType
AX = mybir.AxisListType

P = 128
B, S, D = 16, 256, 256
H, HD = 16, 16
C = 77
FF, E = 1024, 8
LANES = 2
NB = 2 * LANES
TRIPS = B // NB
KT = D // P
FT = FF // P
QT = S // P
NPART = 3
STACK = 6 * HD
EPS = 1e-5
GROUP = S
UNROLL = 4
GROUPS = -(-(2 * B * S // GROUP + E) // UNROLL) * UNROLL
STACK_SELF, STACK_CROSS, SHIFT = 8, 11, 6
LEAD = 7.0
NEG = -float(2 ** 100)
SCALE = HD ** -0.5


class Token:

    def __init__(self, line, k, back=0):
        self.line, self.k, self.back = line, k, back

    @property
    def prev(self):
        return Token(self.line, self.k, 1)


class Late:

    def __init__(self):
        self.tokens = ()


class Line:

    def __init__(self, sem, step, ahead):
        self.sem, self.step, self.ahead, self.n = sem, step, ahead, 0

    def count(self):
        self.n += 1
        return Token(self, self.n)


class Loop:

    ENGINES = ("sync", "tensor", "scalar", "vector", "gpsimd")

    def __init__(self, nc, ctx, name, trips, unused=()):
        self.nc, self.ctx, self.name, self.trips, self.unused = nc, ctx, name, trips, unused
        self.queue = {e: [] for e in self.ENGINES}
        self.before = []
        self.lines = {}
        self.owner = {}
        self.carrier = {e: ctx.enter_context(nc.semaphore(f"{name}_{e}_waits")) for e in self.ENGINES}

    def line(self, name, owner, step):
        if name not in self.lines:
            if owner == "gpsimd" and step == 16:
                sem = self.unused.pop()
            else:
                sem = self.ctx.enter_context(self.nc.semaphore(f"{self.name}_{name}"))
            self.lines[name] = Line(sem, step, not (owner == "gpsimd" and step == 16))
            self.owner[name] = owner
        return self.lines[name]

    def do(self, engine, emit):
        line = self.line(f"{engine}_done", engine, 1)
        self.queue[engine].append(("do", emit, line))
        return line.count()

    def quiet(self, engine, emit):
        self.queue[engine].append(("do", emit, None))

    def dma(self, engine, stream, emit):
        line = self.line(f"dma_{stream}", engine, 16)
        self.queue[engine].append(("do", emit, line))
        return line.count()

    def dma_ahead(self, stream, emit):
        name = f"dma_{stream}"
        if name not in self.lines:
            self.line(name, "gpsimd", 16).ahead = True
        line = self.lines[name]
        self.queue["gpsimd"].append(("next", emit, line))
        self.before.append(("next", emit, line))
        return line.count()

    def wait_ahead(self, token):
        self.queue["gpsimd"].append(("wait", (token,), True))
        self.before.append(("wait", token, None))

    def wait(self, engine, *tokens, alone=None):
        self.queue[engine].append(("wait", tokens, engine in ("sync", "gpsimd") if alone is None else alone))

    def emit(self, block):
        for engine in self.ENGINES:
            getter = {"sync": block.sync, "tensor": block.tensor, "scalar": block.scalar,
                      "vector": block.vector, "gpsimd": block.gpsimd}[engine]
            getter(lambda eng, engine=engine: self.run(engine, eng))

    def run(self, engine, eng):
        for name, line in self.lines.items():
            if self.owner[name] == engine and line.ahead and (engine != "gpsimd" or line.step == 1):
                eng.sem_inc(line.sem, line.n * line.step)
        if engine == "gpsimd":
            for kind, what, line in self.before:
                if kind == "next":
                    what(0).then_inc(line.sem, line.step)
                else:
                    eng.wait_ge(what.line.sem, what.k * what.line.step)
                    eng.sem_inc(self.carrier[engine], 1)
        with eng.Fori(0, self.trips) as i:
            seen = {}
            if engine == "gpsimd" and self.before:
                following = eng.value_load(self.next_trip[0:1, bass.ds(i, 1)], min_val=0, max_val=self.trips - 1)
            for kind, what, line in self.queue[engine]:
                if kind != "wait":
                    ins = what(following if kind == "next" else i)
                    if line is not None:
                        ins.then_inc(line.sem, line.step)
                    continue
                for t in flat(what):
                    assert t.line.ahead or not t.back
                    level = t.k + (t.line.n if t.line.ahead and not t.back else 0)
                    if seen.get(id(t.line), -1) >= level:
                        continue
                    seen[id(t.line)] = level
                    eng.wait_ge(t.line.sem, i * (t.line.n * t.line.step) + level * t.line.step)
                    if line:
                        eng.sem_inc(self.carrier[engine], 1)
        for name, line in self.lines.items():
            if self.owner[name] == engine and name.startswith("dma_"):
                eng.wait_ge(line.sem, (self.trips + line.ahead) * line.n * line.step)


def flat(tokens):
    for t in tokens:
        if isinstance(t, Token):
            yield t
        elif isinstance(t, Late):
            yield from (x.prev for x in flat(t.tokens))
        else:
            yield from flat(t)


class Buffer:

    def __init__(self, ap):
        self.ap, self.ready, self.carried = ap, (), Late()
        self.free = (self.carried,)

    def written(self, *tokens):
        self.ready, self.free = tokens, ()

    def read(self, *tokens):
        self.free += tokens

    def close(self):
        self.carried.tokens = () if self.free == (self.carried,) else self.free


class View:

    def __init__(self, base, ap):
        self.base, self.ap = base, ap

    @property
    def free(self):
        return self.base.free

    @property
    def ready(self):
        return self.base.ready

    def written(self, *tokens):
        self.base.written(*tokens)

    def read(self, *tokens):
        self.base.read(*tokens)


class Ring:

    def __init__(self, aps):
        self.buffers, self.at = [Buffer(ap) for ap in aps], 0

    def next(self):
        self.at += 1
        return self.buffers[(self.at - 1) % len(self.buffers)]


def whole(handle):
    return handle[tuple(slice(None) for _ in handle.shape)]


class Work:

    def __init__(self, nc, ctx, name, loop, tiles, psum_of=None):
        self.nc, self.ctx, self.name, self.loop = nc, ctx, name, loop
        self.nt, self.t = tiles, tiles * P
        self.all = []
        if psum_of is not None:
            self.sc, self.pj = psum_of.sc, psum_of.pj
            self.pv = self.psum("pv", [1])

    def sb(self, name, shape, dt=F32):
        return whole(self.ctx.enter_context(self.nc.sbuf_tensor(f"{self.name}_{name}", shape, dt)))

    def buffer(self, name, shape, dt=F32):
        b = Buffer(self.sb(name, shape, dt))
        self.all.append(b)
        return b

    def ring(self, name, n, shape, dt=F32):
        r = Ring([self.sb(f"{name}{k}", shape, dt) for k in range(n)])
        self.all += r.buffers
        return r

    def psum(self, name, banks, width=512):
        r = Ring([whole(self.ctx.enter_context(self.nc.psum_tensor(f"{self.name}_{name}{k}", [P, b, width], F32)))
                  for k, b in enumerate(banks)])
        self.all += r.buffers
        return r

    def close(self):
        for b in self.all:
            b.close()


def take_turns(first, second, lead):
    ready = [[0.0, 0, first], [lead, 1, second]]
    tensor_free = vector_free = 0.0
    while ready:
        ready.sort(key=lambda c: c[:2])
        try:
            tensor, latency, vector = next(ready[0][2])
        except StopIteration:
            ready.pop(0)
            continue
        start = max(tensor_free, ready[0][0])
        tensor_free = start + tensor
        vector_free = max(vector_free, start) + vector
        ready[0][0] = max(tensor_free, vector_free if vector else 0) + latency


def lane(steps, w, first):
    for b in range(first, NB, LANES):
        yield from steps(w, b)


def to_features(w, x, scale=None, bias=None, engine="scalar"):
    nc, loop = w.nc, w.loop
    dst = w.xt.next()
    loop.wait(engine, dst.free)
    puts = []
    for b in range(w.nt // QT):
        bank = w.pj.next()
        loop.wait("tensor", bank.free, x.ready)
        for k in range(KT):
            for q in range(QT):
                turned = loop.do("tensor", lambda i, b=b, k=k, q=q, bank=bank: nc.tensor.transpose(
                    bank.ap[:, 0, k * S + q * P:k * S + (q + 1) * P], x.ap[:, QT * b + q, k * P:(k + 1) * P], w.identf))
        x.read(turned)
        loop.wait(engine, turned)
        if engine == "vector":
            put = loop.do("vector", lambda i, b=b, bank=bank: nc.vector.tensor_copy(
                dst.ap[:, :, b * S:(b + 1) * S], bank.ap[:, 0, :].rearrange("p (k t) -> p k t", k=KT)))
        elif scale is None:
            put = loop.do("scalar", lambda i, b=b, bank=bank: nc.scalar.activation(
                dst.ap[:, :, b * S:(b + 1) * S], bank.ap[:, 0, :].rearrange("p (k t) -> p k t", k=KT), ACT.Copy))
        else:
            for k in range(KT):
                put = loop.do("scalar", lambda i, b=b, k=k, bank=bank: nc.scalar.activation(
                    dst.ap[:, k, b * S:(b + 1) * S], bank.ap[:, 0, k * S:(k + 1) * S], ACT.Identity,
                    bias=bias[:, k:k + 1], scale=scale[:, k:k + 1]))
        bank.free = (put,)
        puts.append(put)
    dst.written(*puts)
    return dst


def normalise(w, x, out):
    nc, loop = w.nc, w.loop
    st, mv, rs = w.ln_stats, w.ln_moments, w.ln_rstd
    loop.wait("vector", x.ready, st.free)
    for t in range(w.nt):
        got = loop.do("vector", lambda i, t=t: nc.vector.bn_stats(st.ap[:, t, :], x.ap[:, t, :]))
    loop.wait("vector", got, mv.free, alone=True)
    for t in range(w.nt):
        got = loop.do("vector", lambda i, t=t: nc.vector.bn_aggr(mv.ap[:, t, :], st.ap[:, t, :]))
    st.free = (got,)
    loop.wait("gpsimd", got, rs.free)
    e = loop.do("gpsimd", lambda i: nc.gpsimd.tensor_scalar(rs.ap[:, 0, :], mv.ap[:, :, 1], EPS, None, ALU.add))
    loop.wait("gpsimd", e)
    r = loop.do("gpsimd", lambda i: nc.gpsimd.tensor_tensor(rs.ap[:, 1, :], rs.ap[:, 0, :], w.minus_half, ALU.pow))
    yield 0, 3.5, 1
    loop.wait("vector", r, out.free)
    for t in range(w.nt):
        put = loop.do("vector", lambda i, t=t: nc.vector.tensor_scalar(
            out.ap[:, t, :], x.ap[:, t, :], mv.ap[:, t, 0:1], rs.ap[:, 1, t:t + 1], ALU.subtract, ALU.mult))
    x.read(put)
    mv.free = rs.free = (put,)
    out.written(put)
    yield 0, 1.5, 0


def gain_and_shift(w, x, g, b):
    nc, loop = w.nc, w.loop
    over = lambda row: row.unsqueeze(1).broadcast_to([P, w.nt, D])
    loop.wait("gpsimd", x.ready, x.free)
    m = loop.do("gpsimd", lambda i: nc.gpsimd.tensor_tensor(x.ap, x.ap, over(g), ALU.mult))
    loop.wait("gpsimd", m)
    a = loop.do("gpsimd", lambda i: nc.gpsimd.tensor_tensor(x.ap, x.ap, over(b), ALU.add))
    x.written(a)


def project_parts(w, weight, bias, x, n, parts):
    nc, loop = w.nc, w.loop
    rest = w.rest
    loop.wait("scalar", parts.free)
    loop.wait("vector", rest.free)
    bank = w.pj.next()
    loop.wait("tensor", bank.free, x.ready)
    for m in range(KT):
        for k in range(KT):
            mm = loop.do("tensor", lambda i, k=k, m=m: nc.tensor.matmul(
                bank.ap[:, 0, m * n:(m + 1) * n], weight[:, k, m * P:(m + 1) * P], x.ap[:, k, 0:n],
                start=(k == 0), stop=(k == KT - 1)))
    x.read(mm)
    loop.wait("scalar", mm)
    for m in range(KT):
        p1 = loop.do("scalar", lambda i, m=m: nc.scalar.activation(
            parts.ap[:, 0, m, 0:n], bank.ap[:, 0, m * n:(m + 1) * n], ACT.Identity, bias=bias[:, m:m + 1]))
    loop.wait("vector", p1)
    for m in range(KT):
        r1 = loop.do("vector", lambda i, m=m: nc.vector.scalar_tensor_tensor(
            rest.ap[:, m, 0:n], bank.ap[:, 0, m * n:(m + 1) * n], bias[:, m:m + 1], parts.ap[:, 0, m, 0:n],
            ALU.add, ALU.subtract))
    bank.free = (r1,)
    loop.wait("scalar", r1)
    p2 = loop.do("scalar", lambda i: nc.scalar.activation(parts.ap[:, 1, :, 0:n], rest.ap[:, :, 0:n], ACT.Copy))
    loop.wait("vector", p2)
    p3 = loop.do("vector", lambda i: nc.vector.tensor_tensor(
        parts.ap[:, 2, :, 0:n], rest.ap[:, :, 0:n], parts.ap[:, 1, :, 0:n], ALU.subtract))
    rest.free = (p3,)
    parts.each = (p1, p2, p3)
    parts.written(p3)


def send_parts(w, parts, scratch, n, name):
    nc, loop = w.nc, w.loop
    put_v = scratch.ap[:, 0:D * n].rearrange("s (m p t) -> s p m t", m=KT, p=P)
    loop.wait("sync", scratch.free)
    sent = []
    for s in range(NPART):
        loop.wait("sync", parts.each[s])
        sent.append(loop.dma("sync", f"{w.name}_{name}_out{s}", lambda i, s=s: nc.sync.dma_start(
            put_v[s], parts.ap[:, s, :, 0:n])))
    parts.read(*sent)
    scratch.each = sent
    scratch.written(*sent)


def stack_parts(w, scratch, stacked, n, runs, name):
    nc, loop = w.nc, w.loop
    get_v = scratch.ap[:, 0:D * n].rearrange("s (d x) -> s d x", d=HD)
    loop.wait("sync", stacked.free)
    for first, count, same in runs:
        rows = slice(first * HD, (first + count) * HD)
        if same is None:
            src, last = get_v[0:count], count - 1
        else:
            src, last = get_v[same:same + 1].broadcast_to([count, HD, H * n]), same
        loop.wait("sync", scratch.each[last])
        back = loop.dma("sync", f"{w.name}_{name}_in", lambda i, rows=rows, src=src: nc.sync.dma_start(
            stacked.ap[rows].rearrange("r h t -> r (h t)"), src))
    scratch.free = (back,)
    stacked.written(back)


Q_RUNS = [(0, 3, 0), (3, 2, 1), (5, 1, 2)]
K_RUNS = [(5, 1, None), (3, 2, None), (0, 3, None)]


def project_values(w, weight, x, tiles, values):
    nc, loop = w.nc, w.loop
    bank = w.pj.next()
    loop.wait("tensor", bank.free, x.ready)
    for j, (at, keys) in enumerate(tiles):
        for k in range(KT):
            mm = loop.do("tensor", lambda i, j=j, at=at, keys=keys, k=k: nc.tensor.matmul(
                bank.ap[0:keys, 0, j * D:(j + 1) * D], x.ap[:, k, at:at + keys], weight[:, k, :],
                start=(k == 0), stop=(k == KT - 1)))
    x.read(mm)
    loop.wait("vector", values.free, mm)
    n, keys = len(tiles), tiles[0][1]
    put = loop.do("vector", lambda i: nc.vector.tensor_copy(
        values.ap[0:keys, 0:n, :, 0:HD],
        bank.ap[0:keys, 0, 0:n * D].rearrange("p (t h d) -> p t h d", h=H, d=HD)))
    bank.free = (put,)
    values.written(put)


def attend(w, qs, ks, values, n, causal, mask, heads_t, bv):
    nc, loop = w.nc, w.loop
    G = 2
    key_tiles = -(-n // P)
    maxima = w.maxima
    loop.wait("vector", maxima.free)

    def add_mask(ap, m):
        return loop.do("tensor", lambda i: nc.tensor.matmul(ap, w.identb, m, start=False, stop=True))

    def query_major(hp):
        bank = w.sc.next()
        loop.wait("tensor", bank.free, qs.ready, ks.ready)
        for j in range(G):
            h = G * hp + j
            off = 0
            for q in range(QT):
                m = P * (q + 1) if causal else n
                mm = loop.do("tensor", lambda i, j=j, h=h, q=q, m=m, off=off: nc.tensor.matmul(
                    bank.ap[:, j, off:off + m], qs.ap[0:STACK, h, q * P:(q + 1) * P],
                    ks.ap[0:STACK, h, 0:m], start=True, stop=(mask is None)))
                if mask is not None:
                    mo, mw = (off + q * P, P) if causal else (off, n)
                    mm = add_mask(bank.ap[:, j, mo:mo + mw], mask[0][:, q, :])
                off += m
        loop.wait("vector", mm)
        heads = slice(G * hp, G * (hp + 1))
        if causal:
            off = 0
            for q in range(QT):
                m = P * (q + 1)
                r = loop.do("vector", lambda i, q=q, m=m, off=off: nc.vector.tensor_reduce(
                    maxima.ap[:, q, heads], bank.ap[:, :, off:off + m], AX.X, ALU.max))
                off += m
        else:
            r = loop.do("vector", lambda i: nc.vector.tensor_reduce(
                maxima.ap[:, :, heads].rearrange("p q h -> p h q"),
                bank.ap[:, :, 0:QT * n].rearrange("p j (q n) -> p j q n", q=QT), AX.X, ALU.max))
        bank.free = (r,)
        return r

    def shift_rows(got_max):
        bank = w.pj.next()
        loop.wait("tensor", bank.free, got_max)
        for q in range(QT):
            tr = loop.do("tensor", lambda i, q=q: nc.tensor.transpose(
                bank.ap[0:H, 0, q * P:(q + 1) * P], maxima.ap[:, q, :], w.identf))
        maxima.free = (tr,)
        nm, rest = w.shift, w.rest.ap[0:H, 0, :]
        src = bank.ap[0:H, 0, 0:S]
        loop.wait("scalar", tr, nm.free)
        p1 = loop.do("scalar", lambda i: nc.scalar.mul(nm.ap[:, 0, :], src, -1.0))
        loop.wait("vector", p1, w.rest.free)
        r1 = loop.do("vector", lambda i: nc.vector.scalar_tensor_tensor(
            rest, src, -1.0, nm.ap[:, 0, :], ALU.mult, ALU.subtract))
        bank.free = (r1,)
        loop.wait("vector", r1)
        p2 = loop.do("vector", lambda i: nc.vector.tensor_copy(nm.ap[:, 1, :], rest))
        loop.wait("vector", p2)
        p3 = loop.do("vector", lambda i: nc.vector.tensor_tensor(nm.ap[:, 2, :], rest, nm.ap[:, 1, :], ALU.subtract))
        w.rest.free = (p3,)
        for s in range(NPART):
            loop.wait("sync", (p1, p2, p3)[s])
            back = loop.dma("sync", f"{w.name}_shift_in", lambda i, s=s: nc.sync.dma_start(
                qs.ap[STACK + s:STACK + s + 1, :, :], nm.ap[:, s, :]))
        nm.free = (back,)
        return back

    spans = []
    width = 0
    for kt in range(key_tiles):
        q0 = kt * P if causal else 0
        spans.append((min(P, n - kt * P), q0, S - q0, width))
        width += S - q0
    rows = min(P, n)

    def key_major(g, shifted):
        pr = w.prob.next()
        for hp in range(2):
            bank = w.sc.next()
            loop.wait("tensor", bank.free, shifted)
            for j in range(G):
                h = 4 * g + G * hp + j
                for kt, (kn, q0, qn, at) in enumerate(spans):
                    mm = loop.do("tensor", lambda i, bank=bank, j=j, h=h, kt=kt, kn=kn, q0=q0, qn=qn, at=at: nc.tensor.matmul(
                        bank.ap[0:kn, j, at:at + qn], ks.ap[0:STACK + NPART, h, kt * P:kt * P + kn],
                        qs.ap[0:STACK + NPART, h, q0:q0 + qn], start=True, stop=(mask is None)))
                    if mask is not None:
                        mn = P if causal else qn
                        mm = add_mask(bank.ap[:, j, at:at + mn], mask[1][:, kt, :])
            loop.wait("scalar", mm, pr.free)
            ex = loop.do("scalar", lambda i, hp=hp, bank=bank: nc.scalar.activation(
                pr.ap[0:rows, G * hp:G * (hp + 1), 0:width], bank.ap[0:rows, :, 0:width], ACT.Exp, scale=SCALE))
            bank.free = (ex,)
        pr.written(ex)
        return pr, mm

    def weigh_values(g, pr, o_bank):
        loop.wait("tensor", pr.ready, values.ready, o_bank.free)
        base = (g % 2) * S
        for kt, (kn, q0, qn, at) in enumerate(spans):
            for j in range(4):
                mm = loop.do("tensor", lambda i, j=j, kt=kt, kn=kn, q0=q0, qn=qn, at=at: nc.tensor.matmul(
                    o_bank.ap[32 * j:32 * j + 32, 0, base + q0:base + S],
                    values.ap[0:kn, kt, 4 * g + j, :], pr.ap[0:kn, j, at:at + qn],
                    start=(kt == 0), stop=(kt == key_tiles - 1), tile_position=(0, 32 * j)))
        pr.free = (mm,)
        return mm

    for hp in range(H // G):
        got_max = query_major(hp)
        yield (1.0, 0, 1.3) if n > P else (0.5, 0.1, 0.9)
    shifted = shift_rows(got_max)
    yield 0.4, SHIFT, 0
    pending, raws = None, []
    for g in range(H // 4 + 1):
        if g < H // 4:
            pr, scored = key_major(g, shifted)
            yield (2.0, 0, 0) if n > P else (0.9, 0.7, 0)
        if pending is not None:
            if (g - 1) % 2 == 0:
                o_bank = w.pv.next()
            mm = weigh_values(g - 1, pending, o_bank)
            if (g - 1) % 2 == 1:
                raw = w.raw.next()
                loop.wait("vector", mm, raw.free)
                ev = loop.do("vector", lambda i, raw=raw, o_bank=o_bank: nc.vector.tensor_copy(
                    raw.ap, o_bank.ap[:, 0, :]))
                raw.written(ev)
                o_bank.free = (ev,)
                raws.append(raw)
            yield 0.8, 0, 0
        pending = pr
    qs.free = ks.free = (scored,)
    values.free = (mm,)
    yield 0, 1, 0
    normed = w.normed
    loop.wait("vector", normed.free)
    for q in range(QT):
        bank = w.pv.next()
        loop.wait("tensor", bank.free)
        for g in range(H // 4):
            loop.wait("tensor", raws[g // 2].ready)
            tr = loop.do("tensor", lambda i, g=g, q=q, bank=bank, raw=raws[g // 2]: nc.tensor.transpose(
                bank.ap[:, 0, g * P:(g + 1) * P],
                raw.ap[:, (g % 2) * S + q * P:(g % 2) * S + (q + 1) * P], w.identf))
        loop.wait("vector", tr)
        per_head = bank.ap[:, 0, :].rearrange("p (h c) -> p h c", c=32)
        rc = loop.do("vector", lambda i, q=q, per_head=per_head: nc.vector.reciprocal(
            w.recip[:, q, :], per_head[:, :, HD]))
        loop.wait("vector", rc)
        mu = loop.do("vector", lambda i, per_head=per_head, q=q: nc.vector.tensor_tensor(
            normed.ap[:, q, :].rearrange("p (h c) -> p h c", c=HD), per_head[:, :, 0:HD],
            w.recip[:, q, :].unsqueeze(2).broadcast_to([P, H, HD]), ALU.mult))
        bank.free = (mu,)
    for raw in raws:
        raw.free = (tr,)
    yield 1.7, 1.3, 0
    bank = w.pj.next()
    loop.wait("tensor", bank.free, mu)
    for q in range(QT):
        for k in range(KT):
            tr = loop.do("tensor", lambda i, q=q, k=k, bank=bank: nc.tensor.transpose(
                bank.ap[:, 0, k * S + q * P:k * S + (q + 1) * P], normed.ap[:, q, k * P:(k + 1) * P], w.identf))
    normed.free = (tr,)
    loop.wait("scalar", tr, heads_t.free)
    for k in range(KT):
        put = loop.do("scalar", lambda i, k=k, bank=bank: nc.scalar.activation(
            heads_t.ap[:, k, :], bank.ap[:, 0, k * S:(k + 1) * S], ACT.Identity, bias=bv[:, k:k + 1]))
    bank.free = (put,)
    heads_t.written(put)
    yield 0.9, 1.3, 0


def project_out(w, weight, heads_t, residual, x):
    nc, loop = w.nc, w.loop
    kt = heads_t.ap.shape[1]
    loop.wait("vector", residual.ready, x.free)
    for a in range(0, w.nt, 2):
        bank = w.pj.next()
        loop.wait("tensor", bank.free, heads_t.ready)
        for j in range(2):
            for k in range(kt):
                mm = loop.do("tensor", lambda i, a=a, j=j, k=k, bank=bank: nc.tensor.matmul(
                    bank.ap[:, 0, j * D:(j + 1) * D], heads_t.ap[:, k, (a + j) * P:(a + j + 1) * P],
                    weight[:, k, :], start=(k == 0), stop=(k == kt - 1)))
        loop.wait("vector", mm)
        put = loop.do("vector", lambda i, a=a, bank=bank: nc.vector.tensor_tensor(
            x.ap[:, a:a + 2, :], bank.ap[:, 0, :].rearrange("p (t n) -> p t n", t=2),
            residual.ap[:, a:a + 2, :], ALU.add))
        bank.free = (put,)
    heads_t.read(mm)
    residual.read(put)
    x.written(put)
    yield 0.85 * kt, 0.3, 0


def add_bias(w, x, row, out):
    nc, loop = w.nc, w.loop
    loop.wait("gpsimd", x.ready, out.free)
    put = loop.do("gpsimd", lambda i: nc.gpsimd.tensor_tensor(
        out.ap, x.ap, row.unsqueeze(1).broadcast_to([P, w.nt, D]), ALU.add))
    x.read(put)
    out.written(put)


def feed_forward(w, w1, b1, w2, xt, residual, x):
    nc, loop = w.nc, w.loop
    hid = w.hidden
    loop.wait("scalar", hid.free)
    for f0 in range(0, FT, 2):
        bank = w.pj.next()
        loop.wait("tensor", bank.free, xt.ready)
        for f in (f0, f0 + 1):
            for k in range(KT):
                mm = loop.do("tensor", lambda i, f=f, k=k, bank=bank: nc.tensor.matmul(
                    bank.ap[:, 0, (f % 2) * S:(f % 2 + 1) * S], w1[:, k, f * P:(f + 1) * P], xt.ap[:, k, :],
                    start=(k == 0), stop=(k == KT - 1)))
        loop.wait("scalar", mm)
        for f in (f0, f0 + 1):
            put = loop.do("scalar", lambda i, f=f, bank=bank: nc.scalar.activation(
                hid.ap[:, f, :], bank.ap[:, 0, (f % 2) * S:(f % 2 + 1) * S], ACT.Relu, bias=b1[:, f:f + 1]))
        bank.free = (put,)
        yield 1.7, 0, 0
    xt.read(mm)
    hid.written(put)
    yield from project_out(w, w2, hid, residual, x)


def route(w, rw, rb, xt, pick):
    nc, loop = w.nc, w.loop
    r = w.route
    bank = w.pj.next()
    loop.wait("tensor", bank.free, xt.ready)
    for t in range(w.nt):
        for k in range(KT):
            mm = loop.do("tensor", lambda i, t=t, k=k: nc.tensor.matmul(
                bank.ap[:, 0, t * E:(t + 1) * E], xt.ap[:, k, t * P:(t + 1) * P], rw[:, k, :],
                start=(k == 0), stop=(k == KT - 1)))
    xt.read(mm)
    logit, prob = r["logit"], r["prob"]
    per_tile = lambda a: a.unsqueeze(2).broadcast_to([P, w.nt, E])

    def v(emit, *waits):
        loop.wait("vector", *waits)
        return loop.do("vector", emit)
    a = v(lambda i: nc.vector.tensor_tensor(
        logit, bank.ap[:, 0, 0:w.nt * E].rearrange("p (t e) -> p t e", e=E),
        rb.unsqueeze(1).broadcast_to([P, w.nt, E]), ALU.add), mm)
    bank.free = (a,)
    a = v(lambda i: nc.vector.tensor_reduce(r["max"], logit, AX.X, ALU.max), a)
    a = v(lambda i: nc.vector.tensor_tensor(logit, logit, per_tile(r["max"]), ALU.subtract), a)
    loop.wait("scalar", a)
    e = loop.do("scalar", lambda i: nc.scalar.activation(prob, logit, ACT.Exp))
    yield 0.5, 3, 0
    a = v(lambda i: nc.vector.tensor_reduce(r["sum"], prob, AX.X, ALU.add), e)
    a = v(lambda i: nc.vector.reciprocal(r["rsum"], r["sum"]), a)
    a = v(lambda i: nc.vector.tensor_tensor(prob, prob, per_tile(r["rsum"]), ALU.mult), a)
    loop.wait("vector", a, alone=True)
    for t in range(w.nt):
        top = loop.do("vector", lambda i, t=t: nc.vector.max(r["top"][:, t, :], prob[:, t, :]))
    loop.wait("vector", top, alone=True)
    for t in range(w.nt):
        at = loop.do("vector", lambda i, t=t: nc.vector.max_index(r["at"][:, t, :], r["top"][:, t, :], prob[:, t, :]))
    d = v(lambda i: nc.vector.tensor_tensor(r["gap"], r["top"][:, :, 1], r["top"][:, :, 0], ALU.subtract))
    v(lambda i: nc.vector.tensor_copy(pick.ap[:, :, 0:2], r["at"][:, :, 0:2]), at, pick.free)
    loop.wait("scalar", d)
    e = loop.do("scalar", lambda i: nc.scalar.activation(r["e2"], r["gap"], ACT.Exp))
    yield 0, 4, 0
    a = v(lambda i: nc.vector.tensor_scalar(r["one_e2"], r["e2"], 1.0, None, ALU.add), e)
    a = v(lambda i: nc.vector.reciprocal(pick.ap[:, :, 2], r["one_e2"]), a)
    a = v(lambda i: nc.vector.tensor_tensor(pick.ap[:, :, 3], r["e2"], pick.ap[:, :, 2], ALU.mult), a)
    pick.written(a)


def chain(engine, sem):
    count = [0]

    def link(ins):
        count[0] += 1
        ins.then_inc(sem, 1)
        engine.wait_ge(sem, count[0])
    return link


def place_pairs(nc, ctx, a, pick_dram, rows_dram, owner_dram, x_dram, sorted_dram, x_loaded, sent):
    def sb(name, shape, dt=F32):
        return whole(ctx.enter_context(nc.sbuf_tensor("place_" + name, shape, dt)))

    n_tiles = B * QT
    many = n_tiles // 2
    x = sb("x", [P, many, D])
    x_v = x_dram.rearrange("(i m) (q p) d -> i p (m q) d", m=many // QT, p=P)
    here = sb("here", [P, many, 2], U32)
    pick = sb("pick", [P, n_tiles, 4])
    before, ones = sb("before", [P, P]), sb("ones", [P, P])
    iota_e, steps = sb("iota_e", [P, E]), sb("steps", [P, S // 16])
    group_no = sb("group_no", [1, GROUPS])
    chosen = [sb(f"chosen{k}", [P, n_tiles, E]) for k in range(2)]
    member = sb("member", [P, n_tiles, E])
    total, row = sb("total", [P, n_tiles, E]), sb("row", [P, n_tiles, E])
    scan = [sb(f"scan{k}", [P, n_tiles, E]) for k in range(2)]
    over = sb("over", [P, E, S // 16])
    groups, base = sb("groups", [P, E]), sb("base", [P, E])
    ends = [sb(f"ends{k}", [P, E]) for k in range(2)]
    hit = sb("hit", [P, n_tiles, E])
    rows_f, rows_u = sb("rows_f", [P, n_tiles, 2]), sb("rows_u", [P, n_tiles, 2], U32)
    passed = sb("passed", [1, GROUPS, E - 1])
    owner_f, owner_i = sb("owner_f", [1, GROUPS]), sb("owner_i", [1, GROUPS], I32)
    within = whole(ctx.enter_context(nc.psum_tensor("place_within", [P, n_tiles * E], F32)))
    sums = whole(ctx.enter_context(nc.psum_tensor("place_sums", [P, n_tiles * E], F32)))
    by_tile = lambda ap: ap.rearrange("p (t e) -> p t e", e=E)
    with nc.semaphore("place_loaded") as loaded, nc.semaphore("place_member") as member_done, \
            nc.semaphore("place_summed") as summed, nc.semaphore("place_chain") as steps_done, \
            nc.semaphore("place_rows") as rows_done, \
            nc.semaphore("place_waits") as waits, nc.semaphore("place_x_waits") as x_waits, nc.Block() as block:
        @block.sync
        def _(eng):
            loads = [(pick.rearrange("p (n q) c -> p n (q c)", q=QT), pick_dram.rearrange("n p q c -> p n (q c)")),
                     (before, a["before"]), (ones, a["ones"]), (iota_e, a["iota"].partition_broadcast(P)),
                     (steps, a["steps"].partition_broadcast(P)), (group_no, a["group_no"].partition_broadcast(1))]
            for dst, src in loads:
                eng.dma_start(dst, src).then_inc(loaded, 16)
            eng.wait_ge(rows_done, 1)
            eng.dma_start(rows_dram.rearrange("t p s -> p t s"), rows_u).then_inc(loaded, 16)
            eng.dma_start(owner_dram, owner_i).then_inc(loaded, 16)
            eng.wait_ge(loaded, 16 * (len(loads) + 2))

        @block.gpsimd
        def _(eng):
            eng.wait_ge(rows_done, 1)
            with eng.Fori(0, n_tiles // many) as i:
                eng.dma_start(x, x_v[i]).then_inc(x_loaded, 16)
                eng.tensor_copy(here, rows_u[:, bass.ds(i * many, many), :]).then_inc(waits, 1)
                eng.wait_ge(waits, i * 2 + 1)
                eng.sem_inc(waits, 1)
                eng.wait_ge(x_loaded, (i + 1) * 16)
                eng.sem_inc(x_waits, 1)
                for t in range(many):
                    for k in range(2):
                        eng.indirect_dma_start(
                            sorted_dram, bass.IndirectOffsetOnAxis(ap=here[:, t, k:k + 1], axis=0),
                            x[:, t, :], None).then_inc(sent, 16)
                eng.wait_ge(sent, (i + 1) * (32 * many))

        @block.tensor
        def _(eng):
            eng.wait_ge(member_done, 1)
            eng.matmul(within, before, member.rearrange("p t e -> p (t e)"), start=True, stop=True)
            eng.matmul(sums, ones, member.rearrange("p t e -> p (t e)"), start=True, stop=True).then_inc(summed, 1)

        @block.vector
        def _(eng):
            link = chain(eng, steps_done)
            eng.wait_ge(loaded, 16 * 6)
            for k in range(2):
                link(eng.tensor_tensor(chosen[k], iota_e.unsqueeze(1).broadcast_to([P, n_tiles, E]),
                                       pick[:, :, k:k + 1].broadcast_to([P, n_tiles, E]), ALU.is_equal))
            eng.tensor_tensor(member, chosen[0], chosen[1], ALU.add).then_inc(member_done, 1)
            eng.wait_ge(summed, 1)
            link(eng.tensor_copy(total, by_tile(sums)))
            link(eng.tensor_copy(scan[0], total))
            at, stride = 0, 1
            while stride < n_tiles:
                x, y = scan[at], scan[1 - at]
                link(eng.tensor_copy(y[:, 0:stride, :], x[:, 0:stride, :]))
                link(eng.tensor_tensor(y[:, stride:n_tiles, :], x[:, stride:n_tiles, :],
                                       x[:, 0:n_tiles - stride, :], ALU.add))
                at, stride = 1 - at, 2 * stride
            upto = scan[at]
            link(eng.tensor_tensor(over, upto[:, n_tiles - 1, :].unsqueeze(2).broadcast_to([P, E, S // 16]),
                                   steps.unsqueeze(1).broadcast_to([P, E, S // 16]), ALU.is_gt))
            link(eng.tensor_reduce(groups, over, AX.X, ALU.add))
            link(eng.tensor_copy(ends[0], groups))
            last, stride = 0, 1
            while stride < E:
                x, y = ends[last], ends[1 - last]
                link(eng.tensor_copy(y[:, 0:stride], x[:, 0:stride]))
                link(eng.tensor_tensor(y[:, stride:E], x[:, stride:E], x[:, 0:E - stride], ALU.add))
                last, stride = 1 - last, 2 * stride
            end = ends[last]
            link(eng.tensor_tensor(base, end, groups, ALU.subtract))
            link(eng.tensor_scalar(base, base, float(GROUP), None, ALU.mult))
            link(eng.tensor_tensor(row, upto, total, ALU.subtract))
            link(eng.tensor_tensor(row, row, base.unsqueeze(1).broadcast_to([P, n_tiles, E]), ALU.add))
            link(eng.tensor_tensor(row, by_tile(within), row, ALU.add))
            for k in range(2):
                link(eng.tensor_tensor(hit, chosen[k], row, ALU.mult))
                link(eng.tensor_reduce(rows_f[:, :, k], hit, AX.X, ALU.add))
            link(eng.tensor_copy(rows_u, rows_f))
            link(eng.tensor_tensor(passed, end[0:1, 0:E - 1].unsqueeze(1).broadcast_to([1, GROUPS, E - 1]),
                                   group_no.unsqueeze(2).broadcast_to([1, GROUPS, E - 1]), ALU.is_le))
            link(eng.tensor_reduce(owner_f, passed, AX.X, ALU.add))
            eng.tensor_copy(owner_i, owner_f).then_inc(rows_done, 1)


class Constants:

    def __init__(self, nc, ctx, name):
        self.nc, self.ctx, self.name, self.loads, self.fills = nc, ctx, name, [], []

    def sb(self, name, shape, dt=F32):
        return whole(self.ctx.enter_context(self.nc.sbuf_tensor(f"{self.name}_{name}", shape, dt)))

    def weight(self, name, src):
        rows, cols = src.shape
        t = self.sb(name, [P, rows // P, cols])
        self.loads.append((t[:, :, :], src.rearrange("(k p) n -> p k n", p=P)))
        return t

    def load(self, name, shape, src, dt=F32):
        t = self.sb(name, shape, dt)
        self.loads.append((t[tuple(slice(None) for _ in shape)], src))
        return t

    def fill(self, ap, value):
        self.fills.append((ap, value))

    def start(self, loaded):
        self.loaded = loaded
        with self.nc.Block() as block:
            @block.sync
            def _(eng):
                for dst, src in self.loads:
                    eng.dma_start(dst, src).then_inc(loaded, 16)

    def finish(self):
        with self.nc.Block() as block:
            block.sync(lambda eng: eng.wait_ge(self.loaded, 16 * len(self.loads)))

    def emit(self):
        nc = self.nc
        loaded, filled, filled_too = [self.ctx.enter_context(nc.semaphore(f"{self.name}_{n}"))
                                      for n in ("loaded", "filled", "filled_too")]
        with nc.Block() as block:
            @block.sync
            def _(eng):
                for dst, src in self.loads:
                    eng.dma_start(dst, src).then_inc(loaded, 16)
                eng.wait_ge(loaded, 16 * len(self.loads))

            for engine, done, fills in ((block.gpsimd, filled, self.fills[::2]), (block.vector, filled_too, self.fills[1::2])):
                def fill(eng, done=done, fills=fills):
                    for k, (ap, value) in enumerate(fills):
                        eng.memset(ap, value).then_inc(done, 1)
                        eng.wait_ge(done, k + 1)
                engine(fill)


def common_psum(w):
    w.sc = w.psum("scores", [2, 2])
    w.pj = w.psum("project", [1, 1])


def attention_buffers(w, c, dram, width):
    w.tok = w.ring("tok", 4, [P, QT, D])
    w.xt = w.ring("xt", 1, [P, KT, S])
    w.parts_q = w.buffer("parts_q", [P, NPART, KT, S], BF16)
    w.parts_k = w.buffer("parts_k", [P, NPART, KT, S], BF16)
    w.rest = w.buffer("rest", [P, KT, S])
    w.qs = w.buffer("qs", [P, H, S], BF16)
    w.hidden = View(w.qs, w.qs.ap.rearrange("p h t -> p (h t)").bitcast(F32).rearrange("p (f t) -> p f t", t=S))
    w.ks = w.buffer("ks", [STACK + NPART, H, S], BF16)
    w.values = w.buffer("values", [P, QT, H, 32])
    w.ctx_ks = w.buffer("ctx_ks", [STACK + NPART, H, C], BF16)
    w.ctx_values = w.buffer("ctx_values", [C, 1, H, 32])
    w.maxima = w.buffer("maxima", [P, QT, H])
    w.shift = w.buffer("shift", [H, NPART, S], BF16)
    w.prob = w.ring("prob", 2, [P, 4, width])
    w.raw = w.ring("raw", 2, [P, 2 * S])
    w.normed = w.buffer("normed", [P, QT, D])
    w.recip = w.sb("recip", [P, QT, H])
    w.heads_t = w.buffer("heads_t", [P, KT, S])
    w.ctx_t = w.buffer("ctx_t", [P, KT, C])
    w.loaded = w.buffer("loaded", [P, QT, D])
    norm_buffers(w)
    w.q_dram, w.k_dram, w.c_dram = [Buffer(dram[n]) for n in ("q", "k", "c")]
    w.all += [w.q_dram, w.k_dram, w.c_dram]
    for values, ks in ((w.values, w.ks), (w.ctx_values, w.ctx_ks)):
        c.fill(values.ap[:, :, :, HD:HD + 1], 1.0)
        c.fill(values.ap[:, :, :, HD + 1:32], 0.0)
        c.fill(ks.ap[STACK:STACK + NPART, :, :], 1.0)


def norm_buffers(w):
    w.ln_stats = w.buffer("ln_stats", [P, w.nt, 6])
    w.ln_moments = w.buffer("ln_moments", [P, w.nt, 2])
    w.ln_rstd = w.buffer("ln_rstd", [P, 2, w.nt])


def self_attention(w, wt, xt, mask, causal, heads_t, meanwhile):
    q_bias, k_bias, v_bias = wt["biases"]
    project_parts(w, wt["q"], q_bias, xt, S, w.parts_q)
    send_parts(w, w.parts_q, w.q_dram, S, "q")
    yield 1.7, 0, 1.4
    project_parts(w, wt["k"], k_bias, xt, S, w.parts_k)
    send_parts(w, w.parts_k, w.k_dram, S, "k")
    stack_parts(w, w.q_dram, w.qs, S, Q_RUNS, "q")
    stack_parts(w, w.k_dram, w.ks, S, K_RUNS, "k")
    yield 1.7, 0, 1.4
    project_values(w, wt["v"], xt, [(t * P, P) for t in range(QT)], w.values)
    yield 1.7, 0, 0
    meanwhile()
    yield 1.6, STACK_SELF, 0
    yield from attend(w, w.qs, w.ks, w.values, S, causal, mask, heads_t, v_bias)


def context_operands(w, wt):
    project_parts(w, wt["k"], wt["biases"][1], w.ctx_t, C, w.parts_k)
    send_parts(w, w.parts_k, w.c_dram, C, "c")
    project_values(w, wt["v"], w.ctx_t, [(0, C)], w.ctx_values)
    stack_parts(w, w.c_dram, w.ctx_ks, C, K_RUNS, "c")


def cross_attention(w, wt, xt, heads_t):
    q_bias, _, v_bias = wt["biases"]
    project_parts(w, wt["q"], q_bias, xt, S, w.parts_q)
    send_parts(w, w.parts_q, w.q_dram, S, "q")
    stack_parts(w, w.q_dram, w.qs, S, Q_RUNS, "q")
    yield 1.7, STACK_CROSS, 0
    yield from attend(w, w.qs, w.ctx_ks, w.ctx_values, C, False, None, heads_t, v_bias)


def attention_layer(w, wt, kind, xt, x, mask=None, causal=False, meanwhile=None):
    if wt["out_bias"] is not None:
        residual = w.tok.next()
        add_bias(w, x, wt["out_bias"], residual)
    else:
        residual = x
    if kind == "self":
        yield from self_attention(w, wt, xt, mask, causal, w.heads_t, meanwhile)
    else:
        yield from cross_attention(w, wt, xt, w.heads_t)
    out = w.tok.next()
    yield from project_out(w, wt["o"], w.heads_t, residual, out)
    return out


def pre_norm(w, x, gain, shift):
    xn = w.tok.next()
    yield from normalise(w, x, xn)
    xt = to_features(w, xn, gain, shift)
    yield 0.9, 1.2, 0
    return xt


def post_norm_into(w, x, out, gain, shift):
    yield from normalise(w, x, out)
    gain_and_shift(w, out, gain, shift)
    yield 0, 2, 0


def post_norm(w, x, gain, shift):
    out = w.tok.next()
    yield from post_norm_into(w, x, out, gain, shift)
    return out


def fetch(w, buf, stream, ahead, emit):
    loop = w.loop
    loop.wait("gpsimd", buf.free)
    if ahead:
        buf.written(loop.dma_ahead(f"{w.name}_{stream}_ahead", emit))
        buf.first.tokens = buf.ready
    else:
        buf.written(loop.dma("gpsimd", f"{w.name}_{stream}", emit))


def loaded_ahead(buf):
    buf.first = Late()
    buf.ready = (buf.first,)


def next_sequence(b):
    return (b + LANES, False) if b + LANES < NB else (b % LANES, True)


def fetch_tokens(w, src, b):
    at, ahead = next_sequence(b)
    fetch(w, w.loaded, "x", ahead, lambda i: w.nc.gpsimd.dma_start(w.loaded.ap, src(at)(i)))


def fetch_context(w, ctx_t, b):
    at, ahead = next_sequence(b)
    fetch(w, w.ctx_t, "ctx", ahead, lambda i: w.nc.gpsimd.dma_start(w.ctx_t.ap, ctx_t(at)(i)))


def store(w, x, dst, name):
    nc, loop = w.nc, w.loop
    loop.wait("sync", x.ready)
    x.read(loop.dma("sync", f"{w.name}_{name}", lambda i: nc.sync.dma_start(dst(i), x.ap)))


def sequence(ap, b):
    v = ap.rearrange("(i b) (q p) d -> i b p q d", b=NB, p=P)
    return lambda i: v[i, b]


def build(nc, a, out):
    with ExitStack() as program:
        build_phases(nc, a, out, program)


def build_phases(nc, a, out, program):
    def scratch(name, shape, dt=F32):
        return nc.dram_tensor(name, shape, dt, kind="Internal").ap()

    unused = [program.enter_context(nc.semaphore(f"gpsimd_dma{k}")) for k in range(30)]
    x1 = scratch("x_moe_in", [B, S, D])
    pick_dram = scratch("pick", [B, P, QT, 4])
    rows_dram = scratch("pair_rows", [B * QT, P, 2], U32)
    owner_dram = scratch("group_expert", [1, GROUPS], I32)
    sorted_dram = scratch("sorted_in", [GROUPS * GROUP, D])
    result_dram = scratch("sorted_out", [GROUPS * GROUP, D])
    dram = [{"q": scratch(f"q_parts{b}", [NPART, D * S], BF16), "k": scratch(f"k_parts{b}", [NPART, D * S], BF16),
             "c": scratch(f"ctx_k_parts{b}", [NPART, D * C], BF16)} for b in range(LANES)]
    ctx_v = a["ctx_t"].rearrange("(k p) (i b t) -> i b p k t", p=P, b=NB, t=C)
    ctx_t = lambda b: lambda i: ctx_v[i, b]
    cols, rows = a["columns"], a["rows"]

    def common(c):
        packed = c.load("columns", [P, len(COLUMNS)], cols)
        column = lambda name: packed[:, COLUMNS.index((name, 0)):COLUMNS.index((name, 0)) + sum(n == name for n, _ in COLUMNS)]
        identf = c.load("identity", [P, P], a["identity"])
        return column, identf

    def row(c, name):
        r = c.load("row_" + name, [P, D], rows[ROWS.index(name)].partition_broadcast(P))
        return r[:, :]

    def attention_weights(c, column, layer, at, names, bias_names, out_bias):
        wt = {k: c.weight(f"{layer}_{at}_{k}", a[n]) for k, n in zip("qkvo", names)}
        wt["biases"] = [column(n) for n in bias_names]
        wt["out_bias"] = row(c, out_bias) if out_bias else None
        return wt

    def attention_works(ctx, c, loop, identf, name, width):
        shared = Work(nc, ctx, name, loop, QT)
        common_psum(shared)
        loop.next_trip = c.load("next_trip", [1, TRIPS], a["next_trip"].partition_broadcast(1), I32)
        minus_half = c.sb("minus_half", [P, QT])[:, :]
        c.fill(minus_half, -0.5)
        identb = c.sb("identb", [P, P], BF16)[:, :]
        works = []
        for b in range(LANES):
            w = Work(nc, ctx, f"{name}{b}", loop, QT, psum_of=shared)
            w.identf, w.identb, w.minus_half = identf[:, :], identb, minus_half
            attention_buffers(w, c, dram[b], width)
            loaded_ahead(w.loaded)
            loaded_ahead(w.ctx_t)
            works.append(w)
        return shared, works

    with ExitStack() as ctx:
        c = Constants(nc, ctx, "a_const")
        column, identf = common(c)
        loop = Loop(nc, ctx, "a", TRIPS, unused)
        shared, works = attention_works(ctx, c, loop, identf, "a", S + P)
        L0s = attention_weights(c, column, "l0", "self", ["L0_xattn_mq_w", "L0_xattn_mk_w", "L0_xattn_mv_w", "L0_xattn_m_proj_w"],
                                ["L0_xattn_mq_b", "L0_xattn_mk_b", "L0_xattn_mv_b"], "L0_xattn_m_proj_b")
        L0c = attention_weights(c, column, "l0", "cross", ["L0_xattn_cq_w", "L0_xattn_ck_w", "L0_xattn_cv_w", "L0_xattn_c_proj_w"],
                                ["L0_xattn_cq_b", "L0_xattn_ck_b", "L0_xattn_cv_b"], "L0_xattn_c_proj_b")
        f1, f2 = c.weight("f1", a["L0_xattn_f_w1"]), c.weight("f2", a["L0_xattn_f_w2"])
        f_b2 = row(c, "L0_xattn_f_b2")
        n1 = lambda q: f"L1_xattn_{q}"
        L1 = {at: attention_weights(c, column, "l1", at, [n1(f"{at}_w{k}") for k in "qkvo"],
                                    [n1(f"{at}_b{k}") for k in "qkv"], n1(f"{at}_bo")) for at in ("sa", "ca")}
        ln = {k: row(c, n1(k)) for k in ("ln1_g", "ln1_b", "ln2_g", "ln2_b")}
        rw = c.weight("router", a["L1_xattn_router_w"])
        rb = c.load("router_b", [P, E], a["L1_xattn_router_b"].partition_broadcast(P))
        causal_f = c.load("causal", [P, 2, P], a["causal"])
        mask_b = c.sb("mask_b", [P, 2, P], BF16)
        for w in works:
            w.pick = w.buffer("pick", [P, QT, 4])
            w.route = {n: w.sb("route_" + n, sh, d) for n, sh, d in [
                ("logit", [P, QT, E], F32), ("prob", [P, QT, E], F32), ("max", [P, QT], F32), ("sum", [P, QT], F32),
                ("rsum", [P, QT], F32), ("top", [P, QT, E], F32), ("at", [P, QT, E], U32), ("gap", [P, QT], F32),
                ("e2", [P, QT], F32), ("one_e2", [P, QT], F32)]}
        zeros = c.sb("zeros", [P, D])
        c.fill(zeros[:, :], 0.0)
        c.emit()
        with nc.Block() as block:
            @block.vector
            def _(eng):
                eng.tensor_copy(works[0].identb, works[0].identf)
                eng.tensor_copy(mask_b[:, :, :], causal_f[:, :, :])
        cleared_v = sorted_dram.rearrange("(i p r) d -> i p r d", i=TRIPS, p=P)

        mask = (Diagonal(mask_b[:, 0, :]), Diagonal(mask_b[:, 1, :]))

        def steps(w, b):
            xt = yield from pre_norm(w, w.loaded, column("L0_xattn_ln1_g"), column("L0_xattn_ln1_b"))
            x = yield from attention_layer(w, L0s, "self", xt, w.loaded, mask, True,
                                            lambda: context_operands(w, L0c))
            fetch_tokens(w, lambda b: sequence(a["x"], b), b)
            xt = yield from pre_norm(w, x, column("L0_xattn_ln2_g"), column("L0_xattn_ln2_b"))
            x = yield from attention_layer(w, L0c, "cross", xt, x)
            xt = yield from pre_norm(w, x, column("L0_xattn_ln3_g"), column("L0_xattn_ln3_b"))
            residual = w.tok.next()
            add_bias(w, x, f_b2, residual)
            x = w.tok.next()
            if b == 0:
                loop.dma("sync", "cleared", lambda i: nc.sync.dma_start(
                    cleared_v[i], zeros[:, :].unsqueeze(1).broadcast_to([P, cleared_v.shape[2], D])))
            yield from feed_forward(w, f1, column("L0_xattn_f_b1"), f2, xt, residual, x)

            xt = to_features(w, x)
            yield 0.9, 1.2, 0
            x = yield from attention_layer(w, L1["sa"], "self", xt, x, mask, True,
                                            lambda: context_operands(w, L1["ca"]))
            fetch_context(w, ctx_t, b)
            x = yield from post_norm(w, x, ln["ln1_g"], ln["ln1_b"])
            xt = to_features(w, x)
            yield 0.9, 1.2, 0
            x = yield from attention_layer(w, L1["ca"], "cross", xt, x)
            x = yield from post_norm(w, x, ln["ln2_g"], ln["ln2_b"])
            store(w, x, sequence(x1, b), "x1")
            xt = to_features(w, x)
            yield 0.9, 1.2, 0
            yield from route(w, rw, rb[:, :], xt, w.pick)
            store(w, w.pick, lambda i: pick_dram[i * NB + b], "pick")
            yield 0, 1, 0

        take_turns(lane(steps, works[0], 0), lane(steps, works[1], 1), LEAD)
        for w in [shared] + works:
            w.close()
        with nc.Block() as block:
            loop.emit(block)

    c_ctx = program.enter_context(ExitStack())
    cc = Constants(nc, c_ctx, "c_weights")
    column, identf = common(cc)
    n2 = lambda q: f"L2_xattn_{q}"
    L2 = {at: attention_weights(cc, column, "l2", at, [n2(f"{at}_w{k}") for k in "qkvo"],
                                [n2(f"{at}_b{k}") for k in "qkv"], n2(f"{at}_bo")) for at in ("sa", "ca")}
    f1, f2 = cc.weight("f1", a[n2("ff_w1")]), cc.weight("f2", a[n2("ff_w2")])
    f_b2 = row(cc, n2("ff_b2"))
    ln = {k: row(cc, n2(k)) for k in ("ln1_g", "ln1_b", "ln2_g", "ln2_b", "ln3_g", "ln3_b")}
    L3 = attention_weights(cc, column, "l3", "cross", [f"L3_xattn_W{k}" for k in "qkvo"],
                           [f"L3_xattn_b{k}" for k in "qkv"], None)
    gamma, beta = row(cc, "L3_xattn_ln_gamma"), row(cc, "L3_xattn_ln_beta")
    ln3 = {k: row(cc, n1(f"ln3_{k}")) for k in "gb"}
    cc.start(c_ctx.enter_context(nc.semaphore("c_weights_loaded")))

    with ExitStack() as ctx:
        place_pairs(nc, ctx, a, pick_dram, rows_dram, owner_dram, x1, sorted_dram, unused.pop(), unused.pop())
    with ExitStack() as ctx:
        c = Constants(nc, ctx, "b_const")
        owner = c.load("owner", [1, GROUPS], owner_dram, I32)
        loop = Loop(nc, ctx, "b", GROUPS // UNROLL)
        w = Work(nc, ctx, "b", loop, QT)
        w.identf = identf[:, :]
        w.xt = w.ring("xt", 2, [P, KT, GROUP])
        xs = w.ring("x", 2, [P, QT, D])
        ys = w.ring("y", 2, [P, QT, D])
        w1s = w.ring("w1_", 2, [P, KT, FF])
        w2s = w.ring("w2_", 2, [P, FT, D])
        b1s = w.ring("b1_", 2, [P, FT])
        b2s = w.ring("b2_", 2, [P, D])
        hidden = w.ring("hidden", 2, [P, FT, GROUP])
        w.pj = w.psum("project", [1] * 8)
        c.emit()
        in_v = sorted_dram.rearrange("(i g q p) d -> i g p q d", g=UNROLL, q=QT, p=P)
        out_v = result_dram.rearrange("(i g q p) d -> i g p q d", g=UNROLL, q=QT, p=P)
        w1_v = a["L1_xattn_e_w1"].rearrange("e (k p) n -> e p k n", p=P)
        w2_v = a["L1_xattn_e_w2"].rearrange("e (k p) n -> e p k n", p=P)
        expert = {}

        def load(g):
            w1, w2, b1, b2, x = w1s.next(), w2s.next(), b1s.next(), b2s.next(), xs.next()

            def w1_load(i):
                expert[g] = nc.sync.value_load(owner[0:1, bass.ds(i * UNROLL + g, 1)], min_val=0, max_val=E - 1)
                return nc.sync.dma_start(w1.ap, w1_v[expert[g]])
            loop.wait("sync", w1.free)
            w1.written(loop.dma("sync", f"w1_{g % 2}", w1_load))
            loop.wait("sync", x.free, b1.free)
            x.written(loop.dma("sync", f"x_{g % 2}", lambda i: nc.sync.dma_start(x.ap, in_v[i, g])))
            b1.written(loop.dma("sync", f"b1_{g % 2}", lambda i: nc.sync.dma_start(b1.ap, a["e_b1"][expert[g]])))
            loop.wait("sync", w2.free, b2.free)
            w2.written(loop.dma("sync", f"w2_{g % 2}", lambda i: nc.sync.dma_start(w2.ap, w2_v[expert[g]])))
            b2.written(loop.dma("sync", f"b2_{g % 2}", lambda i: nc.sync.dma_start(
                b2.ap, a["L1_xattn_e_b2"][expert[g]].partition_broadcast(P))))
            return w1, w2, b1, b2, x

        def hide(got):
            w1, w2, b1, b2, x = got
            xt, hid = to_features(w, x, engine="vector"), hidden.next()
            loop.wait("scalar", hid.free, b1.ready)
            for f0 in range(0, FT, 2):
                bank = w.pj.next()
                loop.wait("tensor", bank.free, xt.ready, w1.ready)
                for f in (f0, f0 + 1):
                    for k in range(KT):
                        mm = loop.do("tensor", lambda i, f=f, k=k, bank=bank: nc.tensor.matmul(
                            bank.ap[:, 0, (f % 2) * GROUP:(f % 2 + 1) * GROUP], w1.ap[:, k, f * P:(f + 1) * P],
                            xt.ap[:, k, :], start=(k == 0), stop=(k == KT - 1)))
                loop.wait("scalar", mm)
                for f in (f0, f0 + 1):
                    put = loop.do("scalar", lambda i, f=f, bank=bank: nc.scalar.activation(
                        hid.ap[:, f, :], bank.ap[:, 0, (f % 2) * GROUP:(f % 2 + 1) * GROUP], ACT.Gelu,
                        bias=b1.ap[:, f:f + 1]))
                bank.free = (put,)
            xt.read(mm)
            w1.free, b1.free = (mm,), (put,)
            hid.written(put)
            return hid

        def finish(g, got, hid):
            w1, w2, b1, b2, x = got
            y = ys.next()
            bank = w.pj.next()
            loop.wait("tensor", bank.free, hid.ready, w2.ready)
            for q in range(QT):
                for f in range(FT):
                    mm = loop.do("tensor", lambda i, q=q, f=f: nc.tensor.matmul(
                        bank.ap[:, 0, q * D:(q + 1) * D], hid.ap[:, f, q * P:(q + 1) * P], w2.ap[:, f, :],
                        start=(f == 0), stop=(f == FT - 1)))
            hid.free = w2.free = (mm,)
            loop.wait("vector", mm, b2.ready, y.free)
            put = loop.do("vector", lambda i: nc.vector.tensor_tensor(
                y.ap, bank.ap[:, 0, :].rearrange("p (q n) -> p q n", q=QT),
                b2.ap.unsqueeze(1).broadcast_to([P, QT, D]), ALU.add))
            bank.free = b2.free = (put,)
            loop.wait("scalar", put)
            y.free = (loop.dma("scalar", f"y_{g % 2}", lambda i: nc.scalar.dma_start(out_v[i, g], y.ap)),)

        got = [load(0), load(1)]
        hid = hide(got[0])
        for g in range(UNROLL):
            following = hide(got[g + 1]) if g + 1 < UNROLL else None
            finish(g, got[g], hid)
            if g + 2 < UNROLL:
                got.append(load(g + 2))
            hid = following
        w.close()
        with nc.Block() as block:
            loop.emit(block)

    with ExitStack() as ctx:
        cc.finish()
        c = Constants(nc, ctx, "c_const")
        loop = Loop(nc, ctx, "c", TRIPS, unused)
        shared, works = attention_works(ctx, c, loop, identf, "c", 2 * S)
        mask_i = works[0].prob.buffers[0].ap[:, 0:QT, 0:S].bitcast(I32)
        mask_f = works[0].prob.buffers[1].ap[:, 0:QT, 0:S]
        c.loads.append((mask_i, a["mask"].rearrange("(q p) k -> p q k", p=P)))
        mask_q = c.sb("mask_q", [P, QT, S], BF16)
        mask_k = c.sb("mask_k", [P, QT, S], BF16)
        c.emit()
        with nc.semaphore("mask_f_done") as mask_f_done, nc.semaphore("mask_turned") as mask_turned, nc.Block() as block:
            mask_bank = shared.pj.buffers[0].ap

            @block.vector
            def _(eng):
                eng.tensor_copy(works[0].identb, works[0].identf)
                eng.tensor_scalar(mask_f[:, :, :], mask_i[:, :, :], 0.0, NEG, ALU.is_equal, ALU.mult).then_inc(mask_f_done, 1)
                eng.wait_ge(mask_f_done, 1)
                eng.tensor_copy(mask_q[:, :, :], mask_f[:, :, :])
                eng.wait_ge(mask_turned, 1)
                eng.tensor_copy(mask_k[:, :, :], mask_bank[:, 0, :].rearrange("p (k q) -> p k q", k=QT))

            @block.tensor
            def _(eng):
                eng.wait_ge(mask_f_done, 1)
                for k in range(QT):
                    for q in range(QT):
                        ins = eng.transpose(mask_bank[:, 0, k * S + q * P:k * S + (q + 1) * P],
                                            mask_f[:, q, k * P:(k + 1) * P], works[0].identf)
                ins.then_inc(mask_turned, 1)

        for w in works:
            w.pair_rows = w.buffer("pair_rows", [P, 2 * QT], U32)
            w.pair_y = w.buffer("pair_y", [P, 2 * QT, D])
            w.pick = w.buffer("pick", [P, QT, 4])

        for w in works:
            for buf in (w.pair_rows, w.pair_y, w.pick):
                loaded_ahead(buf)

        def fetch_pairs(w, b):
            fetch_tokens(w, lambda b: sequence(x1, b), b)
            at, ahead = next_sequence(b)
            rows, y, pick = w.pair_rows, w.pair_y, w.pick
            for q in range(QT):
                if q:
                    rows.free = ()
                fetch(w, rows, "rows", ahead, lambda i, q=q: nc.gpsimd.dma_start(
                    rows.ap[:, 2 * q:2 * q + 2], rows_dram[(i * NB + at) * QT + q]))
            fetch(w, pick, "pick", ahead, lambda i: nc.gpsimd.dma_start(pick.ap, pick_dram[i * NB + at]))
            if ahead:
                loop.wait_ahead(rows.ready[0])
            else:
                loop.wait("gpsimd", rows.ready)
            loop.wait("gpsimd", y.free)
            y.free = ()
            for j in range(2 * QT):
                fetch(w, y, "y", ahead, lambda i, j=j: nc.gpsimd.indirect_dma_start(
                    y.ap[:, j, :], None, result_dram, bass.IndirectOffsetOnAxis(ap=rows.ap[:, j:j + 1], axis=0)))
            rows.free = y.ready

        def mix_experts(w):
            x, y, pick = w.loaded, w.pair_y, w.pick
            out = w.tok.next()
            loop.wait("vector", x.ready, pick.ready, y.ready, out.free)
            for q in range(QT):
                mid = loop.do("vector", lambda i, q=q: nc.vector.scalar_tensor_tensor(
                    out.ap[:, q, :], y.ap[:, 2 * q, :], pick.ap[:, q, 2:3], x.ap[:, q, :], ALU.mult, ALU.add))
            loop.wait("vector", mid)
            for q in range(QT):
                put = loop.do("vector", lambda i, q=q: nc.vector.scalar_tensor_tensor(
                    out.ap[:, q, :], y.ap[:, 2 * q + 1, :], pick.ap[:, q, 3:4], out.ap[:, q, :], ALU.mult, ALU.add))
            x.read(mid)
            y.free = pick.free = (put,)
            out.written(put)
            yield 0, 1.5, 0
            return out

        def steps(w, b):
            x = yield from mix_experts(w)
            x = yield from post_norm(w, x, ln3["g"], ln3["b"])
            xt = to_features(w, x)
            yield 0.9, 1.2, 0
            x = yield from attention_layer(w, L2["sa"], "self", xt, x, (mask_q, mask_k), False,
                                            lambda: (context_operands(w, L2["ca"]), fetch_pairs(w, b)))
            x = yield from post_norm(w, x, ln["ln1_g"], ln["ln1_b"])
            xt = to_features(w, x)
            yield 0.9, 1.2, 0
            x = yield from attention_layer(w, L2["ca"], "cross", xt, x)
            x = yield from post_norm(w, x, ln["ln2_g"], ln["ln2_b"])
            xt = to_features(w, x)
            yield 0.9, 1.2, 0
            residual = w.tok.next()
            add_bias(w, x, f_b2, residual)
            x = w.tok.next()
            context_operands(w, L3)
            fetch_context(w, ctx_t, b)
            yield from feed_forward(w, f1, column(n2("ff_b1")), f2, xt, residual, x)
            x = yield from post_norm(w, x, ln["ln3_g"], ln["ln3_b"])
            xt = to_features(w, x)
            yield 0.9, 1.2, 0
            x = yield from attention_layer(w, L3, "cross", xt, x)
            x = yield from post_norm(w, x, gamma, beta)
            store(w, x, sequence(out, b), "out")
            yield 0, 1, 0

        take_turns(lane(steps, works[0], 0), lane(steps, works[1], 1), LEAD)
        for w in [shared] + works:
            w.close()
        with nc.Block() as block:
            loop.emit(block)


class Diagonal:

    def __init__(self, tile):
        self.tile = tile

    def __getitem__(self, _):
        return self.tile


_VECTORS = (["L0_xattn_ln1_g", "L0_xattn_ln1_b", "L0_xattn_ln2_g", "L0_xattn_ln2_b", "L0_xattn_ln3_g",
             "L0_xattn_ln3_b", "L0_xattn_mq_b", "L0_xattn_mk_b", "L0_xattn_mv_b", "L0_xattn_cq_b",
             "L0_xattn_ck_b", "L0_xattn_cv_b", "L0_xattn_f_b1", "L2_xattn_ff_b1"]
            + [f"{l}_xattn_{at}_b{k}" for l in ("L1", "L2") for at in ("sa", "ca") for k in "qkv"]
            + [f"L3_xattn_b{k}" for k in "qkv"])
_TURNED = [n for n in _VECTORS if n[-2:] in ("bq", "bk") or n[-3:-1] == "q_" or n[-4:] in ("mq_b", "mk_b", "cq_b", "ck_b")]
_SIZES = {"L0_xattn_f_b1": FF, "L2_xattn_ff_b1": FF}
COLUMNS = [(n, k) for n in _VECTORS for k in range(_SIZES.get(n, D) // P)]
ROWS = (["L0_xattn_m_proj_b", "L0_xattn_c_proj_b", "L0_xattn_f_b2", "L2_xattn_ff_b2",
         "L3_xattn_ln_gamma", "L3_xattn_ln_beta"]
        + [f"{l}_xattn_{at}_bo" for l in ("L1", "L2") for at in ("sa", "ca")]
        + [f"{l}_xattn_ln{k}_{j}" for l in ("L1", "L2") for k in (1, 2, 3) for j in "gb"])


def kernel(**inputs):
    import concourse.bacc as bacc
    from concourse.bass_utils import run_bass_kernel_spmd

    v = {k: np.asarray(x) for k, x in inputs.items()}
    turn = lambda x: np.moveaxis(x.reshape(x.shape[:-1] + (H, HD)), -1, -2).reshape(x.shape)
    arrays = {"x": v["x"], "mask": v["mask_1x1xSxS_ik0"].reshape(S, S),
              "ctx_t": v["ctx_1024"].reshape(B * C, D).T,
              "columns": np.concatenate([(turn(v[n].reshape(D)) if n in _TURNED else v[n]).reshape(-1, P)
                                         for n in _VECTORS]).T,
              "rows": np.stack([v[n] for n in ROWS]),
              "identity": np.eye(P, dtype=np.float32),
              "iota": np.arange(E, dtype=np.float32),
              "ones": np.ones((P, P), np.float32),
              "before": np.triu(np.ones((P, P), np.float32), 1),
              "steps": np.arange(S // 16, dtype=np.float32) * GROUP,
              "next_trip": ((np.arange(TRIPS) + 1) % TRIPS).astype(np.int32),
              "group_no": np.arange(GROUPS, dtype=np.float32),
              "e_b1": v["L1_xattn_e_b1"].reshape(E, FT, P).transpose(0, 2, 1)}
    k, q = np.meshgrid(np.arange(P), np.arange(P))
    future = np.where(k > q, np.float32(NEG), np.float32(0))
    arrays["causal"] = np.stack([future, future.T], axis=1)
    for n in ("mq", "mk", "mv", "cq", "ck", "cv"):
        arrays[f"L0_xattn_{n}_w"] = v[f"L0_xattn_{n}_w"].transpose(1, 0, 2).reshape(D, D)
    for n in ("L0_xattn_m_proj_w", "L0_xattn_c_proj_w", "L0_xattn_f_w1", "L0_xattn_f_w2", "L1_xattn_router_w",
              "L1_xattn_router_b", "L1_xattn_e_w1", "L1_xattn_e_w2", "L1_xattn_e_b2"):
        arrays[n] = v[n]
    for at in ("sa", "ca"):
        for m in "qkvo":
            arrays[f"L1_xattn_{at}_w{m}"] = v[f"L1_xattn_{at}_w{m}"]
            arrays[f"L2_xattn_{at}_w{m}"] = v[f"L2_xattn_{at}_w{m}"].T
    for m in (1, 2):
        arrays[f"L2_xattn_ff_w{m}"] = v[f"L2_xattn_ff_w{m}"].T
    for m in "qkvo":
        arrays[f"L3_xattn_W{m}"] = v[f"L3_xattn_W{m}"]
    for n in ("L0_xattn_mq_w", "L0_xattn_mk_w", "L0_xattn_cq_w", "L0_xattn_ck_w", "L3_xattn_Wq", "L3_xattn_Wk",
              *(f"{l}_xattn_{at}_w{m}" for l in ("L1", "L2") for at in ("sa", "ca") for m in "qk")):
        arrays[n] = turn(arrays[n])
    arrays = {n: np.ascontiguousarray(x) for n, x in arrays.items()}

    nc = bacc.Bacc("TRN2", target_bir_lowering=False, num_devices=1)
    ins = {n: nc.dram_tensor(f"in_{n}", x.shape, mybir.dt.from_np(x.dtype), kind="ExternalInput").ap()
           for n, x in arrays.items()}
    out = nc.dram_tensor("out", (B, S, D), F32, kind="ExternalOutput").ap()
    build(nc, ins, out)
    r = run_bass_kernel_spmd(nc, [{f"in_{n}": x for n, x in arrays.items()}], core_ids=[0])
    return r.results[0]["out"]
```
